# Optimizing a Trainium2 kernel written in Bass

```python
import numpy as np
import jax
import jax.numpy as jnp

def _softmax(x, axis=-1):
    return jax.nn.softmax(x, axis=axis)

def _gelu(x):
    return jax.nn.gelu(x, approximate=True)

def _silu(x):
    return jax.nn.silu(x)

def _sigmoid(x):
    return jax.nn.sigmoid(x)

def _layernorm(x, axis=-1, eps=1e-05):
    m = jnp.mean(x, axis=axis, keepdims=True)
    v = jnp.var(x, axis=axis, keepdims=True)
    return (x - m) / jnp.sqrt(v + eps)

def _scatter_add(tgt, idx, src, axis=0):
    return tgt.at[idx].add(src)

def _segment_sum(src, seg, n):
    return jax.ops.segment_sum(src, seg, n)
kernel_name = 'mk_xattn_ffn_d2_seqx_r8_5e1348'

def setup_inputs(seed: int=0):
    np.random.seed(seed)
    _w = jnp.asarray

    def _rec_inputs():
        import jax
        import jax.numpy as jnp
        _rk = jax.random.key(seed)
        x = -0.000125 + 0.9999 * jax.random.normal(jax.random.fold_in(_rk, 1), (4, 256, 256), jnp.float32)
        _lenS = 256 - jax.random.randint(jax.random.fold_in(_rk, 7), (4,), 0, max(1, 256 // 4) + 1, jnp.int32)
        _lenS2 = 256 - jax.random.randint(jax.random.fold_in(_rk, 8), (4,), 0, max(1, 256 // 4) + 1, jnp.int32)
        itok_BxS_13_99985 = jax.random.randint(jax.random.fold_in(_rk, 11), (4, 256), 13, 99986, jnp.int32)
        _ctx_2048P = jax.random.normal(jax.random.fold_in(_rk, 12), (4, 16, 256), jnp.float32)
        _ctx_2048c = jax.random.dirichlet(jax.random.fold_in(_rk, 512), 0.3 * jnp.ones((16,), jnp.float32), (4, 256))
        _ctx_2048t = jnp.einsum('bsk,bkd->bsd', _ctx_2048c, _ctx_2048P)
        _ctx_2048t = _ctx_2048t * jax.lax.rsqrt(jnp.mean(jnp.square(_ctx_2048t)) + 1e-12) * 0.953939
        ctx_2048 = 6.82029e-06 + 0.0200006 * (_ctx_2048t + 0.3 * jax.random.normal(jax.random.fold_in(_rk, 612), (4, 256, 256), jnp.float32))
        return (x, itok_BxS_13_99985, ctx_2048)
    x, itok_BxS_13_99985, ctx_2048 = _rec_inputs()

    def _L0_xattn_setup():
        import jax, jax.numpy as jnp
        import numpy as np
        B, S, D = (4, 512, 256)
        E = 4
        F = 1024 // E
        VOCAB = 12500
        key = jax.random.key(seed)
        k1, k2, k3, k4, k5 = jax.random.split(key, 5)
        hidden_states = jax.random.normal(k1, (B, S, D), dtype=jnp.float32)
        token_ids = jax.random.randint(k2, (B, S), 0, VOCAB, dtype=jnp.int64)
        Wg = jax.random.normal(k3, (E, F, D), dtype=jnp.float32) * 0.02
        Wu = jax.random.normal(k4, (E, F, D), dtype=jnp.float32) * 0.02
        Wd = jax.random.normal(k5, (E, D, F), dtype=jnp.float32) * 0.02
        return {'hidden_states': hidden_states, 'token_ids': token_ids, 'Wg': Wg, 'Wu': Wu, 'Wd': Wd}
    _L0_xattn_all = _L0_xattn_setup()
    _L0_xattn_in = {k: v for k, v in _L0_xattn_all.items() if k in ()}
    del _L0_xattn_all

    def _L0_ffn_setup():
        import jax, jax.numpy as jnp
        import numpy as np
        H, F, E, K = (256, 128, 16, 4)
        ROUTED_SCALE = 1.0
        key = jax.random.key(seed)
        ks = jax.random.split(key, 9)
        s = 0.02
        return {'x': jax.random.normal(ks[0], (4, 64, H), jnp.float32), 'router_w': jax.random.normal(ks[1], (E, H), jnp.float32) * s, 'router_bias': jnp.zeros((E,), jnp.float32), 'expert_gate_w': jax.random.normal(ks[2], (E, F, H), jnp.float32) * s, 'expert_up_w': jax.random.normal(ks[3], (E, F, H), jnp.float32) * s, 'expert_down_w': jax.random.normal(ks[4], (E, H, F), jnp.float32) * s, 'shared_gate_w': jax.random.normal(ks[5], (F, H), jnp.float32) * s, 'shared_up_w': jax.random.normal(ks[6], (F, H), jnp.float32) * s, 'shared_down_w': jax.random.normal(ks[7], (H, F), jnp.float32) * s}
    _L0_ffn_all = _L0_ffn_setup()
    _L0_ffn_in = {k: v for k, v in _L0_ffn_all.items() if k in ('router_w', 'router_bias', 'expert_gate_w', 'expert_up_w', 'expert_down_w', 'shared_gate_w', 'shared_up_w', 'shared_down_w')}
    del _L0_ffn_all

    def _L1_xattn_setup():
        import jax, jax.numpy as jnp
        import numpy as np
        HIDDEN = 256
        NUM_HEADS = 16
        NUM_KV_HEADS = 4
        HEAD_DIM = 128
        ROPE_THETA = 10000.0
        EPS = 1e-06

        def rms_norm(x, w, eps=EPS):
            var = jnp.mean(jnp.square(x), axis=-1, keepdims=True)
            return x * jax.lax.rsqrt(var + eps) * w

        def rope_cache(L, head_dim, theta, dtype):
            inv_freq = 1.0 / theta ** (jnp.arange(0, head_dim, 2, dtype=jnp.float32) / head_dim)
            t = jnp.arange(L, dtype=jnp.float32)
            freqs = jnp.outer(t, inv_freq)
            emb = jnp.concatenate([freqs, freqs], -1)
            cos = jnp.cos(emb).astype(dtype)[None, :, None, :]
            sin = jnp.sin(emb).astype(dtype)[None, :, None, :]
            return (cos, sin)

        def rotate_half(x):
            x1, x2 = jnp.split(x, 2, axis=-1)
            return jnp.concatenate([-x2, x1], axis=-1)
        key = jax.random.key(seed)
        ks = jax.random.split(key, 10)
        B, L, T = (2, 256, 64)
        q_out = NUM_HEADS * HEAD_DIM
        kv_out = NUM_KV_HEADS * HEAD_DIM
        s = lambda fan_in: 1.0 / np.sqrt(fan_in)
        return {'x': jax.random.normal(ks[0], (B, L, HIDDEN), jnp.float32), 'h_ctx_kv': jax.random.normal(ks[1], (B, T, HIDDEN), jnp.float32), 'wq': jax.random.normal(ks[2], (HIDDEN, q_out), jnp.float32) * s(HIDDEN), 'wk': jax.random.normal(ks[3], (HIDDEN, kv_out), jnp.float32) * s(HIDDEN), 'wv': jax.random.normal(ks[4], (HIDDEN, kv_out), jnp.float32) * s(HIDDEN), 'wo': jax.random.normal(ks[5], (q_out, HIDDEN), jnp.float32) * s(q_out), 'wk_ctx': jax.random.normal(ks[6], (HIDDEN, kv_out), jnp.float32) * s(HIDDEN), 'wv_ctx': jax.random.normal(ks[7], (HIDDEN, kv_out), jnp.float32) * s(HIDDEN), 'q_norm_w': jnp.ones((HEAD_DIM,), jnp.float32), 'k_norm_w': jnp.ones((HEAD_DIM,), jnp.float32)}
    _L1_xattn_all = _L1_xattn_setup()
    _L1_xattn_in = {k: v for k, v in _L1_xattn_all.items() if k in ('wq', 'wk', 'wv', 'wo', 'wk_ctx', 'wv_ctx', 'q_norm_w', 'k_norm_w')}
    del _L1_xattn_all

    def _L1_ffn_setup():
        import jax, jax.numpy as jnp
        import numpy as np
        B, S, D, F, E, K = (2, 256, 256, 1024, 8, 2)
        key = jax.random.key(seed)
        k0, k1, k2, k3 = jax.random.split(key, 4)
        scale = lambda k, shape, fan_in: jax.random.normal(k, shape, jnp.float32) * fan_in ** (-0.5)
        return {'inputs': jax.random.normal(k0, (B, S, D), jnp.float32), 'gate_w': scale(k1, (D, E), D), 'gate_b': jnp.zeros((E,), jnp.float32), 'w1': scale(k2, (E, D, F), D), 'b1': jnp.zeros((E, F), jnp.float32), 'w2': scale(k3, (E, F, D), F), 'b2': jnp.zeros((E, D), jnp.float32)}
    _L1_ffn_all = _L1_ffn_setup()
    _L1_ffn_in = {k: v for k, v in _L1_ffn_all.items() if k in ('gate_w', 'gate_b', 'w1', 'b1', 'w2', 'b2')}
    del _L1_ffn_all
    return {'x': x, 'itok_BxS_13_99985': itok_BxS_13_99985, 'ctx_2048': ctx_2048, 'L0_ffn_router_w': _L0_ffn_in['router_w'], 'L0_ffn_router_bias': _L0_ffn_in['router_bias'], 'L0_ffn_expert_gate_w': _L0_ffn_in['expert_gate_w'], 'L0_ffn_expert_up_w': _L0_ffn_in['expert_up_w'], 'L0_ffn_expert_down_w': _L0_ffn_in['expert_down_w'], 'L0_ffn_shared_gate_w': _L0_ffn_in['shared_gate_w'], 'L0_ffn_shared_up_w': _L0_ffn_in['shared_up_w'], 'L0_ffn_shared_down_w': _L0_ffn_in['shared_down_w'], 'L1_xattn_wq': _L1_xattn_in['wq'], 'L1_xattn_wk': _L1_xattn_in['wk'], 'L1_xattn_wv': _L1_xattn_in['wv'], 'L1_xattn_wo': _L1_xattn_in['wo'], 'L1_xattn_wk_ctx': _L1_xattn_in['wk_ctx'], 'L1_xattn_wv_ctx': _L1_xattn_in['wv_ctx'], 'L1_xattn_q_norm_w': _L1_xattn_in['q_norm_w'], 'L1_xattn_k_norm_w': _L1_xattn_in['k_norm_w'], 'L1_ffn_gate_w': _L1_ffn_in['gate_w'], 'L1_ffn_gate_b': _L1_ffn_in['gate_b'], 'L1_ffn_w1': _L1_ffn_in['w1'], 'L1_ffn_b1': _L1_ffn_in['b1'], 'L1_ffn_w2': _L1_ffn_in['w2'], 'L1_ffn_b2': _L1_ffn_in['b2']}

def reference(x, itok_BxS_13_99985, ctx_2048, L0_ffn_router_w, L0_ffn_router_bias, L0_ffn_expert_gate_w, L0_ffn_expert_up_w, L0_ffn_expert_down_w, L0_ffn_shared_gate_w, L0_ffn_shared_up_w, L0_ffn_shared_down_w, L1_xattn_wq, L1_xattn_wk, L1_xattn_wv, L1_xattn_wo, L1_xattn_wk_ctx, L1_xattn_wv_ctx, L1_xattn_q_norm_w, L1_xattn_k_norm_w, L1_ffn_gate_w, L1_ffn_gate_b, L1_ffn_w1, L1_ffn_b1, L1_ffn_w2, L1_ffn_b2):
    import jax
    import jax.numpy as jnp

    def _L0_xattn_ref(hidden_states, token_ids, Wg, Wu, Wd):
        import jax, jax.numpy as jnp
        import numpy as np
        B, S, D = (4, 512, 256)
        E = 4
        F = 1024 // E
        VOCAB = 12500
        tokens_per_expert = VOCAB // E
        tid = jnp.clip(token_ids, 0, VOCAB - 1)
        expert_ids = jnp.minimum(tid // tokens_per_expert, E - 1)
        out = jnp.zeros_like(hidden_states)
        for e in range(E):
            g = jax.nn.silu(jnp.einsum('bsd,fd->bsf', hidden_states, Wg[e]))
            u = jnp.einsum('bsd,fd->bsf', hidden_states, Wu[e])
            y = jnp.einsum('bsf,df->bsd', g * u, Wd[e])
            out = jnp.where((expert_ids == e)[..., None], y, out)
        return out

    def _L0_ffn_ref(x, router_w, router_bias, expert_gate_w, expert_up_w, expert_down_w, shared_gate_w, shared_up_w, shared_down_w):
        import jax, jax.numpy as jnp
        import numpy as np
        H, F, E, K = (256, 128, 16, 4)
        ROUTED_SCALE = 1.0
        orig_shape = x.shape
        h = x.reshape(-1, orig_shape[-1])
        T = h.shape[0]
        logits = h @ router_w.T
        scores = jax.nn.sigmoid(logits)
        choice = scores + router_bias[None, :]
        _, topk_idx = jax.lax.top_k(choice, K)
        topk_w = jnp.take_along_axis(scores, topk_idx, axis=1)
        topk_w = topk_w / (topk_w.sum(-1, keepdims=True) + 1e-20)
        topk_w = topk_w * ROUTED_SCALE
        comb = jnp.zeros((T, E), h.dtype).at[jnp.arange(T)[:, None], topk_idx].set(topk_w)
        g = jnp.einsum('th,efh->tef', h, expert_gate_w)
        u = jnp.einsum('th,efh->tef', h, expert_up_w)
        a = jax.nn.silu(g) * u
        routed = jnp.einsum('tef,te,ehf->th', a, comb, expert_down_w)
        shared = jax.nn.silu(h @ shared_gate_w.T) * (h @ shared_up_w.T) @ shared_down_w.T
        return (routed + shared).reshape(orig_shape)

    def _L1_xattn_ref(x, h_ctx_kv, wq, wk, wv, wo, wk_ctx, wv_ctx, q_norm_w, k_norm_w):
        import jax, jax.numpy as jnp
        import numpy as np
        HIDDEN = 256
        NUM_HEADS = 16
        NUM_KV_HEADS = 4
        HEAD_DIM = 128
        ROPE_THETA = 10000.0
        EPS = 1e-06

        def rms_norm(x, w, eps=EPS):
            var = jnp.mean(jnp.square(x), axis=-1, keepdims=True)
            return x * jax.lax.rsqrt(var + eps) * w

        def rope_cache(L, head_dim, theta, dtype):
            inv_freq = 1.0 / theta ** (jnp.arange(0, head_dim, 2, dtype=jnp.float32) / head_dim)
            t = jnp.arange(L, dtype=jnp.float32)
            freqs = jnp.outer(t, inv_freq)
            emb = jnp.concatenate([freqs, freqs], -1)
            cos = jnp.cos(emb).astype(dtype)[None, :, None, :]
            sin = jnp.sin(emb).astype(dtype)[None, :, None, :]
            return (cos, sin)

        def rotate_half(x):
            x1, x2 = jnp.split(x, 2, axis=-1)
            return jnp.concatenate([-x2, x1], axis=-1)
        B, L, _ = x.shape
        T = h_ctx_kv.shape[1]
        rep = NUM_HEADS // NUM_KV_HEADS
        q = (x @ wq).reshape(B, L, NUM_HEADS, HEAD_DIM)
        k = (x @ wk).reshape(B, L, NUM_KV_HEADS, HEAD_DIM)
        v = (x @ wv).reshape(B, L, NUM_KV_HEADS, HEAD_DIM)
        q = rms_norm(q, q_norm_w)
        k = rms_norm(k, k_norm_w)
        k_ctx = (h_ctx_kv @ wk_ctx).reshape(B, T, NUM_KV_HEADS, HEAD_DIM)
        v_ctx = (h_ctx_kv @ wv_ctx).reshape(B, T, NUM_KV_HEADS, HEAD_DIM)
        k_ctx = rms_norm(k_ctx, k_norm_w)
        cos, sin = rope_cache(L, HEAD_DIM, ROPE_THETA, x.dtype)
        q = q * cos + rotate_half(q) * sin
        k = k * cos + rotate_half(k) * sin
        k_full = jnp.concatenate([k_ctx, k], axis=1)
        v_full = jnp.concatenate([v_ctx, v], axis=1)
        k_full = jnp.repeat(k_full, rep, axis=2)
        v_full = jnpp_repeat = jnp.repeat(v_full, rep, axis=2)
        i = jnp.arange(L)[:, None]
        j = jnp.arange(L)[None, :]
        causal = jnp.where(j > i, -jnp.inf, 0.0).astype(x.dtype)
        mask = jnp.concatenate([jnp.zeros((L, T), x.dtype), causal], axis=1)
        scale = 1.0 / np.sqrt(HEAD_DIM)
        scores = jnp.einsum('blhd,bmhd->bhlm', q, k_full) * scale + mask
        probs = jax.nn.softmax(scores, axis=-1)
        out = jnp.einsum('bhlm,bmhd->blhd', probs, v_full)
        out = out.reshape(B, L, NUM_HEADS * HEAD_DIM)
        return out @ wo

    def _L1_ffn_ref(inputs, gate_w, gate_b, w1, b1, w2, b2):
        import jax, jax.numpy as jnp
        import numpy as np
        B, S, D, F, E, K = (2, 256, 256, 1024, 8, 2)
        x = inputs.reshape(-1, inputs.shape[-1])
        n = x.shape[0]
        gate_probs = jax.nn.softmax(x @ gate_w + gate_b, axis=-1)
        weights, selected = jax.lax.top_k(gate_probs, K)
        weights = weights / jnp.sum(weights, axis=-1, keepdims=True)
        comb = jnp.zeros((n, E), x.dtype).at[jnp.arange(n)[:, None], selected].set(weights)
        h = jax.nn.gelu(jnp.einsum('nd,edf->enf', x, w1) + b1[:, None, :])
        expert_out = jnp.einsum('enf,efd->end', h, w2) + b2[:, None, :]
        out = jnp.einsum('ne,end->nd', comb, expert_out)
        return out.reshape(inputs.shape[:-1] + (out.shape[-1],))
    x = x + _L0_xattn_ref(_layernorm(x, axis=-1), itok_BxS_13_99985, ctx_2048, ctx_2048, ctx_2048)
    x = x + _L0_ffn_ref(_layernorm(x, axis=-1), L0_ffn_router_w, L0_ffn_router_bias, L0_ffn_expert_gate_w, L0_ffn_expert_up_w, L0_ffn_expert_down_w, L0_ffn_shared_gate_w, L0_ffn_shared_up_w, L0_ffn_shared_down_w)
    x = x + _L1_xattn_ref(_layernorm(x, axis=-1), ctx_2048, L1_xattn_wq, L1_xattn_wk, L1_xattn_wv, L1_xattn_wo, L1_xattn_wk_ctx, L1_xattn_wv_ctx, L1_xattn_q_norm_w, L1_xattn_k_norm_w)
    x = x + _L1_ffn_ref(_layernorm(x, axis=-1), L1_ffn_gate_w, L1_ffn_gate_b, L1_ffn_w1, L1_ffn_b1, L1_ffn_w2, L1_ffn_b2)
    return x

_drawn_inputs = setup_inputs


def setup_inputs(seed=0):
    import zlib

    import numpy as np

    out = dict(_drawn_inputs(seed))
    spreads = {'L0_ffn_router_bias': (0.0, 0.308),
     'L1_xattn_q_norm_w': (1.0, 0.2),
     'L1_xattn_k_norm_w': (1.0, 0.2),
     'L1_ffn_gate_b': (0.0, 0.1),
     'L1_ffn_b1': (0.0, 0.1),
     'L1_ffn_b2': (0.0, 0.1)}
    factors = {}
    for name, (base, spread) in spreads.items():
        noise = np.random.default_rng([zlib.crc32(name.encode()), seed]).standard_normal(out[name].shape)
        drawn = base * np.exp(spread * noise) if base else spread * noise
        out[name] = jnp.asarray(drawn.astype(out[name].dtype))
    for name, factor in factors.items():
        out[name] = (out[name] * factor).astype(out[name].dtype)
    return out
```

```python
from contextlib import ExitStack

import concourse.bass as bass
from concourse import mybir

F32 = mybir.dt.float32
F32R = mybir.dt.float32r
I32 = mybir.dt.int32
U32 = mybir.dt.uint32
ALU = mybir.AluOpType
ACT = mybir.ActivationFunctionType
AX_X = mybir.AxisListType.X

P = 128
B, S, D = 4, 256, 256
TILES = B * S // P
KD = D // P
HALF = 512
HT = HALF // P
EA = 4
VOCAB = 12500
PER_EXPERT = VOCAB // EA
EB, KB, FB = 16, 4, 128
WG = 2 * KD * FB
WB = WG + D
HEADS, KV, HD = 16, 4, 128
REP = HEADS // KV
KEYS = 2 * S
SCALE = HD ** -0.5
RMS_EPS = 1e-6
WQ = KD * REP * HD
WK = KD * 2 * HD
WO = REP * D
ED, KDTOP, FD = 8, 2, 1024
CHUNKS = FD // P
WD = KD * P + D
LN_EPS = 1e-5
MASKED = -float(2 ** 100)


class Count:

    def __init__(self, sem):
        self.sem, self.n, self.base = sem, 0, 0

    def tick(self, ins):
        ins.then_inc(self.sem, 1)
        self.n += 1

    def settle(self, eng):
        eng.wait_ge(self.sem, self.base + self.n)

    def turn(self, i, per):
        self.base, self.start, self.per = i * per, self.n, per

    def turned(self, turns):
        assert self.n - self.start == self.per, (self.n - self.start, self.per)
        self.n, self.base = self.start + turns * self.per, 0


def f32(ap):
    return ap.bitcast(F32)


def product(pe, out, left, right, first=True, last=True, shared=False):
    (lh, ll), (rh, rl) = left, right
    pe.matmul(out, ll, rh, start=first, stop=False, skip_group_check=shared)
    pe.matmul(out, lh, rl, start=False, stop=False, skip_group_check=shared)
    return pe.matmul(out, lh, rh, start=False, stop=last, skip_group_check=shared)


def both(pair, *index):
    return tuple(t[index] for t in pair)


class Norm:

    def __init__(self, nc, sb, sem, tag, x, hT, banks, ident):
        self.x, self.hT, self.banks, self.ident = x, hT, banks, ident
        self.stats = sb(f"{tag}_stats", [P, TILES, 6], F32)
        self.moments = sb(f"{tag}_moments", [P, TILES, 2], F32)
        self.shifted = sb(f"{tag}_var_eps", [P, TILES], F32)
        self.power = sb(f"{tag}_minus_half", [P, TILES], F32)
        self.rstd = sb(f"{tag}_rstd", [P, TILES], F32)
        self.h = sb(f"{tag}_h", [P, TILES, D], F32)
        self.stats_done = sem(f"{tag}_stats_done")
        self.moments_done = sem(f"{tag}_moments_done")
        self.power_set = sem(f"{tag}_power_set")
        self.eps_added = sem(f"{tag}_eps_added")
        self.rstd_ready = sem(f"{tag}_rstd_ready")
        self.normed = sem(f"{tag}_normed")
        self.turned = sem(f"{tag}_h_transposed")
        self.hi_ready = sem(f"{tag}_hT_hi_ready")
        self.lo_ready = sem(f"{tag}_hT_lo_ready")

    def vector_moments(self, v, half):
        tiles = range(HT * half, HT * half + HT)
        for t in tiles:
            v.bn_stats(self.stats[:, t, :], self.x[:, t, :]).then_inc(self.stats_done, 1)
        for t in tiles:
            v.wait_ge(self.stats_done, t + 1)
            v.bn_aggr(self.moments[:, t, :], self.stats[:, t, :]).then_inc(self.moments_done, 1)

    def gpsimd(self, p):
        p.memset(self.power[:], -0.5).then_inc(self.power_set, 1)
        p.wait_ge(self.power_set, 1)
        for half in range(2):
            a, b = HT * half, HT * half + HT
            p.wait_ge(self.moments_done, b)
            p.tensor_scalar(self.shifted[:, a:b], self.moments[:, a:b, 1], LN_EPS, None,
                            ALU.add).then_inc(self.eps_added, 1)
            p.wait_ge(self.eps_added, half + 1)
            p.tensor_tensor(self.rstd[:, a:b], self.shifted[:, a:b], self.power[:, a:b],
                            ALU.pow).then_inc(self.rstd_ready, 1)

    def vector_normalize(self, v, half):
        v.wait_ge(self.moments_done, HT * half + HT)
        v.wait_ge(self.rstd_ready, half + 1)
        for t in range(HT * half, HT * half + HT):
            v.tensor_scalar(self.h[:, t, :], self.x[:, t, :], self.moments[:, t, 0:1],
                            self.rstd[:, t:t + 1], ALU.subtract, ALU.mult).then_inc(self.normed, 1)

    def tensor(self, pe, half):
        for k in range(KD):
            for r in range(HT):
                t = HT * half + r
                pe.wait_ge(self.normed, t + 1)
                ins = pe.transpose(self.banks[KD * half + k][:, r * P:(r + 1) * P],
                                   self.h[:, t, k * P:(k + 1) * P], self.ident[:])
            ins.then_inc(self.turned, 1)

    def scalar_hi(self, act, half):
        for k in range(KD):
            u = KD * half + k
            act.wait_ge(self.turned, u + 1)
            act.activation(self.hT[0][:, k, half * HALF:(half + 1) * HALF], self.banks[u][:],
                           ACT.Copy).then_inc(self.hi_ready, 1)

    def vector_lo(self, v, half):
        for k in range(KD):
            u = KD * half + k
            v.wait_ge(self.hi_ready, u + 1)
            v.tensor_tensor(self.hT[1][:, k, half * HALF:(half + 1) * HALF], self.banks[u][:],
                            f32(self.hT[0][:, k, half * HALF:(half + 1) * HALF]),
                            ALU.subtract).then_inc(self.lo_ready, 1)

    def wait_half(self, eng, half):
        eng.wait_ge(self.hi_ready, KD * (half + 1))
        eng.wait_ge(self.lo_ready, KD * (half + 1))


def choose(v, own, sb, tag, choice, weights, iota, k, experts, eps, comb):
    best = sb(f"{tag}_best", [P, TILES, 8], F32)
    index = sb(f"{tag}_index", [P, TILES, 8], U32)
    indexf = sb(f"{tag}_indexf", [P, TILES, 8], F32)
    hit = sb(f"{tag}_hit", [P, TILES, experts], F32)
    picked = sb(f"{tag}_picked", [P, TILES, experts], F32)
    total = sb(f"{tag}_total", [P, TILES], F32)
    for t in range(TILES):
        own.tick(v.max(best[:, t, :], choice[:, t, :]))
    own.settle(v)
    for t in range(TILES):
        own.tick(v.max_index(index[:, t, :], best[:, t, :], choice[:, t, :]))
    own.settle(v)
    own.tick(v.tensor_copy(indexf[:], index[:]))
    own.settle(v)
    shape = [P, TILES, experts]
    for j in range(k):
        into = picked if j == 0 else hit
        own.tick(v.tensor_tensor(into[:], iota[:, None, 0:experts].to_broadcast(shape),
                                 indexf[:, :, j:j + 1].to_broadcast(shape), ALU.is_equal))
        own.settle(v)
        if j:
            own.tick(v.tensor_tensor(picked[:], picked[:], hit[:], ALU.add))
            own.settle(v)
    own.tick(v.tensor_tensor(picked[:], picked[:], weights[:], ALU.mult))
    own.settle(v)
    own.tick(v.tensor_reduce(total[:], picked[:], AX_X, ALU.add))
    own.settle(v)
    if eps:
        own.tick(v.tensor_scalar(total[:], total[:], eps, None, ALU.add))
        own.settle(v)
    own.tick(v.reciprocal(total[:], total[:]))
    own.settle(v)
    return v.tensor_tensor(comb[:], picked[:], total[:, :, None].to_broadcast(shape), ALU.mult)


def token_expert_ffn(nc, banks, x, hT, ctxT, ident, dram, loads):
    with ExitStack() as ctx:
        sb = lambda n, s, d: ctx.enter_context(nc.sbuf_tensor(n, s, d))
        sem = lambda n: ctx.enter_context(nc.semaphore(n))
        norm = Norm(nc, sb, sem, "ln1", x, hT, banks[4:8], ident)
        raw = sb("ctxT_raw", [P, KD, EA, D], F32)
        token = sb("token", [P, TILES], I32)
        tokenf = sb("tokenf", [P, TILES], F32)
        atleast = sb("atleast", [P, EA, TILES], F32)
        mask = sb("mask", [P, EA, TILES], F32)
        z = sb("z", [P, 2, D], F32)
        silu = sb("silu", [P, 2, D], F32)
        gu = sb("gu", [P, 2, D], F32)
        guT = (sb("guT_hi", [P, 2, KD, P], F32R), sb("guT_lo", [P, 2, KD, P], F32R))

        x_loaded = [sem("x_loaded0"), sem("x_loaded1")]
        ctx_loaded = [sem(f"ctx_loaded{k}") for k in range(KD)]
        token_loaded = sem("token_loaded")
        ident_loaded = sem("ident_loaded")
        ctx_hi = sem("ctx_hi_ready")
        ctx_lo = sem("ctx_lo_ready")
        own = Count(sem("a_vector_own"))
        z_done = sem("z_done")
        z_chosen = sem("z_chosen")
        silu_ready = sem("silu_ready")
        gu_ready = sem("gu_ready")
        gu_turned = sem("gu_transposed")
        guT_hi = sem("guT_hi_ready")
        guT_lo = sem("guT_lo_ready")
        y_done = sem("y_done")
        y_added = sem("y_added")
        block = ctx.enter_context(nc.Block())

        @block.sync
        def _(sp):
            for half in range(2):
                sp.dma_start(x[:, HT * half:HT * half + HT, :],
                             dram["x"][:, HT * half:HT * half + HT, :]).then_inc(x_loaded[half], 16)
                if half == 0:
                    sp.dma_start(ident[:], dram["ident"]).then_inc(ident_loaded, 16)
                sp.dma_start(raw[:, half], dram["ctxT"][:, half]).then_inc(ctx_loaded[half], 16)
            sp.dma_start(token[:], dram["token"]).then_inc(token_loaded, 16)
            for into, source, landed in loads:
                sp.dma_start(into, source).then_inc(landed, 16)

        @block.gpsimd
        def _(p):
            norm.gpsimd(p)

        @block.scalar
        def _(act):
            def split_ctx(k):
                act.wait_ge(ctx_loaded[k], 16)
                for n in range(2):
                    act.activation(ctxT[0][:, k, 2 * n:2 * n + 2, :], raw[:, k, 2 * n:2 * n + 2, :],
                                   ACT.Copy).then_inc(ctx_hi, 1)

            def silu_of(i):
                act.wait_ge(z_chosen, i + 1)
                if i >= 2:
                    act.wait_ge(gu_ready, i - 1)
                act.activation(silu[:, i % 2], z[:, i % 2], ACT.Silu).then_inc(silu_ready, 1)

            split_ctx(0)
            split_ctx(1)
            norm.scalar_hi(act, 0)
            norm.scalar_hi(act, 1)
            silu_of(0)
            for i in range(TILES):
                act.wait_ge(gu_turned, i + 1)
                if i >= 2:
                    act.wait_ge(y_done, i - 1)
                act.activation(guT[0][:, i % 2], banks[6 + i % 2][:, 0:D],
                               ACT.Copy).then_inc(guT_hi, 1)
                if i + 1 < TILES:
                    silu_of(i + 1)

        @block.tensor
        def _(pe):
            def z_of(i):
                norm.wait_half(pe, i // HT)
                if i >= 2:
                    pe.wait_ge(z_chosen, i - 1)
                for n in range(2):
                    for k in range(KD):
                        if i == 0:
                            pe.wait_ge(ctx_hi, 2 * k + n + 1)
                            pe.wait_ge(ctx_lo, 2 * k + n + 1)
                        ins = product(pe, banks[2 * (i % 2) + n][:],
                                      both(hT, slice(None), k, slice(i * P, i * P + P)),
                                      both(ctxT, slice(None), k, slice(2 * n, 2 * n + 2)),
                                      k == 0, k == KD - 1)
                ins.then_inc(z_done, 1)

            pe.wait_ge(ident_loaded, 16)
            norm.tensor(pe, 0)
            norm.tensor(pe, 1)
            z_of(0)
            for i in range(TILES):
                if i == 0:
                    norm.wait_half(pe, 1)
                pe.wait_ge(gu_ready, i + 1)
                if i >= 2:
                    pe.wait_ge(guT_lo, i - 1)
                for k in range(KD):
                    ins = pe.transpose(banks[6 + i % 2][:, k * P:(k + 1) * P],
                                       gu[:, i % 2, k * P:(k + 1) * P], ident[:])
                ins.then_inc(gu_turned, 1)
                if i + 1 < TILES:
                    z_of(i + 1)
                pe.wait_ge(guT_hi, i + 1)
                pe.wait_ge(guT_lo, i + 1)
                if i >= 1:
                    pe.wait_ge(y_added, EA * i)
                for n in range(2):
                    for k in range(KD):
                        ins = product(pe, banks[4 + n][:], both(guT, slice(None), i % 2, k),
                                      both(ctxT, slice(None), k, slice(2 * n, 2 * n + 2)),
                                      k == 0, k == KD - 1)
                ins.then_inc(y_done, 1)

        @block.vector
        def _(v):
            def choose_z(i):
                v.wait_ge(z_done, i + 1)
                if i >= 2:
                    v.wait_ge(gu_ready, i - 1)
                for e in range(EA):
                    ze = banks[2 * (i % 2) + e // 2][:, (e % 2) * D:(e % 2) * D + D]
                    m = mask[:, e, i:i + 1]
                    if e == 0:
                        ins = v.tensor_scalar(z[:, i % 2], ze, m, None, ALU.mult)
                    else:
                        own.settle(v)
                        ins = v.scalar_tensor_tensor(z[:, i % 2], ze, m, z[:, i % 2], ALU.mult, ALU.add)
                    if e < EA - 1:
                        own.tick(ins)
                ins.then_inc(z_chosen, 1)

            def gate_z(i):
                v.wait_ge(silu_ready, i + 1)
                v.wait_ge(z_chosen, i + 1)
                if i >= 2:
                    v.wait_ge(gu_turned, i - 1)
                v.tensor_tensor(gu[:, i % 2], silu[:, i % 2], z[:, i % 2], ALU.mult).then_inc(gu_ready, 1)

            for half in range(2):
                v.wait_ge(x_loaded[half], 16)
                norm.vector_moments(v, half)
            v.wait_ge(token_loaded, 16)
            own.tick(v.tensor_copy(tokenf[:], token[:]))
            own.settle(v)
            for e in range(1, EA):
                own.tick(v.tensor_scalar(atleast[:, e, :], tokenf[:], float(e * PER_EXPERT), None, ALU.is_ge))
            own.settle(v)
            own.tick(v.tensor_scalar(mask[:, 0, :], atleast[:, 1, :], -1.0, 1.0, ALU.mult, ALU.add))
            for e in range(1, EA - 1):
                own.tick(v.tensor_tensor(mask[:, e, :], atleast[:, e, :], atleast[:, e + 1, :], ALU.subtract))
            own.tick(v.tensor_copy(mask[:, EA - 1, :], atleast[:, EA - 1, :]))
            norm.vector_normalize(v, 0)
            norm.vector_normalize(v, 1)
            for k in range(KD):
                for n in range(2):
                    v.wait_ge(ctx_hi, 2 * k + n + 1)
                    v.tensor_tensor(ctxT[1][:, k, 2 * n:2 * n + 2, :], raw[:, k, 2 * n:2 * n + 2, :],
                                    f32(ctxT[0][:, k, 2 * n:2 * n + 2, :]), ALU.subtract).then_inc(ctx_lo, 1)
                norm.vector_lo(v, k)
            own.settle(v)
            choose_z(0)
            gate_z(0)
            for i in range(TILES):
                v.wait_ge(guT_hi, i + 1)
                if i >= 2:
                    v.wait_ge(y_done, i - 1)
                v.tensor_tensor(guT[1][:, i % 2], banks[6 + i % 2][:, 0:D].rearrange("p (k n) -> p k n", k=KD),
                                f32(guT[0][:, i % 2]), ALU.subtract).then_inc(guT_lo, 1)
                if i + 1 < TILES:
                    choose_z(i + 1)
                    gate_z(i + 1)
                v.wait_ge(y_done, i + 1)
                for e in range(EA):
                    if e:
                        v.wait_ge(y_added, EA * i + e)
                    ye = banks[4 + e // 2][:, (e % 2) * D:(e % 2) * D + D]
                    v.scalar_tensor_tensor(x[:, i, :], ye, mask[:, e, i:i + 1], x[:, i, :],
                                           ALU.mult, ALU.add).then_inc(y_added, 1)


def routed_ffn(nc, banks, x, hT, ident, iota, dram, raw, raw_loaded, router, router_loaded):
    with ExitStack() as ctx:
        sb = lambda n, s, d: ctx.enter_context(nc.sbuf_tensor(n, s, d))
        sem = lambda n: ctx.enter_context(nc.semaphore(n))
        norm = Norm(nc, sb, sem, "ln2", x, hT, banks[4:8], ident)
        w = (sb("b_w_hi", [P, 2, WB], F32R), sb("b_w_lo", [P, 2, WB], F32R))
        rw = (sb("router_hi", [P, KD * EB], F32R), sb("router_lo", [P, KD * EB], F32R))
        scores = sb("scores", [P, TILES, EB], F32)
        choice = sb("choice", [P, TILES, EB], F32)
        comb = sb("b_comb", [P, TILES, EB], F32)
        mine = sb("b_comb_of_expert", [P, 2, TILES], F32)
        gate = sb("b_gate", [P, 2, HALF], F32)
        a = sb("b_a", [P, 2, HALF], F32)
        aT = (sb("b_aT_hi", [P, 2, HALF], F32R), sb("b_aT_lo", [P, 2, HALF], F32R))

        own = Count(sem("b_vector_own"))
        wg_hi, wg_lo = sem("b_wg_hi_ready"), sem("b_wg_lo_ready")
        wd_hi, wd_lo = sem("b_wd_hi_ready"), sem("b_wd_lo_ready")
        rw_ready = sem("router_w_ready")
        logits_done = sem("logits_done")
        scores_ready = sem("scores_ready")
        gu_done = sem("b_gate_up_done")
        gate_ready = sem("b_silu_ready")
        a_ready = sem("b_a_ready")
        a_hi = sem("b_aT_hi_ready")
        a_lo = sem("b_aT_lo_ready")
        down_done = sem("b_down_done")
        mine_ready = sem("b_mine_ready")
        added = sem("b_added")
        block = ctx.enter_context(nc.Block())
        PAIRS = EB // 2
        LAST = 2 * (EB + 1) - 1

        @block.sync
        def _(sp):
            def load(e, slot):
                sp.wait_ge(wg_lo, e - 1)
                sp.wait_ge(wd_lo, e - 1)
                sp.dma_start(raw[:, slot, :], dram["wb"][bass.ds(e, 1)].rearrange("a p n -> (a p) n"))\
                    .then_inc(raw_loaded[slot], 16)
            with sp.Fori(0, PAIRS - 1) as i:
                load(i * 2 + 2, 0)
                load(i * 2 + 3, 1)
            load(EB, 0)

        @block.gpsimd
        def _(p):
            def split_lo(e, slot):
                p.wait_ge(wg_hi, e + 1)
                p.tensor_tensor(w[1][:, slot, 0:WG], raw[:, slot, 0:WG], f32(w[0][:, slot, 0:WG]),
                                ALU.subtract).then_inc(wg_lo, 1)
                p.wait_ge(wd_hi, e + 1)
                p.tensor_tensor(w[1][:, slot, WG:], raw[:, slot, WG:], f32(w[0][:, slot, WG:]),
                                ALU.subtract).then_inc(wd_lo, 1)
            split_lo(0, 0)
            norm.gpsimd(p)
            split_lo(1, 1)
            split_lo(2, 0)
            with p.Fori(1, PAIRS) as i:
                split_lo(i * 2 + 1, 1)
                split_lo(i * 2 + 2, 0)

        @block.scalar
        def _(act):
            def unit(u, slot, first=False):
                act.wait_ge(gu_done, u + 1)
                if not first:
                    act.wait_ge(a_ready, u - 1)
                act.activation(gate[:, slot], banks[2 * slot][:], ACT.Silu).then_inc(gate_ready, 1)
                act.wait_ge(a_ready, u + 1)
                if not first:
                    act.wait_ge(down_done, u - 1)
                act.activation(aT[0][:, slot], a[:, slot], ACT.Copy).then_inc(a_hi, 1)

            norm.scalar_hi(act, 0)
            norm.scalar_hi(act, 1)
            act.wait_ge(logits_done, 1)
            act.activation(scores[:], banks[3][:, 0:TILES * EB].rearrange("p (t e) -> p t e", e=EB),
                           ACT.Sigmoid).then_inc(scores_ready, 1)
            unit(0, 0, True)
            unit(1, 1, True)
            with act.Fori(0, PAIRS) as i:
                for c in range(4):
                    unit(i * 4 + 2 + c, c % 2)

        @block.tensor
        def _(pe):
            def gate_up(u, e, half, slot, first=False):
                if half == 0:
                    pe.wait_ge(wg_lo, e + 1)
                if first:
                    norm.wait_half(pe, half)
                else:
                    pe.wait_ge(a_ready, u - 1)
                for m in range(2):
                    for k in range(KD):
                        c = (m * KD + k) * FB
                        ins = product(pe, banks[2 * half + m][:], both(w, slice(None), slot, slice(c, c + FB)),
                                      both(hT, slice(None), k, slice(half * HALF, half * HALF + HALF)),
                                      k == 0, k == KD - 1)
                ins.then_inc(gu_done, 1)

            def down(u, e, half, slot, first=False):
                if half == 0:
                    pe.wait_ge(wd_lo, e + 1)
                pe.wait_ge(a_hi, u + 1)
                pe.wait_ge(a_lo, u + 1)
                if not first:
                    pe.wait_ge(added, u * HT - HT + 1)
                for r in range(HT):
                    ins = product(pe, banks[4 + 2 * half + r // 2][:, (r % 2) * D:(r % 2) * D + D],
                                  both(aT, slice(None), half, slice(r * P, r * P + P)),
                                  both(w, slice(None), slot, slice(WB - D, WB)))
                ins.then_inc(down_done, 1)

            norm.tensor(pe, 0)
            norm.tensor(pe, 1)
            norm.wait_half(pe, 0)
            norm.wait_half(pe, 1)
            pe.wait_ge(rw_ready, 2)
            for t in range(TILES):
                for k in range(KD):
                    ins = product(pe, banks[3][:, t * EB:t * EB + EB],
                                  both(hT, slice(None), k, slice(t * P, t * P + P)),
                                  both(rw, slice(None), slice(k * EB, k * EB + EB)), k == 0, k == KD - 1)
            ins.then_inc(logits_done, 1)
            gate_up(0, 0, 0, 0, True)
            pe.wait_ge(scores_ready, 1)
            gate_up(1, 0, 1, 0, True)
            down(0, 0, 0, 0, True)
            with pe.Fori(0, PAIRS) as i:
                for c in range(4):
                    gate_up(i * 4 + (2 + c), i * 2 + (1 + c // 2), c % 2, (1 + c // 2) % 2)
                    down(i * 4 + (1 + c), i * 2 + (1 + c) // 2, (1 + c) % 2, (1 + c) // 2 % 2)
            down(LAST, EB, 1, 0)

        @block.vector
        def _(v):
            def split_gate_up(e, slot, landed, first=False):
                v.wait_ge(raw_loaded[slot], landed)
                if not first:
                    v.wait_ge(gu_done, e * 2 - 2)
                    v.wait_ge(wg_lo, e - 1)
                v.tensor_copy(w[0][:, slot, 0:WG], raw[:, slot, 0:WG]).then_inc(wg_hi, 1)

            def split_down(e, slot, first=False):
                if not first:
                    v.wait_ge(down_done, e * 2 - 2)
                    v.wait_ge(wd_lo, e - 1)
                v.tensor_copy(w[0][:, slot, WG:], raw[:, slot, WG:]).then_inc(wd_hi, 1)

            def gated(u, slot, first=False):
                v.wait_ge(gate_ready, u + 1)
                if not first:
                    v.wait_ge(a_hi, u - 1)
                    v.wait_ge(a_lo, u - 1)
                v.tensor_tensor(a[:, slot], gate[:, slot], banks[2 * slot + 1][:], ALU.mult).then_inc(a_ready, 1)
                v.wait_ge(a_hi, u + 1)
                if not first:
                    v.wait_ge(down_done, u - 1)
                v.tensor_tensor(aT[1][:, slot], a[:, slot], f32(aT[0][:, slot]), ALU.subtract).then_inc(a_lo, 1)

            def add(u, half, slot):
                v.wait_ge(down_done, u + 1)
                v.wait_ge(added, u * HT + 1)
                for r in range(HT):
                    t = HT * half + r
                    y = banks[4 + 2 * half + r // 2][:, (r % 2) * D:(r % 2) * D + D]
                    v.scalar_tensor_tensor(x[:, t, :], y, mine[:, slot, t:t + 1], x[:, t, :],
                                           ALU.mult, ALU.add).then_inc(added, 1)

            def pair(i, last=False):
                for c in range(4):
                    e = i * 2 + (1 + c // 2)
                    slot = (1 + c // 2) % 2
                    gated(i * 4 + (2 + c), c % 2)
                    add(i * 4 + (1 + c), (1 + c) % 2, (1 + c) // 2 % 2)
                    if c % 2 == 0:
                        own.tick(v.tensor_copy(mine[:, slot, :], comb[:, :, bass.ds(e - 1, 1)]
                                               .rearrange("p t a -> p (t a)")))
                        own.settle(v)
                        if not (last and c == 2):
                            split_down(e + 1, 1 - slot)
                    elif not last:
                        split_gate_up(e + 2, slot, i * 16 + (48 if c == 3 else 32))

            v.memset(mine[:, 0, :], 1.0).then_inc(added, 1)
            split_gate_up(0, 0, 16, True)
            split_down(0, 0, True)
            v.wait_ge(router_loaded, 32)
            v.tensor_copy(rw[0][:], router[:, 0:KD * EB]).then_inc(rw_ready, 1)
            v.wait_ge(rw_ready, 1)
            v.tensor_tensor(rw[1][:], router[:, 0:KD * EB], f32(rw[0][:]), ALU.subtract).then_inc(rw_ready, 1)
            norm.vector_moments(v, 0)
            norm.vector_moments(v, 1)
            norm.vector_normalize(v, 0)
            norm.vector_normalize(v, 1)
            split_gate_up(1, 1, 16, True)
            split_down(1, 1, True)
            norm.vector_lo(v, 0)
            norm.vector_lo(v, 1)
            gated(0, 0, True)
            v.wait_ge(scores_ready, 1)
            own.tick(v.tensor_tensor(choice[:], scores[:],
                                     router[:, None, KD * EB:KD * EB + EB].to_broadcast([P, TILES, EB]), ALU.add))
            own.settle(v)
            gated(1, 1, True)
            split_gate_up(2, 0, 32)
            own.tick(choose(v, own, sb, "b", choice, scores, iota, KB, EB, 1e-20, comb))
            own.settle(v)
            add(0, 0, 0)
            with v.Fori(0, PAIRS - 1) as i:
                own.turn(i, 2)
                pair(i)
            own.turned(PAIRS - 1)
            pair(PAIRS - 1, last=True)
            add(LAST, 1, 0)


def at_least(eng, sem, value):
    if not isinstance(value, int) or value > 0:
        eng.wait_ge(sem, value)


def turns(eng, n, body, own=None, per=0):
    body(0)
    with eng.Fori(1, n - 1) as i:
        if own:
            own.turn(i - 1, per)
        body(i)
    if own:
        own.turned(n - 2)
    body(n - 1)


def attention(nc, banks, x, hT, ctxT, ident, dram):
    GROUPS = KV * B
    UNITS = 2 * REP

    def lies(g):
        return not isinstance(g, int) or 0 <= g < GROUPS

    def ahead(work, g, b, n):
        g, b, n = (g + 1, b + 1, n - UNITS) if n >= UNITS else (g, b, n)
        if lies(g):
            work(g, b, n)

    with ExitStack() as ctx:
        sb = lambda n, s, d: ctx.enter_context(nc.sbuf_tensor(n, s, d))
        sem = lambda n: ctx.enter_context(nc.semaphore(n))
        pair = lambda n, s: (sb(n + "_hi", s, F32R), sb(n + "_lo", s, F32R))
        ALL = slice(None)
        norm = Norm(nc, sb, sem, "ln3", x, hT, banks[4:8], ident)
        raw = sb("c_w_raw", [P, WQ + 2 * WK], F32)
        raw_o = sb("c_wo_raw", [P, WO], F32)
        w = pair("c_w", [P, WQ + 2 * WK])
        wo = pair("c_wo", [P, WO])
        cos, sin = sb("cos", [P, 2, HD], F32), sb("sin", [P, 2, HD], F32)
        headnorm = sb("headnorm", [P, 2, HD], F32)
        cosw = [sb(f"cosw_{n}", [P, 2, HD], F32) for n in "qk"]
        sinw = [sb(f"sinw_{n}", [P, 2, HD], F32) for n in "qk"]
        above = sb("above", [P, P], F32)
        aboveR = sb("above_r", [P, P], F32R)
        identR = sb("ident_r", [P, P], F32R)
        power = sb("c_minus_half", [P, 6], F32)
        NQ = REP * HD
        qs = sb("q_rows", [P, 2, NQ], F32)
        ks = sb("kv_rows", [P, 2, 4 * HD], F32)
        sq = sb("squares", [P, NQ + 2 * HD], F32)
        sums = sb("sums", [P, 6], F32)
        means = sb("means", [P, 6], F32)
        r = sb("r", [P, 4, 2, 6], F32)
        t1 = sb("rope_cos", [P, NQ + HD], F32)
        t2 = sb("rope_sin", [P, NQ + HD], F32)
        qk = sb("qk", [P, 2, NQ + 2 * HD], F32)
        qT = pair("qT", [P, 2, REP, S])
        kT = pair("kT", [P, 2, KEYS])
        V = pair("V", [P, 4, 2, 2, HD])
        negmax = sb("negmax", [P, 2], F32)
        bias = sb("exp_bias", [P, 2], F32)
        total = sb("exp_total", [P, 2], F32)
        rtotal = sb("exp_rtotal", [P, 2], F32)
        probs = sb("probs", [P, 2, KEYS], F32)
        PT = pair("PT", [P, 2, 4, 2, S])
        OT = pair("OT", [P, REP, S])

        def heads(eng, step, own=None, per=0):
            def head(kv):
                for b in range(B):
                    for n in range(UNITS):
                        step(kv * B + b, b, n, kv)
            turns(eng, KV, head, own, per)
            for n in range(UNITS + 3):
                step(GROUPS + n // UNITS, n // UNITS, n % UNITS, KV)

        names = """w_loaded wo_loaded tables_loaded w_hi w_lo wo_hi wo_lo constants power_set projected
            q_copied copied squared roped_q sums_done means_done r_ready roped rope_added qk_ready
            qk_turned qkT_hi qkT_lo v_hi v_lo scores_ready negmax_done bias_ready exp_done rtotal_done
            probs_ready p_turned pT_hi pT_lo pv_done oT_hi oT_lo out_half_done out_done out_added"""
        s = {n: sem("c_" + n) for n in names.split()}
        own = Count(sem("c_vector_own"))
        block = ctx.enter_context(nc.Block())

        def keys_of(j):
            return S + (j + 1) * P

        @block.sync
        def _(sp):
            sp.dma_start(raw[:], dram["wqkv"][0]).then_inc(s["w_loaded"], 16)
            sp.dma_start(raw_o[:], dram["wo"][0]).then_inc(s["wo_loaded"], 16)
            for into, name in ((cos, "cos"), (sin, "sin"), (headnorm, "headnorm"), (above, "above")):
                sp.dma_start(into[:], dram[name]).then_inc(s["tables_loaded"], 16)
            with sp.Fori(1, KV) as kv:
                one = lambda t: t[bass.ds(kv, 1)].rearrange("a p n -> (a p) n")
                sp.wait_ge(s["w_lo"], kv * 2)
                sp.dma_start(raw[:], one(dram["wqkv"])).then_inc(s["w_loaded"], 16)
                sp.wait_ge(s["wo_lo"], kv)
                sp.dma_start(raw_o[:], one(dram["wo"])).then_inc(s["wo_loaded"], 16)

        @block.gpsimd
        def _(p):
            norm.gpsimd(p)
            p.memset(power[:], -0.5).then_inc(s["power_set"], 1)
            p.wait_ge(s["power_set"], 1)
            p.wait_ge(s["constants"], 6)

            def rope(g, b, j):
                n = g * 2 + j
                p.wait_ge(s["copied"], n + 1)
                at_least(p, s["sums_done"], n)
                p.tensor_tensor(sq[:, 0:NQ], qs[:, j], qs[:, j], ALU.mult).then_inc(s["squared"], 1)
                kk = ks[:, j].rearrange("p (c n) -> p c n", c=2)[:, :, 0:HD]
                p.tensor_tensor(sq[:, NQ:].rearrange("p (c n) -> p c n", c=2), kk, kk,
                                ALU.mult).then_inc(s["squared"], 1)
                at_least(p, s["rope_added"], n)
                H2 = HD // 2
                heads = lambda ap: ap.rearrange("p (h d) -> p h d", d=HD)
                for src, at, table, m in ((qs[:, j], slice(0, NQ), 0, REP),
                                          (ks[:, j, 2 * HD:3 * HD], slice(NQ, NQ + HD), 1, 1)):
                    a, o1, o2 = heads(src), heads(t1[:, at]), heads(t2[:, at])
                    wide = lambda t: t[:, None, :].to_broadcast([P, m, t.shape[-1]])
                    p.tensor_tensor(o1, a, wide(cosw[table][:, j]), ALU.mult).then_inc(s["roped_q"], 1)
                    p.tensor_tensor(o2[:, :, 0:H2], a[:, :, H2:], wide(sinw[table][:, j, 0:H2]),
                                    ALU.mult).then_inc(s["roped_q"], 1)
                    ins = p.tensor_tensor(o2[:, :, H2:], a[:, :, 0:H2], wide(sinw[table][:, j, H2:]), ALU.mult)
                    ins.then_inc(s["roped"], 1)
                p.wait_ge(s["means_done"], n + 1)
                at_least(p, s["exp_done"], (g - 3) * UNITS)
                p.tensor_tensor(r[:, b % 4, j, :], means[:], power[:], ALU.pow).then_inc(s["r_ready"], 1)

            for g, j in ((0, 0), (0, 1)):
                rope(g, 0, j)
            for j in range(2):
                rope(1, 1, j)

            def step(g, b, n, kv):
                if n in (3, 7) and lies(g + 2):
                    rope(g + 2, b + 2, n // 4)
            heads(p, step)

        @block.scalar
        def _(act):
            def split_hi(kv, part):
                act.wait_ge(s["w_loaded"], kv * 16 + 16)
                at_least(act, s["projected"], kv * (2 * B))
                at = slice(part * WQ, part * WQ + WQ)
                act.activation(w[0][:, at], raw[:, at], ACT.Copy).then_inc(s["w_hi"], 1)

            def split_wo_hi(kv):
                act.wait_ge(s["wo_loaded"], kv * 16 + 16)
                at_least(act, s["out_done"], kv * B)
                act.activation(wo[0][:], raw_o[:], ACT.Copy).then_inc(s["wo_hi"], 1)

            def copy(g, j):
                n = g * 2 + j
                act.wait_ge(s["projected"], n + 1)
                at_least(act, s["roped"], n * 2 - 2)
                at_least(act, s["qk_ready"], n - 1)
                at_least(act, s["v_lo"], n - 1)
                act.activation(qs[:, j], banks[4][:], ACT.Copy).then_inc(s["q_copied"], 1)
                act.activation(ks[:, j], banks[5][:], ACT.Copy).then_inc(s["copied"], 1)

            def v_hi(g, b, j):
                at_least(act, s["pv_done"], (g - 3) * 2)
                act.wait_ge(s["copied"], g * 2 + j + 1)
                vv = ks[:, j].rearrange("p (c n) -> p c n", c=2)[:, :, HD:2 * HD]
                act.activation(V[0][:, b % 4, :, j, :], vv, ACT.Copy).then_inc(s["v_hi"], 1)

            def qkT_hi(g, b, j):
                act.wait_ge(s["qk_turned"], g * 2 + j + 1)
                at_least(act, s["scores_ready"], (g - 1) * UNITS)
                act.activation(qT[0][:, b % 2, :, j * P:j * P + P],
                               banks[4][:].rearrange("p (h n) -> p h n", h=REP), ACT.Copy).then_inc(s["qkT_hi"], 1)
                act.activation(kT[0][:, b % 2, :].rearrange("p (c n) -> p c n", c=2)[:, :, j * P:j * P + P],
                               banks[5][:, 0:2 * P].rearrange("p (c n) -> p c n", c=2),
                               ACT.Copy).then_inc(s["qkT_hi"], 1)

            def oT_hi(g, half):
                act.wait_ge(s["pv_done"], g * 2 + half + 1)
                at_least(act, s["out_done"] if half else s["out_half_done"], g)
                act.activation(OT[0][:, 2 * half:2 * half + 2, :], banks[6][:].rearrange("p (h n) -> p h n", h=2),
                               ACT.Copy).then_inc(s["oT_hi"], 1)

            def exp(g, b, n):
                u, slot, keys = g * UNITS + n, n % 2, keys_of(n % 2)
                act.wait_ge(s["bias_ready"], u + 1)
                at_least(act, s["p_turned"], u - 1)
                at_least(act, s["probs_ready"], u - 1)
                act.activation(probs[:, slot, 0:keys], banks[slot][:, 0:keys], ACT.Exp,
                               bias=bias[:, slot:slot + 1], scale=r[:, b % 4, n % 2, n // 2:n // 2 + 1],
                               accum_out=total[:, slot:slot + 1]).then_inc(s["exp_done"], 1)

            def divide(g, b, n):
                u, slot, keys = g * UNITS + n, n % 2, keys_of(n % 2)
                act.wait_ge(s["rtotal_done"], u + 1)
                act.activation(probs[:, slot, 0:keys], probs[:, slot, 0:keys], ACT.Copy,
                               scale=rtotal[:, slot:slot + 1]).then_inc(s["probs_ready"], 1)

            def pT_hi(g, n):
                u, j, kt = g * UNITS + n, n % 2, keys_of(n % 2) // P
                act.wait_ge(s["p_turned"], u + 1)
                at_least(act, s["pv_done"], g * 2 + n // 4 - 1)
                act.activation(PT[0][:, n // 4, 0:kt, n // 2 % 2, j * P:j * P + P],
                               banks[2 + j][:, 0:kt * P].rearrange("p (k n) -> p k n", k=kt),
                               ACT.Copy).then_inc(s["pT_hi"], 1)

            split_hi(0, 0)
            split_hi(0, 1)
            norm.scalar_hi(act, 0)
            norm.scalar_hi(act, 1)
            act.wait_ge(s["tables_loaded"], 64)
            act.activation(aboveR[:], above[:], ACT.Copy).then_inc(s["constants"], 1)
            act.activation(identR[:], ident[:], ACT.Copy).then_inc(s["constants"], 1)
            copy(0, 0)
            copy(0, 1)
            v_hi(0, 0, 0)
            v_hi(0, 0, 1)
            qkT_hi(0, 0, 0)
            copy(1, 0)
            qkT_hi(0, 0, 1)
            copy(1, 1)
            exp(0, 0, 0)
            divide(0, 0, 0)

            def step(g, b, n, kv):
                ahead(exp, g, b, n + 1)
                if n == 0:
                    if lies(g - 1):
                        oT_hi(g - 1, 0)
                    if b == 2 and lies(g + 2):
                        split_hi(kv + 1, 1)
                if n == 1:
                    if lies(g + 1):
                        qkT_hi(g + 1, b + 1, 0)
                        v_hi(g + 1, b + 1, 0)
                        v_hi(g + 1, b + 1, 1)
                    if b == 1 and lies(g):
                        split_wo_hi(kv)
                if n == 3 and lies(g + 2):
                    copy(g + 2, 0)
                if n == 4 and lies(g - 1):
                    oT_hi(g - 1, 1)
                if n == 5 and lies(g + 1):
                    qkT_hi(g + 1, b + 1, 1)
                if n == 7 and lies(g + 2):
                    copy(g + 2, 1)
                    if b == 1 and lies(g + 3):
                        split_hi(kv + 1, 0)
                if lies(g):
                    pT_hi(g, n)
                ahead(divide, g, b, n + 1)
            heads(act, step)

        @block.tensor
        def _(pe):
            def project(g, b, j, pieces=range(4)):
                n, b = g * 2 + j, b % B
                own_rows = both(hT, ALL, slice(0, KD), slice((2 * b + j) * P, (2 * b + j) * P + P))
                ctx_rows = both(ctxT, ALL, slice(0, KD), b, slice(j * P, j * P + P))
                if 0 in pieces:
                    if isinstance(n, int) and n < 2:
                        at_least(pe, s["copied"], n)
                    else:
                        pe.wait_ge(s["qkT_hi"], n * 2 - 2)
                        pe.wait_ge(s["qkT_lo"], n * 2 - 2)
                for piece in pieces:
                    if piece < KD:
                        c = piece * NQ
                        product(pe, banks[4][:], both(own_rows, ALL, piece), both(w, ALL, slice(c, c + NQ)),
                                piece == 0, piece == KD - 1)
                        continue
                    rows, at, out = ((ctx_rows, WQ, banks[5][:, 0:2 * HD]) if piece == 2 else
                                     (own_rows, WQ + WK, banks[5][:, 2 * HD:]))
                    for k in range(KD):
                        c = at + k * 2 * HD
                        ins = product(pe, out, both(rows, ALL, k), both(w, ALL, slice(c, c + 2 * HD)),
                                      k == 0, k == KD - 1)
                if 3 in pieces:
                    ins.then_inc(s["projected"], 1)

            def wait_weights(kv):
                pe.wait_ge(s["w_hi"], kv * 2 + 2)
                pe.wait_ge(s["w_lo"], kv * 2 + 2)

            def turn_qk(g, j, copied):
                n = g * 2 + j
                pe.wait_ge(s["qk_ready"], n + 1)
                pe.wait_ge(s["copied"], copied)
                for h in range(REP):
                    pe.transpose(banks[4][:, h * P:h * P + P], qk[:, j, h * HD:h * HD + HD], ident[:])
                pe.transpose(banks[5][:, 0:P], qk[:, j, NQ + HD:], ident[:])
                pe.transpose(banks[5][:, P:2 * P], qk[:, j, NQ:NQ + HD], ident[:]).then_inc(s["qk_turned"], 1)

            def scores(g, b, n):
                u, j, h, keys = g * UNITS + n, n % 2, n // 2, keys_of(n % 2)
                if n == 0:
                    pe.wait_ge(s["qkT_hi"], g * 4 + 4)
                    pe.wait_ge(s["qkT_lo"], g * 4 + 4)
                at_least(pe, s["exp_done"], u - 1)
                out = banks[j]
                product(pe, out[:, 0:keys], both(qT, ALL, b % 2, h, slice(j * P, j * P + P)),
                        both(kT, ALL, b % 2, slice(0, keys)), True, False, shared=True)
                pe.matmul(out[:, keys - P:keys], identR[:], aboveR[:], start=False, stop=True,
                          skip_group_check=True).then_inc(s["scores_ready"], 1)

            def turn_p(g, n):
                u, j, kt = g * UNITS + n, n % 2, keys_of(n % 2) // P
                pe.wait_ge(s["probs_ready"], u + 1)
                at_least(pe, s["pT_hi"], u - 1)
                at_least(pe, s["pT_lo"], u - 1)
                for k in range(kt):
                    ins = pe.transpose(banks[2 + j][:, k * P:k * P + P], probs[:, j, k * P:k * P + P], ident[:])
                ins.then_inc(s["p_turned"], 1)

            def values(g, b, half, key_tiles):
                if 0 in key_tiles:
                    pe.wait_ge(s["pT_hi"], g * UNITS + 4 * half + 4)
                    pe.wait_ge(s["pT_lo"], g * UNITS + 4 * half + 4)
                    pe.wait_ge(s["v_lo"], g * 2 + 2)
                    at_least(pe, s["oT_hi"], g * 2 + half)
                    at_least(pe, s["oT_lo"], g * 2 + half)
                out = banks[6][:].rearrange("p (h n) -> p h n", h=2)
                for kt in key_tiles:
                    at = slice(P if kt == 3 else 0, S)
                    ins = product(pe, out[:, :, at], both(V, ALL, b % 4, kt // 2, kt % 2),
                                  both(PT, ALL, half, kt, ALL, at), kt == 0, kt == 3, shared=True)
                if 3 in key_tiles:
                    ins.then_inc(s["pv_done"], 1)

            def project_out(g, kv, j, half):
                if half == 0 and j == 0:
                    pe.wait_ge(s["oT_hi"], g * 2 + 1)
                    pe.wait_ge(s["oT_lo"], g * 2 + 1)
                    pe.wait_ge(s["wo_lo"], kv + 1)
                    at_least(pe, s["out_added"], g)
                if half == 1 and j == 0:
                    pe.wait_ge(s["oT_hi"], g * 2 + 2)
                    pe.wait_ge(s["oT_lo"], g * 2 + 2)
                for h in range(2 * half, 2 * half + 2):
                    ins = product(pe, banks[7][:, j * D:j * D + D], both(OT, ALL, h, slice(j * P, j * P + P)),
                                  both(wo, ALL, slice(h * D, h * D + D)), j == 0 and h == 0, h == REP - 1,
                                  shared=True)
                if j == 1:
                    ins.then_inc(s["out_done"] if half else s["out_half_done"], 1)

            norm.tensor(pe, 0)
            norm.tensor(pe, 1)
            norm.wait_half(pe, 0)
            norm.wait_half(pe, 1)
            wait_weights(0)
            project(0, 0, 0)
            project(0, 0, 1)
            turn_qk(0, 0, 2)
            project(1, 1, 0)
            turn_qk(0, 1, 3)
            project(1, 1, 1)
            pe.wait_ge(s["constants"], 6)
            scores(0, 0, 0)
            scores(0, 0, 1)

            def step(g, b, n, kv):
                before = kv if b else kv - 1
                ahead(scores, g, b, n + 2)
                if n == 0:
                    if lies(g + 1):
                        turn_qk(g + 1, 0, g * 2 + 4)
                    if lies(g - 2):
                        project_out(g - 2, None, 1, 1)
                if n in (1, 2, 3) and lies(g - 1):
                    values(g - 1, b - 1, 1, ((0, 1), (2,), (3,))[n - 1])
                if n == 2 and lies(g + 2):
                    project(g + 2, b + 2, 0, (1,))
                if n == 3 and lies(g - 1):
                    project_out(g - 1, before, 0, 0)
                if n == 4:
                    if lies(g + 1):
                        turn_qk(g + 1, 1, g * 2 + 5 if lies(g + 2) else g * 2 + 4)
                    if lies(g - 1):
                        project_out(g - 1, before, 1, 0)
                if n in (5, 6, 7) and lies(g):
                    values(g, b, 0, ((0, 1), (2,), (3,))[n - 5])
                if n == 6 and lies(g + 2):
                    project(g + 2, b + 2, 1, (1,))
                if n == 7 and lies(g - 1):
                    project_out(g - 1, before, 0, 1)
                if lies(g):
                    turn_p(g, n)
                if lies(g + 2):
                    if n == 1:
                        if b == 2:
                            wait_weights(kv + 1)
                        project(g + 2, b + 2, 0, (0,))
                    if n == 2:
                        project(g + 2, b + 2, 0, (2, 3))
                    if n == 5:
                        project(g + 2, b + 2, 1, (0,))
                    if n == 6:
                        project(g + 2, b + 2, 1, (2, 3))
            heads(pe, step)

        @block.vector
        def _(v):
            def split_lo(kv, part):
                v.wait_ge(s["w_hi"], kv * 2 + part + 1)
                at_least(v, s["projected"], kv * (2 * B))
                at = slice(part * WQ, part * WQ + WQ)
                v.tensor_tensor(w[1][:, at], raw[:, at], f32(w[0][:, at]), ALU.subtract).then_inc(s["w_lo"], 1)

            def split_wo_lo(kv):
                v.wait_ge(s["wo_hi"], kv + 1)
                v.tensor_tensor(wo[1][:], raw_o[:], f32(wo[0][:]), ALU.subtract).then_inc(s["wo_lo"], 1)

            def v_lo(g, b, j):
                v.wait_ge(s["v_hi"], g * 2 + j + 1)
                vv = ks[:, j].rearrange("p (c n) -> p c n", c=2)[:, :, HD:2 * HD]
                v.tensor_tensor(V[1][:, b % 4, :, j, :], vv, f32(V[0][:, b % 4, :, j, :]),
                                ALU.subtract).then_inc(s["v_lo"], 1)

            def sum_squares(g, j):
                n = g * 2 + j
                v.wait_ge(s["squared"], n * 2 + 2)
                v.tensor_reduce(sums[:], sq[:].rearrange("p (h d) -> p h d", d=HD), AX_X,
                                ALU.add).then_inc(s["sums_done"], 1)
                v.wait_ge(s["sums_done"], n + 1)
                at_least(v, s["r_ready"], n)
                v.tensor_scalar(means[:], sums[:], 1.0 / HD, RMS_EPS, ALU.mult,
                                ALU.add).then_inc(s["means_done"], 1)

            def add_rope(g, b, j):
                n = g * 2 + j
                v.wait_ge(s["roped"], n * 2 + 2)
                v.wait_ge(s["r_ready"], n + 1)
                at_least(v, s["qk_turned"], n - 1)
                v.tensor_tensor(qk[:, j, 0:NQ + HD], t1[:], t2[:], ALU.add).then_inc(s["rope_added"], 1)
                own.tick(v.scalar_tensor_tensor(qk[:, j, NQ + HD:], ks[:, j, 0:HD], r[:, b % 4, j, 4:5],
                                                headnorm[:, 1, :], ALU.mult, ALU.mult))
                own.settle(v)
                v.wait_ge(s["rope_added"], n + 1)
                v.tensor_scalar(qk[:, j, NQ:NQ + HD], qk[:, j, NQ:NQ + HD], r[:, b % 4, j, 5:6], None,
                                ALU.mult).then_inc(s["qk_ready"], 1)

            def qkT_lo(g, b, j):
                v.wait_ge(s["qkT_hi"], g * 4 + 2 * j + 2)
                at = (ALL, b % 2, ALL, slice(j * P, j * P + P))
                v.tensor_tensor(qT[1][at], banks[4][:].rearrange("p (h n) -> p h n", h=REP), f32(qT[0][at]),
                                ALU.subtract).then_inc(s["qkT_lo"], 1)
                part = lambda t: t[:, b % 2, :].rearrange("p (c n) -> p c n", c=2)[:, :, j * P:j * P + P]
                v.tensor_tensor(part(kT[1]), banks[5][:, 0:2 * P].rearrange("p (c n) -> p c n", c=2),
                                f32(part(kT[0])), ALU.subtract).then_inc(s["qkT_lo"], 1)

            def oT_lo(g, half):
                v.wait_ge(s["oT_hi"], g * 2 + half + 1)
                v.tensor_tensor(OT[1][:, 2 * half:2 * half + 2, :], banks[6][:].rearrange("p (h n) -> p h n", h=2),
                                f32(OT[0][:, 2 * half:2 * half + 2, :]), ALU.subtract).then_inc(s["oT_lo"], 1)

            def row_max(g, b, n):
                u, slot, keys = g * UNITS + n, n % 2, keys_of(n % 2)
                if n == 0:
                    v.wait_ge(s["r_ready"], g * 2 + 2)
                v.wait_ge(s["scores_ready"], u + 1)
                at_least(v, s["bias_ready"], u - 1)
                v.tensor_reduce(negmax[:, slot:slot + 1], banks[slot][:, 0:keys], AX_X, ALU.max,
                                negate=True).then_inc(s["negmax_done"], 1)
                v.wait_ge(s["negmax_done"], u + 1)
                at_least(v, s["exp_done"], u - 1)
                v.tensor_tensor(bias[:, slot:slot + 1], negmax[:, slot:slot + 1],
                                r[:, b % 4, n % 2, n // 2:n // 2 + 1], ALU.mult).then_inc(s["bias_ready"], 1)

            def pT_lo(g, n):
                u, j, kt = g * UNITS + n, n % 2, keys_of(n % 2) // P
                v.wait_ge(s["pT_hi"], u + 1)
                at = (ALL, n // 4, slice(0, kt), n // 2 % 2, slice(j * P, j * P + P))
                v.tensor_tensor(PT[1][at], banks[2 + j][:, 0:kt * P].rearrange("p (k n) -> p k n", k=kt),
                                f32(PT[0][at]), ALU.subtract).then_inc(s["pT_lo"], 1)

            def row_sum(g, b, n):
                u, slot = g * UNITS + n, n % 2
                v.wait_ge(s["exp_done"], u + 1)
                at_least(v, s["probs_ready"], u - 1)
                v.reciprocal(rtotal[:, slot:slot + 1], total[:, slot:slot + 1]).then_inc(s["rtotal_done"], 1)

            def add_out(g, b):
                v.wait_ge(s["out_done"], g + 1)
                at_least(v, s["out_added"], g)
                at = slice(2 * (b % B), 2 * (b % B) + 2)
                v.tensor_tensor(x[:, at, :], banks[7][:].rearrange("p (j d) -> p j d", j=2), x[:, at, :],
                                ALU.add).then_inc(s["out_added"], 1)

            norm.vector_moments(v, 0)
            norm.vector_moments(v, 1)
            v.wait_ge(s["tables_loaded"], 64)
            H2 = HD // 2
            for m, scale in ((0, SCALE), (1, 1.0)):
                wide = headnorm[:, m:m + 1, :].to_broadcast([P, 2, HD])
                own.tick(v.scalar_tensor_tensor(cosw[m][:], cos[:], scale, wide, ALU.mult, ALU.mult))
                own.tick(v.scalar_tensor_tensor(sinw[m][:, :, 0:H2], sin[:, :, 0:H2], scale, wide[:, :, H2:],
                                                ALU.mult, ALU.mult))
                own.settle(v)
                v.scalar_tensor_tensor(sinw[m][:, :, H2:], sin[:, :, H2:], scale, wide[:, :, 0:H2],
                                       ALU.mult, ALU.mult).then_inc(s["constants"], 2)
            norm.vector_normalize(v, 0)
            norm.vector_normalize(v, 1)
            split_lo(0, 0)
            split_lo(0, 1)
            norm.vector_lo(v, 0)
            norm.vector_lo(v, 1)
            sum_squares(0, 0)
            add_rope(0, 0, 0)
            sum_squares(0, 1)
            v_lo(0, 0, 0)
            v_lo(0, 0, 1)
            add_rope(0, 0, 1)
            qkT_lo(0, 0, 0)
            sum_squares(1, 0)
            qkT_lo(0, 0, 1)
            add_rope(1, 1, 0)
            row_max(0, 0, 0)
            row_max(0, 0, 1)
            row_sum(0, 0, 0)

            def step(g, b, n, kv):
                if n and lies(g):
                    pT_lo(g, n - 1)
                if n == 0 and lies(g - 1):
                    pT_lo(g - 1, UNITS - 1)
                ahead(row_max, g, b, n + 2)
                ahead(row_sum, g, b, n + 1)
                if n == 0:
                    if lies(g - 1):
                        oT_lo(g - 1, 0)
                    if b == 2 and lies(g + 2):
                        split_lo(kv + 1, 1)
                if n == 1:
                    if lies(g + 1):
                        qkT_lo(g + 1, b + 1, 0)
                        sum_squares(g + 1, 1)
                    if b == 1 and lies(g):
                        split_wo_lo(kv)
                if n == 2:
                    if lies(g - 2):
                        add_out(g - 2, b - 2)
                    if lies(g + 1):
                        v_lo(g + 1, b + 1, 0)
                        v_lo(g + 1, b + 1, 1)
                if n == 3 and lies(g + 1):
                    add_rope(g + 1, b + 1, 1)
                if n == 4 and lies(g - 1):
                    oT_lo(g - 1, 1)
                if n == 5:
                    if lies(g + 1):
                        qkT_lo(g + 1, b + 1, 1)
                    if lies(g + 2):
                        sum_squares(g + 2, 0)
                if n == 7 and lies(g + 2):
                    add_rope(g + 2, b + 2, 0)
                    if b == 1 and lies(g + 3):
                        split_lo(kv + 1, 0)
            heads(v, step, own, 2 * B)


def top2_ffn(nc, banks, x, hT, ident, iota, dram, out):
    CH = ED * CHUNKS
    with ExitStack() as ctx:
        sb = lambda n, s, d: ctx.enter_context(nc.sbuf_tensor(n, s, d))
        sem = lambda n: ctx.enter_context(nc.semaphore(n))
        pair = lambda n, s: (sb(n + "_hi", s, F32R), sb(n + "_lo", s, F32R))
        ALL = slice(None)
        norm = Norm(nc, sb, sem, "ln4", x, hT, banks[4:8], ident)
        raw1 = sb("w1_raw", [P, 2, KD * P], F32)
        raw2 = sb("w2_raw", [P, 2, D], F32)
        w1 = pair("w1", [P, 2, KD * P])
        w2 = pair("w2", [P, 2, D])
        b1 = sb("b1", [P, CH], F32)
        b1e = sb("b1_of_expert", [P, CHUNKS], F32)
        b2raw = sb("b2_raw", [ED, D], F32)
        b2 = pair("b2", [ED, D])
        gate = sb("gate_w", [P, KD * ED + ED], F32)
        gw = pair("gate_split", [P, KD * ED])
        logits = sb("logits", [P, TILES, ED], F32)
        top = sb("logits_max", [P, TILES], F32)
        exps = sb("gate_exps", [P, TILES, ED], F32)
        gsum = sb("gate_sum", [P, TILES], F32)
        gprobs = sb("gate_probs", [P, TILES, ED], F32)
        comb = sb("d_comb", [P, TILES, ED], F32)
        mine = sb("d_comb_of_expert", [P, TILES], F32)
        combT = pair("combT", [ED, 2, HALF])
        g = sb("d_gelu", [P, 2, HALF], F32)
        aT = pair("d_aT", [P, 2, B * S])

        names = """w1_loaded0 w1_loaded1 w2_loaded0 w2_loaded1 small_loaded w1_hi w1_lo w2_hi w2_lo
            small_hi small_lo logits_done logits_shifted exps_ready comb_ready combT_done combT_hi combT_lo
            bias_done b1_ready up_done gelu_ready aT_hi aT_lo down_done added stored"""
        s = {n: sem("d_" + n) for n in names.split()}
        own = Count(sem("d_vector_own"))
        block = ctx.enter_context(nc.Block())

        def lies(q):
            return not isinstance(q, int) or q < CH

        @block.sync
        def _(sp):
            def load(q, slot):
                one = dram["wd"][q] if isinstance(q, int) else \
                    dram["wd"][bass.ds(q, 1)].rearrange("a p n -> (a p) n")
                at_least(sp, s["w1_lo"], q - 1)
                sp.dma_start(raw1[:, slot], one[:, 0:KD * P]).then_inc(s[f"w1_loaded{slot}"], 16)
                at_least(sp, s["w2_lo"], q - 1)
                sp.dma_start(raw2[:, slot], one[:, KD * P:]).then_inc(s[f"w2_loaded{slot}"], 16)
            load(0, 0)
            for into, name in ((gate, "gate"), (b1, "b1"), (b2raw, "b2")):
                sp.dma_start(into[:], dram[name]).then_inc(s["small_loaded"], 16)
            load(1, 1)
            with sp.Fori(1, CH // 2) as i:
                load(i * 2, 0)
                load(i * 2 + 1, 1)
            for t in range(0, TILES, 2):
                sp.wait_ge(s["added"], (ED - 1) * TILES + 4 + t + 2)
                sp.dma_start(out[:, t:t + 2, :], x[:, t:t + 2, :]).then_inc(s["stored"], 16)
            sp.wait_ge(s["stored"], 16 * (TILES // 2))

        @block.gpsimd
        def _(p):
            def lo1(q, slot):
                p.wait_ge(s["w1_hi"], q + 1)
                p.tensor_tensor(w1[1][:, slot], raw1[:, slot], f32(w1[0][:, slot]),
                                ALU.subtract).then_inc(s["w1_lo"], 1)

            def lo2(q, slot):
                p.wait_ge(s["w2_hi"], q + 1)
                p.tensor_tensor(w2[1][:, slot], raw2[:, slot], f32(w2[0][:, slot]),
                                ALU.subtract).then_inc(s["w2_lo"], 1)

            lo1(0, 0)
            lo2(0, 0)
            lo1(1, 1)
            norm.gpsimd(p)

            def expert(e):
                for c in range(CHUNKS):
                    q = e * CHUNKS + c
                    if lies(q + 1):
                        lo2(q + 1, (c + 1) % 2)
                    if lies(q + 2):
                        lo1(q + 2, c % 2)
            turns(p, ED, expert)

        @block.scalar
        def _(act):
            norm.scalar_hi(act, 0)
            norm.scalar_hi(act, 1)
            act.wait_ge(s["small_loaded"], 48)
            act.wait_ge(s["logits_shifted"], 1)
            act.activation(exps[:], logits[:], ACT.Exp).then_inc(s["exps_ready"], 1)

            def unit(q, c, half):
                act.wait_ge(s["up_done"], q * 2 + half + 1)
                at_least(act, s["aT_hi"], q * 2 + half - 1)
                at_least(act, s["aT_lo"], q * 2 + half - 1)
                act.activation(g[:, half], banks[2 * (c % 2) + half][:], ACT.Gelu_apprx_tanh,
                               bias=b1e[:, c:c + 1]).then_inc(s["gelu_ready"], 1)
                act.wait_ge(s["gelu_ready"], q * 2 + half + 1)
                at_least(act, s["down_done"], q - 1)
                act.activation(aT[0][:, c % 2, half * HALF:(half + 1) * HALF], g[:, half],
                               ACT.Copy).then_inc(s["aT_hi"], 1)

            def expert(e):
                at = slice(e * CHUNKS, e * CHUNKS + CHUNKS) if isinstance(e, int) else bass.ds(e * CHUNKS, CHUNKS)
                act.activation(b1e[:], b1[:, at], ACT.Copy).then_inc(s["b1_ready"], 1)
                act.wait_ge(s["b1_ready"], e + 1)
                for c in range(CHUNKS):
                    for half in range(2):
                        unit(e * CHUNKS + c, c, half)
                    if isinstance(e, int) and e == 0 and c == 0:
                        act.wait_ge(s["combT_done"], 2)
                        for half in range(2):
                            act.activation(combT[0][:, half], banks[6 + half][0:ED, :],
                                           ACT.Copy).then_inc(s["combT_hi"], 1)
            turns(act, ED, expert)

        @block.tensor
        def _(pe):
            def up(q, c):
                pe.wait_ge(s["w1_lo"], q + 1)
                for half in range(2):
                    at_least(pe, s["gelu_ready"], (q - 2) * 2 + half + 1)
                    for k in range(KD):
                        ins = product(pe, banks[2 * (c % 2) + half][:],
                                      both(w1, ALL, c % 2, slice(k * P, k * P + P)),
                                      both(hT, ALL, k, slice(half * HALF, half * HALF + HALF)), k == 0, k == KD - 1)
                    ins.then_inc(s["up_done"], 1)

            def down(e, q, c):
                pe.wait_ge(s["w2_lo"], q + 1)
                for t in range(TILES):
                    if t % HT == 0:
                        pe.wait_ge(s["aT_lo"], q * 2 + t // HT + 1)
                    if c == 0 and t % 2 == 0:
                        pe.wait_ge(s["added"], 4 if isinstance(e, int) and e == 0 else (e - 1) * TILES + 4 + t + 2)
                    ins = product(pe, banks[4 + t // 2][:, (t % 2) * D:(t % 2) * D + D],
                                  both(aT, ALL, c % 2, slice(t * P, t * P + P)), both(w2, ALL, c % 2),
                                  c == 0 and t % 2 == 0, c == CHUNKS - 1, shared=True)
                ins.then_inc(s["down_done"], 1)

            norm.tensor(pe, 0)
            norm.tensor(pe, 1)
            norm.wait_half(pe, 0)
            norm.wait_half(pe, 1)
            pe.wait_ge(s["small_lo"], 2)
            for t in range(TILES):
                for k in range(KD):
                    ins = product(pe, banks[2][:, t * ED:t * ED + ED], both(hT, ALL, k, slice(t * P, t * P + P)),
                                  both(gw, ALL, slice(k * ED, k * ED + ED)), k == 0, k == KD - 1)
            ins.then_inc(s["logits_done"], 1)
            up(0, 0)
            pe.wait_ge(s["logits_shifted"], 1)

            def expert(e):
                for c in range(CHUNKS):
                    q = e * CHUNKS + c
                    if lies(q + 1):
                        up(q + 1, c + 1)
                    if isinstance(e, int) and e == 0 and c == 0:
                        pe.wait_ge(s["comb_ready"], 1)
                        for half in range(2):
                            for i in range(HT):
                                ins = pe.transpose(banks[6 + half][0:ED, i * P:i * P + P],
                                                   comb[:, HT * half + i, :], ident[:])
                            ins.then_inc(s["combT_done"], 1)
                        pe.wait_ge(s["combT_hi"], 2)
                        pe.wait_ge(s["combT_lo"], 2)
                        for t in range(TILES):
                            ins = product(pe, banks[4 + t // 2][:, (t % 2) * D:(t % 2) * D + D],
                                          both(combT, ALL, t // HT, slice(t % HT * P, t % HT * P + P)),
                                          both(b2, ALL, ALL))
                        ins.then_inc(s["bias_done"], 1)
                    down(e, q, c)
            turns(pe, ED, expert)

        @block.vector
        def _(v):
            def hi1(q, slot):
                at_least(v, s["up_done"], q * 2 - 2)
                at_least(v, s["w1_lo"], q - 1)
                v.wait_ge(s[f"w1_loaded{slot}"], (q - slot) * 8 + 16)
                v.tensor_copy(w1[0][:, slot], raw1[:, slot]).then_inc(s["w1_hi"], 1)

            def hi2(q, slot):
                at_least(v, s["down_done"], q - 1)
                at_least(v, s["w2_lo"], q - 1)
                v.wait_ge(s[f"w2_loaded{slot}"], (q - slot) * 8 + 16)
                v.tensor_copy(w2[0][:, slot], raw2[:, slot]).then_inc(s["w2_hi"], 1)

            def lo(q, c, half):
                v.wait_ge(s["aT_hi"], q * 2 + half + 1)
                v.tensor_tensor(aT[1][:, c % 2, half * HALF:(half + 1) * HALF], g[:, half],
                                f32(aT[0][:, c % 2, half * HALF:(half + 1) * HALF]),
                                ALU.subtract).then_inc(s["aT_lo"], 1)

            def add(e):
                v.wait_ge(s["down_done"], (e + 1) * CHUNKS)
                v.wait_ge(s["added"], e * TILES + 4)
                column = comb[:, :, e:e + 1] if isinstance(e, int) else comb[:, :, bass.ds(e, 1)]
                own.tick(v.tensor_copy(mine[:], column.rearrange("p t a -> p (t a)")))
                own.settle(v)
                for t in range(TILES):
                    v.scalar_tensor_tensor(x[:, t, :], banks[4 + t // 2][:, (t % 2) * D:(t % 2) * D + D],
                                           mine[:, t:t + 1], x[:, t, :], ALU.mult, ALU.add).then_inc(s["added"], 1)

            hi1(0, 0)
            hi2(0, 0)
            hi1(1, 1)
            v.wait_ge(s["small_loaded"], 48)
            v.tensor_copy(gw[0][:], gate[:, 0:KD * ED]).then_inc(s["small_hi"], 1)
            v.tensor_copy(b2[0][:], b2raw[:]).then_inc(s["small_hi"], 1)
            norm.vector_moments(v, 0)
            norm.vector_moments(v, 1)
            v.wait_ge(s["small_hi"], 2)
            v.tensor_tensor(gw[1][:], gate[:, 0:KD * ED], f32(gw[0][:]), ALU.subtract).then_inc(s["small_lo"], 1)
            v.tensor_tensor(b2[1][:], b2raw[:], f32(b2[0][:]), ALU.subtract).then_inc(s["small_lo"], 1)
            norm.vector_normalize(v, 0)
            norm.vector_normalize(v, 1)
            norm.vector_lo(v, 0)
            norm.vector_lo(v, 1)
            shape = [P, TILES, ED]
            v.wait_ge(s["logits_done"], 1)
            own.tick(v.tensor_tensor(logits[:], banks[2][:, 0:TILES * ED].rearrange("p (t e) -> p t e", e=ED),
                                     gate[:, None, KD * ED:].to_broadcast(shape), ALU.add))
            own.settle(v)
            own.tick(v.tensor_reduce(top[:], logits[:], AX_X, ALU.max))
            own.settle(v)
            v.tensor_tensor(logits[:], logits[:], top[:, :, None].to_broadcast(shape),
                            ALU.subtract).then_inc(s["logits_shifted"], 1)
            v.wait_ge(s["exps_ready"], 1)
            own.tick(v.tensor_reduce(gsum[:], exps[:], AX_X, ALU.add))
            own.settle(v)
            own.tick(v.reciprocal(gsum[:], gsum[:]))
            own.settle(v)
            own.tick(v.tensor_tensor(gprobs[:], exps[:], gsum[:, :, None].to_broadcast(shape), ALU.mult))
            own.settle(v)
            choose(v, own, sb, "d", gprobs, gprobs, iota, KDTOP, ED, 0.0, comb).then_inc(s["comb_ready"], 1)
            v.wait_ge(s["comb_ready"], 1)

            def expert(e):
                for c in range(CHUNKS):
                    q = e * CHUNKS + c
                    lo(q, c, 0)
                    lo(q, c, 1)
                    if isinstance(e, int) and e == 0:
                        if c == 0:
                            v.wait_ge(s["combT_hi"], 2)
                            for half in range(2):
                                v.tensor_tensor(combT[1][:, half], banks[6 + half][0:ED, :],
                                                f32(combT[0][:, half]), ALU.subtract).then_inc(s["combT_lo"], 1)
                            v.wait_ge(s["bias_done"], 1)
                            for i in range(4):
                                v.tensor_tensor(x[:, 2 * i:2 * i + 2, :],
                                                banks[4 + i][:].rearrange("p (t d) -> p t d", t=2),
                                                x[:, 2 * i:2 * i + 2, :], ALU.add).then_inc(s["added"], 1)
                    elif c == 0:
                        add(e - 1)
                    if lies(q + 1):
                        hi2(q + 1, (c + 1) % 2)
                    if lies(q + 2):
                        hi1(q + 2, c % 2)
            turns(v, ED, expert, own, 1)
            add(ED - 1)


STAGES = 4


def program(nc, dram, out):
    with ExitStack() as ctx:
        sb = lambda n, s, d: ctx.enter_context(nc.sbuf_tensor(n, s, d))
        sem = lambda n: ctx.enter_context(nc.semaphore(n))
        banks = [ctx.enter_context(nc.psum_tensor(f"bank{i}", [P, HALF], F32)) for i in range(8)]
        x = sb("x", [P, TILES, D], F32)
        hT = (sb("hT_hi", [P, KD, B * S], F32R), sb("hT_lo", [P, KD, B * S], F32R))
        ctxT = (sb("ctxT_hi", [P, KD, B, S], F32R), sb("ctxT_lo", [P, KD, B, S], F32R))
        ident = sb("ident", [P, P], F32)
        iota = sb("iota", [P, EB], F32)
        router = sb("router", [P, KD * EB + EB], F32)
        router_loaded = sem("router_loaded")
        with ExitStack() as part:
            raw_b = part.enter_context(nc.sbuf_tensor("b_w_raw", [P, 2, WB], F32))
            raw_b_loaded = [sem("b_w_loaded0"), sem("b_w_loaded1")]
            loads = [(iota[:], dram["iota"], router_loaded), (router[:], dram["router"], router_loaded),
                     (raw_b[:, 0, :], dram["wb"][0], raw_b_loaded[0]),
                     (raw_b[:, 1, :], dram["wb"][1], raw_b_loaded[1])]
            token_expert_ffn(nc, banks, x, hT, ctxT, ident, dram, loads)
            if STAGES >= 2:
                routed_ffn(nc, banks, x, hT, ident, iota, dram, raw_b, raw_b_loaded, router, router_loaded)
        if STAGES >= 3:
            attention(nc, banks, x, hT, ctxT, ident, dram)
        if STAGES >= 4:
            top2_ffn(nc, banks, x, hT, ident, iota, dram, out)
            return
        st = sem("stored")
        with nc.Block() as block:
            @block.sync
            def _(sp):
                sp.dma_start(out, x[:]).then_inc(st, 16)
                sp.wait_ge(st, 16)


def kernel(**inputs):
    import numpy as np
    import concourse.bacc as bacc
    from concourse import mybir as mb
    from concourse.bass_utils import run_bass_kernel_spmd

    a = {n: np.asarray(v) for n, v in inputs.items()}

    def rows(w):
        return w.reshape(-1, P, w.shape[-1]).transpose(1, 0, 2)

    def flat(w):
        return rows(w).reshape(P, -1)

    lay = {}
    lay["x"] = rows(a["x"].reshape(B * S, D))
    lay["token"] = a["itok_BxS_13_99985"].reshape(TILES, P).T
    lay["ctxT"] = rows(a["ctx_2048"].transpose(2, 0, 1).reshape(D, B * S)).reshape(P, KD, B, S)
    lay["ident"] = np.eye(P, dtype=np.float32)
    lay["iota"] = np.broadcast_to(np.arange(EB, dtype=np.float32), (P, EB))
    lay["router"] = np.concatenate([flat(a["L0_ffn_router_w"].T),
                                    np.broadcast_to(a["L0_ffn_router_bias"], (P, EB))], 1)
    gate = [a["L0_ffn_shared_gate_w"], *a["L0_ffn_expert_gate_w"]]
    up = [a["L0_ffn_shared_up_w"], *a["L0_ffn_expert_up_w"]]
    down = [a["L0_ffn_shared_down_w"], *a["L0_ffn_expert_down_w"]]
    lay["wb"] = np.stack([np.concatenate([flat(g.T), flat(u.T), flat(d.T)], 1)
                          for g, u, d in zip(gate, up, down)])
    wk = [a["L1_xattn_wk_ctx"], a["L1_xattn_wv_ctx"], a["L1_xattn_wk"], a["L1_xattn_wv"]]
    head = lambda w, g: w[:, g * HD:(g + 1) * HD]
    lay["wqkv"] = np.stack([np.concatenate([
        flat(a["L1_xattn_wq"][:, g * REP * HD:(g + 1) * REP * HD]),
        flat(np.concatenate([head(w, g) for w in wk[:2]], 1)),
        flat(np.concatenate([head(w, g) for w in wk[2:]], 1))], 1) for g in range(KV)])
    lay["wo"] = np.stack([flat(a["L1_xattn_wo"][g * REP * HD:(g + 1) * REP * HD]) for g in range(KV)])
    inv = (np.float32(1) / np.float32(10000) ** (np.arange(0, HD, 2, dtype=np.float32) / np.float32(HD)))
    angle = np.outer(np.arange(S, dtype=np.float32), inv.astype(np.float32))
    cos, sin = np.cos(angle), np.sin(angle)
    lay["cos"] = rows(np.concatenate([cos, cos], 1).astype(np.float32))
    lay["sin"] = rows(np.concatenate([-sin, sin], 1).astype(np.float32))
    lay["headnorm"] = np.stack([np.broadcast_to(a[f"L1_xattn_{n}_norm_w"], (P, HD)) for n in "qk"], 1)
    lay["above"] = np.triu(np.full((P, P), MASKED, np.float32), 1)
    lay["wd"] = np.stack([np.concatenate([flat(a["L1_ffn_w1"][e][:, c * P:(c + 1) * P]),
                                          a["L1_ffn_w2"][e][c * P:(c + 1) * P]], 1)
                          for e in range(ED) for c in range(CHUNKS)])
    lay["b1"] = a["L1_ffn_b1"].reshape(ED * CHUNKS, P).T
    lay["b2"] = a["L1_ffn_b2"]
    lay["gate"] = np.concatenate([flat(a["L1_ffn_gate_w"]), np.broadcast_to(a["L1_ffn_gate_b"], (P, ED))], 1)

    nc = bacc.Bacc("TRN2", target_bir_lowering=False, num_devices=1)
    arrays, dram = {}, {}
    for name, v in lay.items():
        arrays[f"in_{name}"] = v = np.ascontiguousarray(v)
        dram[name] = nc.dram_tensor(f"in_{name}", v.shape, mb.dt.from_np(v.dtype), kind="ExternalInput").ap()
    out = nc.dram_tensor("out_x", (P, TILES, D), mb.dt.float32, kind="ExternalOutput").ap()
    program(nc, dram, out)
    got = run_bass_kernel_spmd(nc, [arrays], core_ids=[0]).results[0]["out_x"]
    return np.ascontiguousarray(got.transpose(1, 0, 2)).reshape(B, S, D)
```

```python
from contextlib import ExitStack

import concourse.bass as bass
from concourse import mybir

F32 = mybir.dt.float32
F32R = mybir.dt.float32r
I32 = mybir.dt.int32
U32 = mybir.dt.uint32
ALU = mybir.AluOpType
ACT = mybir.ActivationFunctionType
AX_X = mybir.AxisListType.X

P = 128
B, S, D = 4, 256, 256
TILES = B * S // P
KD = D // P
HALF = 512
HT = HALF // P
EA = 4
VOCAB = 12500
PER_EXPERT = VOCAB // EA
EB, KB, FB = 16, 4, 128
WG = 2 * KD * FB
WB = WG + D
HEADS, KV, HD = 16, 4, 128
REP = HEADS // KV
KEYS = 2 * S
SCALE = HD ** -0.5
RMS_EPS = 1e-6
WQ = KD * REP * HD
WK = KD * 2 * HD
WO = REP * D
ED, KDTOP, FD = 8, 2, 1024
CHUNKS = FD // P
WD = KD * P + D
LN_EPS = 1e-5
MASKED = -float(2 ** 100)


class Count:

    def __init__(self, sem):
        self.sem, self.n, self.base = sem, 0, 0

    def tick(self, ins):
        ins.then_inc(self.sem, 1)
        self.n += 1

    def settle(self, eng):
        eng.wait_ge(self.sem, self.base + self.n)

    def turn(self, i, per):
        self.base, self.start, self.per = i * per, self.n, per

    def turned(self, turns):
        assert self.n - self.start == self.per, (self.n - self.start, self.per)
        self.n, self.base = self.start + turns * self.per, 0


def f32(ap):
    return ap.bitcast(F32)


def product(pe, out, left, right, first=True, last=True, shared=False):
    (lh, ll), (rh, rl) = left, right
    pe.matmul(out, ll, rh, start=first, stop=False, skip_group_check=shared)
    pe.matmul(out, lh, rl, start=False, stop=False, skip_group_check=shared)
    return pe.matmul(out, lh, rh, start=False, stop=last, skip_group_check=shared)


def both(pair, *index):
    return tuple(t[index] for t in pair)


class Norm:

    def __init__(self, sb, sem, tag, x, h, hT, banks, ident):
        self.x, self.h, self.hT, self.banks, self.ident = x, h, hT, banks, ident
        self.stats = sb(f"{tag}_stats", [P, TILES, 6], F32)
        self.moments = sb(f"{tag}_moments", [P, TILES, 2], F32)
        self.shifted = sb(f"{tag}_var_eps", [P, TILES], F32)
        self.power = sb(f"{tag}_minus_half", [P, TILES], F32)
        self.rstd = sb(f"{tag}_rstd", [P, TILES], F32)
        self.stats_done = sem(f"{tag}_stats_done")
        self.moments_done = sem(f"{tag}_moments_done")
        self.power_set = sem(f"{tag}_power_set")
        self.eps_added = sem(f"{tag}_eps_added")
        self.rstd_ready = sem(f"{tag}_rstd_ready")
        self.normed = sem(f"{tag}_normed")
        self.turned = sem(f"{tag}_h_transposed")
        self.hi_ready = sem(f"{tag}_hT_hi_ready")
        self.lo_ready = sem(f"{tag}_hT_lo_ready")

    def vector_moments(self, v, half):
        tiles = range(HT * half, HT * half + HT)
        for t in tiles:
            v.bn_stats(self.stats[:, t, :], self.x[:, t, :]).then_inc(self.stats_done, 1)
        for t in tiles:
            v.wait_ge(self.stats_done, t + 1)
            v.bn_aggr(self.moments[:, t, :], self.stats[:, t, :]).then_inc(self.moments_done, 1)

    def gpsimd(self, p, half):
        if half == 0:
            p.memset(self.power[:], -0.5).then_inc(self.power_set, 1)
            p.wait_ge(self.power_set, 1)
        a, b = HT * half, HT * half + HT
        p.wait_ge(self.moments_done, b)
        p.tensor_scalar(self.shifted[:, a:b], self.moments[:, a:b, 1], LN_EPS, None,
                        ALU.add).then_inc(self.eps_added, 1)
        p.wait_ge(self.eps_added, half + 1)
        p.tensor_tensor(self.rstd[:, a:b], self.shifted[:, a:b], self.power[:, a:b],
                        ALU.pow).then_inc(self.rstd_ready, 1)

    def vector_normalize(self, v, half):
        v.wait_ge(self.moments_done, HT * half + HT)
        v.wait_ge(self.rstd_ready, half + 1)
        for t in range(HT * half, HT * half + HT):
            v.tensor_scalar(self.h[:, t, :], self.x[:, t, :], self.moments[:, t, 0:1],
                            self.rstd[:, t:t + 1], ALU.subtract, ALU.mult).then_inc(self.normed, 1)

    def tensor(self, pe, half):
        for k in range(KD):
            for r in range(HT):
                t = HT * half + r
                pe.wait_ge(self.normed, t + 1)
                ins = pe.transpose(self.banks[KD * half + k][:, r * P:(r + 1) * P],
                                   self.h[:, t, k * P:(k + 1) * P], self.ident[:])
            ins.then_inc(self.turned, 1)

    def scalar_hi(self, act, half):
        for k in range(KD):
            u = KD * half + k
            act.wait_ge(self.turned, u + 1)
            act.activation(self.hT[0][:, k, half * HALF:(half + 1) * HALF], self.banks[u][:],
                           ACT.Copy).then_inc(self.hi_ready, 1)

    def vector_lo(self, v, half):
        for k in range(KD):
            u = KD * half + k
            v.wait_ge(self.hi_ready, u + 1)
            v.tensor_tensor(self.hT[1][:, k, half * HALF:(half + 1) * HALF], self.banks[u][:],
                            f32(self.hT[0][:, k, half * HALF:(half + 1) * HALF]),
                            ALU.subtract).then_inc(self.lo_ready, 1)

    def wait_half(self, eng, half):
        eng.wait_ge(self.hi_ready, KD * (half + 1))
        eng.wait_ge(self.lo_ready, KD * (half + 1))


def logits_transposed(pe, rows, hT, w, width, half):
    for k in range(KD):
        ins = product(pe, rows, both(w, slice(None), slice(k * width, k * width + width)),
                      both(hT, slice(None), k, slice(half * HALF, half * HALF + HALF)), k == 0, k == KD - 1)
    return ins


def choose(v, own, sb, tag, choice, weights, iota, k, experts, eps, comb):
    best = sb(f"{tag}_best", [P, TILES, 8], F32)
    index = sb(f"{tag}_index", [P, TILES, 8], U32)
    indexf = sb(f"{tag}_indexf", [P, TILES, 8], F32)
    hit = sb(f"{tag}_hit", [P, TILES, experts], F32)
    picked = sb(f"{tag}_picked", [P, TILES, experts], F32)
    total = sb(f"{tag}_total", [P, TILES], F32)
    for t in range(TILES):
        own.tick(v.max(best[:, t, :], choice[:, t, :]))
    own.settle(v)
    for t in range(TILES):
        own.tick(v.max_index(index[:, t, :], best[:, t, :], choice[:, t, :]))
    own.settle(v)
    own.tick(v.tensor_copy(indexf[:], index[:]))
    own.settle(v)
    shape = [P, TILES, experts]
    for j in range(k):
        into = picked if j == 0 else hit
        own.tick(v.tensor_tensor(into[:], iota[:, None, 0:experts].to_broadcast(shape),
                                 indexf[:, :, j:j + 1].to_broadcast(shape), ALU.is_equal))
        own.settle(v)
        if j:
            own.tick(v.tensor_tensor(picked[:], picked[:], hit[:], ALU.add))
            own.settle(v)
    own.tick(v.tensor_tensor(picked[:], picked[:], weights[:], ALU.mult))
    own.settle(v)
    own.tick(v.tensor_reduce(total[:], picked[:], AX_X, ALU.add))
    own.settle(v)
    if eps:
        own.tick(v.tensor_scalar(total[:], total[:], eps, None, ALU.add))
        own.settle(v)
    own.tick(v.reciprocal(total[:], total[:]))
    own.settle(v)
    return v.tensor_tensor(comb[:], picked[:], total[:, :, None].to_broadcast(shape), ALU.mult)


def token_expert_ffn(nc, banks, x, hT, ctxT, ident, dram, loads, norm, next_norm):
    with ExitStack() as ctx:
        sb = lambda n, s, d: ctx.enter_context(nc.sbuf_tensor(n, s, d))
        sem = lambda n: ctx.enter_context(nc.semaphore(n))
        raw = sb("ctxT_raw", [P, KD, EA, D], F32)
        token = sb("token", [P, TILES], I32)
        tokenf = sb("tokenf", [P, TILES], F32)
        atleast = sb("atleast", [P, EA, TILES], F32)
        mask = sb("mask", [P, EA, TILES], F32)
        z = sb("z", [P, 2, D], F32)
        silu = sb("silu", [P, 2, D], F32)
        gu = sb("gu", [P, 2, D], F32)
        guT = (sb("guT_hi", [P, 2, KD, P], F32R), sb("guT_lo", [P, 2, KD, P], F32R))

        x_loaded = [sem("x_loaded0"), sem("x_loaded1")]
        ctx_loaded = [sem(f"ctx_loaded{k}") for k in range(KD)]
        token_loaded = sem("token_loaded")
        ident_loaded = sem("ident_loaded")
        ctx_hi = sem("ctx_hi_ready")
        ctx_lo = sem("ctx_lo_ready")
        own = Count(sem("a_vector_own"))
        z_done = sem("z_done")
        z_chosen = sem("z_chosen")
        silu_ready = sem("silu_ready")
        gu_ready = sem("gu_ready")
        gu_turned = sem("gu_transposed")
        guT_hi = sem("guT_hi_ready")
        guT_lo = sem("guT_lo_ready")
        y_done = sem("y_done")
        y_added = sem("y_added")
        block = ctx.enter_context(nc.Block())

        @block.sync
        def _(sp):
            for half in range(2):
                sp.dma_start(x[:, HT * half:HT * half + HT, :],
                             dram["x"][:, HT * half:HT * half + HT, :]).then_inc(x_loaded[half], 16)
                if half == 0:
                    sp.dma_start(ident[:], dram["ident"]).then_inc(ident_loaded, 16)
                sp.dma_start(raw[:, half], dram["ctxT"][:, half]).then_inc(ctx_loaded[half], 16)
            sp.dma_start(token[:], dram["token"]).then_inc(token_loaded, 16)
            for into, source, landed in loads:
                sp.dma_start(into, source).then_inc(landed, 16)

        @block.gpsimd
        def _(p):
            norm.gpsimd(p, 0)
            norm.gpsimd(p, 1)
            next_norm.gpsimd(p, 0)

        @block.scalar
        def _(act):
            def split_ctx(k):
                act.wait_ge(ctx_loaded[k], 16)
                for n in range(2):
                    act.activation(ctxT[0][:, k, 2 * n:2 * n + 2, :], raw[:, k, 2 * n:2 * n + 2, :],
                                   ACT.Copy).then_inc(ctx_hi, 1)

            def silu_of(i):
                act.wait_ge(z_chosen, i + 1)
                if i >= 2:
                    act.wait_ge(gu_ready, i - 1)
                act.activation(silu[:, i % 2], z[:, i % 2], ACT.Silu).then_inc(silu_ready, 1)

            split_ctx(0)
            norm.scalar_hi(act, 0)
            split_ctx(1)
            norm.scalar_hi(act, 1)
            silu_of(0)
            for i in range(TILES):
                act.wait_ge(gu_turned, i + 1)
                if i >= 2:
                    act.wait_ge(y_done, i - 1)
                act.activation(guT[0][:, i % 2], banks[6 + i % 2][:, 0:D],
                               ACT.Copy).then_inc(guT_hi, 1)
                if i + 1 < TILES:
                    silu_of(i + 1)

        @block.tensor
        def _(pe):
            def z_of(i):
                norm.wait_half(pe, i // HT)
                if i >= 2:
                    pe.wait_ge(z_chosen, i - 1)
                for n in range(2):
                    for k in range(KD):
                        if i == 0:
                            pe.wait_ge(ctx_hi, 2 * k + n + 1)
                            pe.wait_ge(ctx_lo, 2 * k + n + 1)
                        ins = product(pe, banks[2 * (i % 2) + n][:],
                                      both(hT, slice(None), k, slice(i * P, i * P + P)),
                                      both(ctxT, slice(None), k, slice(2 * n, 2 * n + 2)),
                                      k == 0, k == KD - 1)
                ins.then_inc(z_done, 1)

            pe.wait_ge(ident_loaded, 16)
            norm.tensor(pe, 0)
            z_of(0)
            norm.tensor(pe, 1)
            for i in range(TILES):
                if i == 0:
                    norm.wait_half(pe, 1)
                pe.wait_ge(gu_ready, i + 1)
                if i >= 2:
                    pe.wait_ge(guT_lo, i - 1)
                for k in range(KD):
                    ins = pe.transpose(banks[6 + i % 2][:, k * P:(k + 1) * P],
                                       gu[:, i % 2, k * P:(k + 1) * P], ident[:])
                ins.then_inc(gu_turned, 1)
                if i + 1 < TILES:
                    z_of(i + 1)
                pe.wait_ge(guT_hi, i + 1)
                pe.wait_ge(guT_lo, i + 1)
                if i >= 1:
                    pe.wait_ge(y_added, EA * i)
                for n in range(2):
                    for k in range(KD):
                        ins = product(pe, banks[4 + n][:], both(guT, slice(None), i % 2, k),
                                      both(ctxT, slice(None), k, slice(2 * n, 2 * n + 2)),
                                      k == 0, k == KD - 1)
                ins.then_inc(y_done, 1)

        @block.vector
        def _(v):
            def choose_z(i):
                v.wait_ge(z_done, i + 1)
                if i >= 2:
                    v.wait_ge(gu_ready, i - 1)
                for e in range(EA):
                    ze = banks[2 * (i % 2) + e // 2][:, (e % 2) * D:(e % 2) * D + D]
                    m = mask[:, e, i:i + 1]
                    if e == 0:
                        ins = v.tensor_scalar(z[:, i % 2], ze, m, None, ALU.mult)
                    else:
                        own.settle(v)
                        ins = v.scalar_tensor_tensor(z[:, i % 2], ze, m, z[:, i % 2], ALU.mult, ALU.add)
                    if e < EA - 1:
                        own.tick(ins)
                ins.then_inc(z_chosen, 1)

            def gate_z(i):
                v.wait_ge(silu_ready, i + 1)
                v.wait_ge(z_chosen, i + 1)
                if i >= 2:
                    v.wait_ge(gu_turned, i - 1)
                v.tensor_tensor(gu[:, i % 2], silu[:, i % 2], z[:, i % 2], ALU.mult).then_inc(gu_ready, 1)

            v.wait_ge(x_loaded[0], 16)
            norm.vector_moments(v, 0)
            norm.vector_normalize(v, 0)
            for k in range(KD):
                for n in range(2):
                    v.wait_ge(ctx_hi, 2 * k + n + 1)
                    v.tensor_tensor(ctxT[1][:, k, 2 * n:2 * n + 2, :], raw[:, k, 2 * n:2 * n + 2, :],
                                    f32(ctxT[0][:, k, 2 * n:2 * n + 2, :]), ALU.subtract).then_inc(ctx_lo, 1)
                if k == 0:
                    norm.vector_lo(v, 0)
                    v.wait_ge(x_loaded[1], 16)
                    norm.vector_moments(v, 1)
            norm.vector_normalize(v, 1)
            v.wait_ge(token_loaded, 16)
            own.tick(v.tensor_copy(tokenf[:], token[:]))
            own.settle(v)
            for e in range(1, EA):
                own.tick(v.tensor_scalar(atleast[:, e, :], tokenf[:], float(e * PER_EXPERT), None, ALU.is_ge))
            own.settle(v)
            own.tick(v.tensor_scalar(mask[:, 0, :], atleast[:, 1, :], -1.0, 1.0, ALU.mult, ALU.add))
            for e in range(1, EA - 1):
                own.tick(v.tensor_tensor(mask[:, e, :], atleast[:, e, :], atleast[:, e + 1, :], ALU.subtract))
            own.tick(v.tensor_copy(mask[:, EA - 1, :], atleast[:, EA - 1, :]))
            own.settle(v)
            choose_z(0)
            norm.vector_lo(v, 1)
            gate_z(0)
            for i in range(TILES):
                v.wait_ge(guT_hi, i + 1)
                if i >= 2:
                    v.wait_ge(y_done, i - 1)
                v.tensor_tensor(guT[1][:, i % 2], banks[6 + i % 2][:, 0:D].rearrange("p (k n) -> p k n", k=KD),
                                f32(guT[0][:, i % 2]), ALU.subtract).then_inc(guT_lo, 1)
                if i + 1 < TILES:
                    choose_z(i + 1)
                    gate_z(i + 1)
                v.wait_ge(y_done, i + 1)
                for e in range(EA):
                    if e:
                        v.wait_ge(y_added, EA * i + e)
                    ye = banks[4 + e // 2][:, (e % 2) * D:(e % 2) * D + D]
                    v.scalar_tensor_tensor(x[:, i, :], ye, mask[:, e, i:i + 1], x[:, i, :],
                                           ALU.mult, ALU.add).then_inc(y_added, 1)
                if i == HT:
                    v.wait_ge(y_added, EA * HT)
                    next_norm.vector_moments(v, 0)
                if i == HT + 1:
                    next_norm.vector_normalize(v, 0)


def routed_ffn(nc, banks, x, hT, ident, iota, dram, raw, raw_loaded, router, router_loaded, norm,
               next_norm, attention_weights):
    with ExitStack() as ctx:
        sb = lambda n, s, d: ctx.enter_context(nc.sbuf_tensor(n, s, d))
        sem = lambda n: ctx.enter_context(nc.semaphore(n))
        w = (sb("b_w_hi", [P, 2, WB], F32R), sb("b_w_lo", [P, 2, WB], F32R))
        rw = (sb("router_hi", [P, KD * EB], F32R), sb("router_lo", [P, KD * EB], F32R))
        logitsT = sb("router_logitsT", [EB, 2, HALF], F32)
        scores = sb("scores", [P, TILES, EB], F32)
        choice = sb("choice", [P, TILES, EB], F32)
        comb = sb("b_comb", [P, TILES, EB], F32)
        mine = sb("b_comb_of_expert", [P, 2, TILES], F32)
        gate = sb("b_gate", [P, 2, HALF], F32)
        a = sb("b_a", [P, 2, HALF], F32)
        aT = (sb("b_aT_hi", [P, 2, HALF], F32R), sb("b_aT_lo", [P, 2, HALF], F32R))

        own = Count(sem("b_vector_own"))
        wg_hi, wg_lo = sem("b_wg_hi_ready"), sem("b_wg_lo_ready")
        wd_hi, wd_lo = sem("b_wd_hi_ready"), sem("b_wd_lo_ready")
        rw_ready = sem("router_w_ready")
        logitsT_done = sem("router_logitsT_done")
        logitsT_copied = sem("router_logitsT_copied")
        logits_done = sem("logits_done")
        scores_ready = sem("scores_ready")
        gu_done = sem("b_gate_up_done")
        gate_ready = sem("b_silu_ready")
        a_ready = sem("b_a_ready")
        a_hi = sem("b_aT_hi_ready")
        a_lo = sem("b_aT_lo_ready")
        down_done = sem("b_down_done")
        mine_ready = sem("b_mine_ready")
        added = sem("b_added")
        block = ctx.enter_context(nc.Block())
        PAIRS = EB // 2
        LAST = 2 * (EB + 1) - 1

        @block.sync
        def _(sp):
            def load(e, slot):
                sp.wait_ge(wg_lo, e - 1)
                sp.wait_ge(wd_lo, e - 1)
                sp.dma_start(raw[:, slot, :], dram["wb"][bass.ds(e, 1)].rearrange("a p n -> (a p) n"))\
                    .then_inc(raw_loaded[slot], 16)
            with sp.Fori(0, PAIRS - 1) as i:
                load(i * 2 + 2, 0)
                load(i * 2 + 3, 1)
            load(EB, 0)

        @block.gpsimd
        def _(p):
            def split_lo(e, slot):
                p.wait_ge(wg_hi, e + 1)
                p.tensor_tensor(w[1][:, slot, 0:WG], raw[:, slot, 0:WG], f32(w[0][:, slot, 0:WG]),
                                ALU.subtract).then_inc(wg_lo, 1)
                p.wait_ge(wd_hi, e + 1)
                p.tensor_tensor(w[1][:, slot, WG:], raw[:, slot, WG:], f32(w[0][:, slot, WG:]),
                                ALU.subtract).then_inc(wd_lo, 1)
            split_lo(0, 0)
            norm.gpsimd(p, 1)
            split_lo(1, 1)
            split_lo(2, 0)
            with p.Fori(1, PAIRS) as i:
                split_lo(i * 2 + 1, 1)
                split_lo(i * 2 + 2, 0)
            attention_weights.split(p)
            next_norm.gpsimd(p, 0)

        @block.scalar
        def _(act):
            def unit(u, slot, first=False):
                act.wait_ge(gu_done, u + 1)
                if not first:
                    act.wait_ge(a_ready, u - 1)
                act.activation(gate[:, slot], banks[2 * slot][:], ACT.Silu).then_inc(gate_ready, 1)
                act.wait_ge(a_ready, u + 1)
                if not first:
                    act.wait_ge(down_done, u - 1)
                act.activation(aT[0][:, slot], a[:, slot], ACT.Copy).then_inc(a_hi, 1)

            norm.scalar_hi(act, 0)
            norm.scalar_hi(act, 1)
            unit(0, 0, True)
            for half in range(2):
                act.wait_ge(logitsT_done, half + 1)
                act.activation(logitsT[:, half], banks[4 + half][0:EB, :], ACT.Copy).then_inc(logitsT_copied, 1)
            act.wait_ge(logits_done, 1)
            act.activation(scores[:], banks[6][:, 0:TILES * EB].rearrange("p (t e) -> p t e", e=EB),
                           ACT.Sigmoid).then_inc(scores_ready, 1)
            unit(1, 1, True)
            with act.Fori(0, PAIRS) as i:
                for c in range(4):
                    unit(i * 4 + 2 + c, c % 2)

        @block.tensor
        def _(pe):
            def gate_up(u, e, half, slot, first=False):
                if half == 0:
                    pe.wait_ge(wg_lo, e + 1)
                if first:
                    norm.wait_half(pe, half)
                else:
                    pe.wait_ge(a_ready, u - 1)
                for m in range(2):
                    for k in range(KD):
                        c = (m * KD + k) * FB
                        ins = product(pe, banks[2 * half + m][:], both(w, slice(None), slot, slice(c, c + FB)),
                                      both(hT, slice(None), k, slice(half * HALF, half * HALF + HALF)),
                                      k == 0, k == KD - 1)
                ins.then_inc(gu_done, 1)

            def down(u, e, half, slot, first=False):
                if half == 0:
                    pe.wait_ge(wd_lo, e + 1)
                pe.wait_ge(a_hi, u + 1)
                pe.wait_ge(a_lo, u + 1)
                if not first:
                    pe.wait_ge(added, u * HT - HT + 1)
                for r in range(HT):
                    ins = product(pe, banks[4 + 2 * half + r // 2][:, (r % 2) * D:(r % 2) * D + D],
                                  both(aT, slice(None), half, slice(r * P, r * P + P)),
                                  both(w, slice(None), slot, slice(WB - D, WB)))
                ins.then_inc(down_done, 1)

            norm.tensor(pe, 0)
            gate_up(0, 0, 0, 0, True)
            norm.tensor(pe, 1)
            pe.wait_ge(rw_ready, 2)
            for half in range(2):
                norm.wait_half(pe, half)
                logits_transposed(pe, banks[4 + half][0:EB, :], hT, rw, EB, half).then_inc(logitsT_done, 1)
            gate_up(1, 0, 1, 0, True)
            for t in range(TILES):
                pe.wait_ge(logitsT_copied, t // HT + 1)
                ins = pe.transpose(banks[6][:, t * EB:t * EB + EB],
                                   logitsT[:, t // HT, t % HT * P:t % HT * P + P], ident[0:EB, 0:EB])
            ins.then_inc(logits_done, 1)
            down(0, 0, 0, 0, True)
            pe.wait_ge(scores_ready, 1)
            with pe.Fori(0, PAIRS) as i:
                for c in range(4):
                    gate_up(i * 4 + (2 + c), i * 2 + (1 + c // 2), c % 2, (1 + c // 2) % 2)
                    down(i * 4 + (1 + c), i * 2 + (1 + c) // 2, (1 + c) % 2, (1 + c) // 2 % 2)
            down(LAST, EB, 1, 0)

        @block.vector
        def _(v):
            def split_gate_up(e, slot, landed, first=False):
                v.wait_ge(raw_loaded[slot], landed)
                if not first:
                    v.wait_ge(gu_done, e * 2 - 2)
                    v.wait_ge(wg_lo, e - 1)
                v.tensor_copy(w[0][:, slot, 0:WG], raw[:, slot, 0:WG]).then_inc(wg_hi, 1)

            def split_down(e, slot, first=False):
                if not first:
                    v.wait_ge(down_done, e * 2 - 2)
                    v.wait_ge(wd_lo, e - 1)
                v.tensor_copy(w[0][:, slot, WG:], raw[:, slot, WG:]).then_inc(wd_hi, 1)

            def gated(u, slot, first=False):
                v.wait_ge(gate_ready, u + 1)
                if not first:
                    v.wait_ge(a_hi, u - 1)
                    v.wait_ge(a_lo, u - 1)
                v.tensor_tensor(a[:, slot], gate[:, slot], banks[2 * slot + 1][:], ALU.mult).then_inc(a_ready, 1)
                v.wait_ge(a_hi, u + 1)
                if not first:
                    v.wait_ge(down_done, u - 1)
                v.tensor_tensor(aT[1][:, slot], a[:, slot], f32(aT[0][:, slot]), ALU.subtract).then_inc(a_lo, 1)

            def add(u, half, slot):
                v.wait_ge(down_done, u + 1)
                v.wait_ge(added, u * HT + 1)
                for r in range(HT):
                    t = HT * half + r
                    y = banks[4 + 2 * half + r // 2][:, (r % 2) * D:(r % 2) * D + D]
                    v.scalar_tensor_tensor(x[:, t, :], y, mine[:, slot, t:t + 1], x[:, t, :],
                                           ALU.mult, ALU.add).then_inc(added, 1)

            def pair(i, last=False):
                for c in range(4):
                    e = i * 2 + (1 + c // 2)
                    slot = (1 + c // 2) % 2
                    gated(i * 4 + (2 + c), c % 2)
                    add(i * 4 + (1 + c), (1 + c) % 2, (1 + c) // 2 % 2)
                    if c % 2 == 0:
                        own.tick(v.tensor_copy(mine[:, slot, :], comb[:, :, bass.ds(e - 1, 1)]
                                               .rearrange("p t a -> p (t a)")))
                        own.settle(v)
                        if not (last and c == 2):
                            split_down(e + 1, 1 - slot)
                    elif not last:
                        split_gate_up(e + 2, slot, i * 16 + (48 if c == 3 else 32))

            v.memset(mine[:, 0, :], 1.0).then_inc(added, 1)
            split_gate_up(0, 0, 16, True)
            norm.vector_moments(v, 1)
            norm.vector_lo(v, 0)
            split_down(0, 0, True)
            v.wait_ge(router_loaded, 32)
            v.tensor_copy(rw[0][:], router[:, 0:KD * EB]).then_inc(rw_ready, 1)
            v.wait_ge(rw_ready, 1)
            v.tensor_tensor(rw[1][:], router[:, 0:KD * EB], f32(rw[0][:]), ALU.subtract).then_inc(rw_ready, 1)
            norm.vector_normalize(v, 1)
            norm.vector_lo(v, 1)
            split_gate_up(1, 1, 16, True)
            split_down(1, 1, True)
            gated(0, 0, True)
            v.wait_ge(scores_ready, 1)
            own.tick(v.tensor_tensor(choice[:], scores[:],
                                     router[:, None, KD * EB:KD * EB + EB].to_broadcast([P, TILES, EB]), ALU.add))
            own.settle(v)
            gated(1, 1, True)
            split_gate_up(2, 0, 32)
            own.tick(choose(v, own, sb, "b", choice, scores, iota, KB, EB, 1e-20, comb))
            own.settle(v)
            add(0, 0, 0)
            with v.Fori(0, PAIRS - 1) as i:
                own.turn(i, 2)
                pair(i)
            own.turned(PAIRS - 1)
            pair(PAIRS - 1, last=True)
            v.wait_ge(added, LAST * HT + 1)
            next_norm.vector_moments(v, 0)
            add(LAST, 1, 0)
            next_norm.vector_normalize(v, 0)


def at_least(eng, sem, value):
    if not isinstance(value, int) or value > 0:
        eng.wait_ge(sem, value)


def turns(eng, n, body, own=None, per=0):
    body(0)
    with eng.Fori(1, n - 1) as i:
        if own:
            own.turn(i - 1, per)
        body(i)
    if own:
        own.turned(n - 2)
    body(n - 1)


class AttentionWeights:

    def __init__(self, sb, sem, dram):
        self.raw = sb("c_w_raw", [P, WQ + 2 * WK], F32)
        self.raw_o = sb("c_wo_raw", [P, WO], F32)
        self.w = (sb("c_w_hi", [P, WQ + 2 * WK], F32R), sb("c_w_lo", [P, WQ + 2 * WK], F32R))
        self.cos, self.sin = sb("cos", [P, 2, HD], F32), sb("sin", [P, 2, HD], F32)
        self.headnorm = sb("headnorm", [P, 2, HD], F32)
        self.above = sb("above", [P, P], F32)
        self.w_loaded, self.wo_loaded = sem("c_w_loaded"), sem("c_wo_loaded")
        self.tables_loaded = sem("c_tables_loaded")
        self.w_hi, self.w_lo = sem("c_w_hi"), sem("c_w_lo")
        self.loads = [(self.raw[:], dram["wqkv"][0], self.w_loaded),
                      (self.raw_o[:], dram["wo"][0], self.wo_loaded),
                      (self.cos[:], dram["cos"], self.tables_loaded),
                      (self.sin[:], dram["sin"], self.tables_loaded),
                      (self.headnorm[:], dram["headnorm"], self.tables_loaded),
                      (self.above[:], dram["above"], self.tables_loaded)]

    def split(self, p):
        p.wait_ge(self.w_loaded, 16)
        parts = [slice(part * WQ, part * WQ + WQ) for part in range(2)]
        for at in parts:
            p.tensor_copy(self.w[0][:, at], self.raw[:, at]).then_inc(self.w_hi, 1)
        for part, at in enumerate(parts):
            p.wait_ge(self.w_hi, part + 1)
            p.tensor_tensor(self.w[1][:, at], self.raw[:, at], f32(self.w[0][:, at]),
                            ALU.subtract).then_inc(self.w_lo, 1)


def attention(nc, banks, x, hT, ctxT, ident, dram, weights, norm, next_norm, next_loads):
    GROUPS = KV * B
    UNITS = 2 * REP

    def lies(g):
        return not isinstance(g, int) or 0 <= g < GROUPS

    def lies_behind(g):
        return isinstance(g, int) and g == GROUPS

    def ahead(work, g, b, n):
        g, b, n = (g + 1, b + 1, n - UNITS) if n >= UNITS else (g, b, n)
        if lies(g):
            work(g, b, n)

    with ExitStack() as ctx:
        sb = lambda n, s, d: ctx.enter_context(nc.sbuf_tensor(n, s, d))
        sem = lambda n: ctx.enter_context(nc.semaphore(n))
        pair = lambda n, s: (sb(n + "_hi", s, F32R), sb(n + "_lo", s, F32R))
        ALL = slice(None)
        raw, raw_o, w = weights.raw, weights.raw_o, weights.w
        wo = pair("c_wo", [P, WO])
        cos, sin, headnorm, above = weights.cos, weights.sin, weights.headnorm, weights.above
        cosw = [sb(f"cosw_{n}", [P, 2, HD], F32) for n in "qk"]
        sinw = [sb(f"sinw_{n}", [P, 2, HD], F32) for n in "qk"]
        aboveR = sb("above_r", [P, P], F32R)
        identR = sb("ident_r", [P, P], F32R)
        power = sb("c_minus_half", [P, 6], F32)
        NQ = REP * HD
        qs = sb("q_rows", [P, 2, NQ], F32)
        ks = sb("kv_rows", [P, 2, 4 * HD], F32)
        sq = sb("squares", [P, NQ + 2 * HD], F32)
        sums = sb("sums", [P, 6], F32)
        means = sb("means", [P, 6], F32)
        r = sb("r", [P, 4, 2, 6], F32)
        t1 = sb("rope_cos", [P, NQ + HD], F32)
        t2 = sb("rope_sin", [P, NQ + HD], F32)
        qk = sb("qk", [P, 2, NQ + 2 * HD], F32)
        qT = pair("qT", [P, 2, REP, S])
        kT = pair("kT", [P, 2, KEYS])
        V = pair("V", [P, 4, 2, 2, HD])
        negmax = sb("negmax", [P, 2], F32)
        bias = sb("exp_bias", [P, 2], F32)
        total = sb("exp_total", [P, 2], F32)
        rtotal = sb("exp_rtotal", [P, 2], F32)
        probs = sb("probs", [P, 2, KEYS], F32)
        PT = pair("PT", [P, 2, 4, 2, S])
        OT = pair("OT", [P, REP, S])

        def heads(eng, step, own=None, per=0):
            def head(kv):
                for b in range(B):
                    for n in range(UNITS):
                        step(kv * B + b, b, n, kv)
            turns(eng, KV, head, own, per)
            for n in range(UNITS + 3):
                step(GROUPS + n // UNITS, n // UNITS, n % UNITS, KV)

        names = """wo_hi wo_lo constants power_set projected q_copied copied squared sums_done means_done r_ready roped rope_added qk_ready
            qk_turned qkT_hi qkT_lo v_hi v_lo scores_ready negmax_done bias_ready exp_done rtotal_done
            probs_ready p_turned pT_hi pT_lo pv_done oT_hi oT_lo out_half_done out_done out_added"""
        s = {n: sem("c_" + n) for n in names.split()}
        s.update(w_loaded=weights.w_loaded, wo_loaded=weights.wo_loaded, w_hi=weights.w_hi, w_lo=weights.w_lo)
        own = Count(sem("c_vector_own"))
        block = ctx.enter_context(nc.Block())

        first_banks = {(0, 1): banks[2:4], (1, 0): banks[0:2], (1, 1): banks[6:8]}

        def keys_of(j):
            return S + (j + 1) * P

        def rope(eng, g, j):
            n = g * 2 + j
            eng.wait_ge(s["copied"], n + 1)
            at_least(eng, s["rope_added"], n)
            H2 = HD // 2
            heads = lambda ap: ap.rearrange("p (h d) -> p h d", d=HD)
            for src, at, table, m in ((qs[:, j], slice(0, NQ), 0, REP),
                                      (ks[:, j, 2 * HD:3 * HD], slice(NQ, NQ + HD), 1, 1)):
                a, o1, o2 = heads(src), heads(t1[:, at]), heads(t2[:, at])
                wide = lambda t: t[:, None, :].to_broadcast([P, m, t.shape[-1]])
                eng.tensor_tensor(o1, a, wide(cosw[table][:, j]), ALU.mult).then_inc(s["roped"], 1)
                eng.tensor_tensor(o2[:, :, 0:H2], a[:, :, H2:], wide(sinw[table][:, j, 0:H2]),
                                  ALU.mult).then_inc(s["roped"], 1)
                eng.tensor_tensor(o2[:, :, H2:], a[:, :, 0:H2], wide(sinw[table][:, j, H2:]),
                                  ALU.mult).then_inc(s["roped"], 1)

        @block.sync
        def _(sp):
            with sp.Fori(1, KV) as kv:
                one = lambda t: t[bass.ds(kv, 1)].rearrange("a p n -> (a p) n")
                sp.wait_ge(s["w_lo"], kv * 2)
                sp.dma_start(raw[:], one(dram["wqkv"])).then_inc(s["w_loaded"], 16)
                sp.wait_ge(s["wo_lo"], kv)
                sp.dma_start(raw_o[:], one(dram["wo"])).then_inc(s["wo_loaded"], 16)
            for into, source, landed in next_loads:
                sp.dma_start(into, source).then_inc(landed, 16)

        @block.gpsimd
        def _(p):
            norm.gpsimd(p, 1)
            p.memset(power[:], -0.5).then_inc(s["power_set"], 1)
            p.wait_ge(s["power_set"], 1)

            def squares(g, j):
                n = g * 2 + j
                p.wait_ge(s["copied"], n + 1)
                at_least(p, s["sums_done"], n)
                p.tensor_tensor(sq[:, 0:NQ], qs[:, j], qs[:, j], ALU.mult).then_inc(s["squared"], 1)
                kk = ks[:, j].rearrange("p (c n) -> p c n", c=2)[:, :, 0:HD]
                p.tensor_tensor(sq[:, NQ:].rearrange("p (c n) -> p c n", c=2), kk, kk,
                                ALU.mult).then_inc(s["squared"], 1)

            def inverse_root(g, b, j):
                p.wait_ge(s["means_done"], g * 2 + j + 1)
                at_least(p, s["exp_done"], (g - 3) * UNITS)
                p.tensor_tensor(r[:, b % 4, j, :], means[:], power[:], ALU.pow).then_inc(s["r_ready"], 1)

            for g, j in ((0, 0), (0, 1), (1, 0)):
                squares(g, j)
                inverse_root(g, g, j)
            p.wait_ge(s["constants"], 6)
            squares(1, 1)
            rope(p, 1, 1)
            inverse_root(1, 1, 1)

            def step(g, b, n, kv):
                if n in (3, 7) and lies(g + 2):
                    squares(g + 2, n // 4)
                    rope(p, g + 2, n // 4)
                    inverse_root(g + 2, b + 2, n // 4)
            heads(p, step)
            next_norm.gpsimd(p, 0)

        @block.scalar
        def _(act):
            def split_hi(kv, part):
                act.wait_ge(s["w_loaded"], kv * 16 + 16)
                at_least(act, s["projected"], kv * (2 * B))
                at = slice(part * WQ, part * WQ + WQ)
                act.activation(w[0][:, at], raw[:, at], ACT.Copy).then_inc(s["w_hi"], 1)

            def split_wo_hi(kv):
                act.wait_ge(s["wo_loaded"], kv * 16 + 16)
                at_least(act, s["out_done"], kv * B)
                act.activation(wo[0][:], raw_o[:], ACT.Copy).then_inc(s["wo_hi"], 1)

            def copy(g, j, two=banks[4:6]):
                n = g * 2 + j
                act.wait_ge(s["projected"], n + 1)
                at_least(act, s["roped"], (n - 1) * 6)
                at_least(act, s["qk_ready"], n - 1)
                at_least(act, s["v_lo"], n - 1)
                act.activation(qs[:, j], two[0][:], ACT.Copy).then_inc(s["q_copied"], 1)
                act.activation(ks[:, j], two[1][:], ACT.Copy).then_inc(s["copied"], 1)

            def v_hi(g, b, j):
                at_least(act, s["pv_done"], (g - 3) * 2)
                act.wait_ge(s["copied"], g * 2 + j + 1)
                vv = ks[:, j].rearrange("p (c n) -> p c n", c=2)[:, :, HD:2 * HD]
                act.activation(V[0][:, b % 4, :, j, :], vv, ACT.Copy).then_inc(s["v_hi"], 1)

            def qkT_hi(g, b, j):
                act.wait_ge(s["qk_turned"], g * 2 + j + 1)
                at_least(act, s["scores_ready"], (g - 1) * UNITS)
                act.activation(qT[0][:, b % 2, :, j * P:j * P + P],
                               banks[4][:].rearrange("p (h n) -> p h n", h=REP), ACT.Copy).then_inc(s["qkT_hi"], 1)
                act.activation(kT[0][:, b % 2, :].rearrange("p (c n) -> p c n", c=2)[:, :, j * P:j * P + P],
                               banks[5][:, 0:2 * P].rearrange("p (c n) -> p c n", c=2),
                               ACT.Copy).then_inc(s["qkT_hi"], 1)

            def oT_hi(g, half):
                act.wait_ge(s["pv_done"], g * 2 + half + 1)
                at_least(act, s["out_done"] if half else s["out_half_done"], g)
                act.activation(OT[0][:, 2 * half:2 * half + 2, :], banks[6][:].rearrange("p (h n) -> p h n", h=2),
                               ACT.Copy).then_inc(s["oT_hi"], 1)

            def exp(g, b, n):
                u, slot, keys = g * UNITS + n, n % 2, keys_of(n % 2)
                act.wait_ge(s["bias_ready"], u + 1)
                at_least(act, s["p_turned"], u - 1)
                at_least(act, s["probs_ready"], u - 1)
                act.activation(probs[:, slot, 0:keys], banks[slot][:, 0:keys], ACT.Exp,
                               bias=bias[:, slot:slot + 1], scale=r[:, b % 4, n % 2, n // 2:n // 2 + 1],
                               accum_out=total[:, slot:slot + 1]).then_inc(s["exp_done"], 1)

            def divide(g, b, n):
                u, slot, keys = g * UNITS + n, n % 2, keys_of(n % 2)
                act.wait_ge(s["rtotal_done"], u + 1)
                act.activation(probs[:, slot, 0:keys], probs[:, slot, 0:keys], ACT.Copy,
                               scale=rtotal[:, slot:slot + 1]).then_inc(s["probs_ready"], 1)

            def pT_hi(g, n):
                u, j, kt = g * UNITS + n, n % 2, keys_of(n % 2) // P
                act.wait_ge(s["p_turned"], u + 1)
                at_least(act, s["pv_done"], g * 2 + n // 4 - 1)
                act.activation(PT[0][:, n // 4, 0:kt, n // 2 % 2, j * P:j * P + P],
                               banks[2 + j][:, 0:kt * P].rearrange("p (k n) -> p k n", k=kt),
                               ACT.Copy).then_inc(s["pT_hi"], 1)

            norm.scalar_hi(act, 0)
            norm.scalar_hi(act, 1)
            act.wait_ge(weights.tables_loaded, 64)
            act.activation(aboveR[:], above[:], ACT.Copy).then_inc(s["constants"], 1)
            act.activation(identR[:], ident[:], ACT.Copy).then_inc(s["constants"], 1)
            copy(0, 0)
            copy(0, 1, first_banks[0, 1])
            v_hi(0, 0, 0)
            v_hi(0, 0, 1)
            copy(1, 0, first_banks[1, 0])
            qkT_hi(0, 0, 0)
            qkT_hi(0, 0, 1)
            copy(1, 1, first_banks[1, 1])
            exp(0, 0, 0)
            divide(0, 0, 0)

            def step(g, b, n, kv):
                ahead(exp, g, b, n + 1)
                if lies_behind(g) and n == 6:
                    next_norm.scalar_hi(act, 0)
                if n == 0:
                    if lies(g - 1):
                        oT_hi(g - 1, 0)
                    if b == 2 and lies(g + 2):
                        split_hi(kv + 1, 1)
                if n == 1:
                    if lies(g + 1):
                        qkT_hi(g + 1, b + 1, 0)
                        v_hi(g + 1, b + 1, 0)
                        v_hi(g + 1, b + 1, 1)
                    if b == 1 and lies(g):
                        split_wo_hi(kv)
                if n == 3 and lies(g + 2):
                    copy(g + 2, 0)
                if n == 4 and lies(g - 1):
                    oT_hi(g - 1, 1)
                if n == 5 and lies(g + 1):
                    qkT_hi(g + 1, b + 1, 1)
                if n == 7 and lies(g + 2):
                    copy(g + 2, 1)
                    if b == 1 and lies(g + 3):
                        split_hi(kv + 1, 0)
                if lies(g):
                    pT_hi(g, n)
                ahead(divide, g, b, n + 1)
            heads(act, step)

        @block.tensor
        def _(pe):
            def project(g, b, j, pieces=range(4), two=banks[4:6]):
                n, b = g * 2 + j, b % B
                own_rows = both(hT, ALL, slice(0, KD), slice((2 * b + j) * P, (2 * b + j) * P + P))
                ctx_rows = both(ctxT, ALL, slice(0, KD), b, slice(j * P, j * P + P))
                if 0 in pieces:
                    if not isinstance(n, int) or n >= 4:
                        pe.wait_ge(s["qkT_hi"], n * 2 - 2)
                        pe.wait_ge(s["qkT_lo"], n * 2 - 2)
                for piece in pieces:
                    if piece < KD:
                        c = piece * NQ
                        product(pe, two[0][:], both(own_rows, ALL, piece), both(w, ALL, slice(c, c + NQ)),
                                piece == 0, piece == KD - 1)
                        continue
                    rows, at, out = ((ctx_rows, WQ, two[1][:, 0:2 * HD]) if piece == 2 else
                                     (own_rows, WQ + WK, two[1][:, 2 * HD:]))
                    for k in range(KD):
                        c = at + k * 2 * HD
                        ins = product(pe, out, both(rows, ALL, k), both(w, ALL, slice(c, c + 2 * HD)),
                                      k == 0, k == KD - 1)
                if 3 in pieces:
                    ins.then_inc(s["projected"], 1)

            def wait_weights(kv):
                pe.wait_ge(s["w_hi"], kv * 2 + 2)
                pe.wait_ge(s["w_lo"], kv * 2 + 2)

            def turn_qk(g, j, copied):
                n = g * 2 + j
                pe.wait_ge(s["qk_ready"], n + 1)
                pe.wait_ge(s["copied"], copied)
                for h in range(REP):
                    pe.transpose(banks[4][:, h * P:h * P + P], qk[:, j, h * HD:h * HD + HD], ident[:])
                pe.transpose(banks[5][:, 0:P], qk[:, j, NQ + HD:], ident[:])
                pe.transpose(banks[5][:, P:2 * P], qk[:, j, NQ:NQ + HD], ident[:]).then_inc(s["qk_turned"], 1)

            def scores(g, b, n):
                u, j, h, keys = g * UNITS + n, n % 2, n // 2, keys_of(n % 2)
                if n == 0:
                    pe.wait_ge(s["qkT_hi"], g * 4 + 4)
                    pe.wait_ge(s["qkT_lo"], g * 4 + 4)
                at_least(pe, s["exp_done"], u - 1)
                out = banks[j]
                product(pe, out[:, 0:keys], both(qT, ALL, b % 2, h, slice(j * P, j * P + P)),
                        both(kT, ALL, b % 2, slice(0, keys)), True, False, shared=True)
                pe.matmul(out[:, keys - P:keys], identR[:], aboveR[:], start=False, stop=True,
                          skip_group_check=True).then_inc(s["scores_ready"], 1)

            def turn_p(g, n):
                u, j, kt = g * UNITS + n, n % 2, keys_of(n % 2) // P
                pe.wait_ge(s["probs_ready"], u + 1)
                at_least(pe, s["pT_hi"], u - 1)
                at_least(pe, s["pT_lo"], u - 1)
                for k in range(kt):
                    ins = pe.transpose(banks[2 + j][:, k * P:k * P + P], probs[:, j, k * P:k * P + P], ident[:])
                ins.then_inc(s["p_turned"], 1)

            def values(g, b, half, key_tiles):
                if 0 in key_tiles:
                    pe.wait_ge(s["pT_hi"], g * UNITS + 4 * half + 4)
                    pe.wait_ge(s["pT_lo"], g * UNITS + 4 * half + 4)
                    pe.wait_ge(s["v_lo"], g * 2 + 2)
                    at_least(pe, s["oT_hi"], g * 2 + half)
                    at_least(pe, s["oT_lo"], g * 2 + half)
                out = banks[6][:].rearrange("p (h n) -> p h n", h=2)
                for kt in key_tiles:
                    at = slice(P if kt == 3 else 0, S)
                    ins = product(pe, out[:, :, at], both(V, ALL, b % 4, kt // 2, kt % 2),
                                  both(PT, ALL, half, kt, ALL, at), kt == 0, kt == 3, shared=True)
                if 3 in key_tiles:
                    ins.then_inc(s["pv_done"], 1)

            def project_out(g, kv, j, half):
                if half == 0 and j == 0:
                    pe.wait_ge(s["oT_hi"], g * 2 + 1)
                    pe.wait_ge(s["oT_lo"], g * 2 + 1)
                    pe.wait_ge(s["wo_lo"], kv + 1)
                    at_least(pe, s["out_added"], g)
                if half == 1 and j == 0:
                    pe.wait_ge(s["oT_hi"], g * 2 + 2)
                    pe.wait_ge(s["oT_lo"], g * 2 + 2)
                for h in range(2 * half, 2 * half + 2):
                    ins = product(pe, banks[7][:, j * D:j * D + D], both(OT, ALL, h, slice(j * P, j * P + P)),
                                  both(wo, ALL, slice(h * D, h * D + D)), j == 0 and h == 0, h == REP - 1,
                                  shared=True)
                if j == 1:
                    ins.then_inc(s["out_done"] if half else s["out_half_done"], 1)

            norm.tensor(pe, 0)
            norm.tensor(pe, 1)
            norm.wait_half(pe, 0)
            wait_weights(0)
            project(0, 0, 0)
            project(0, 0, 1, two=first_banks[0, 1])
            project(1, 1, 0, two=first_banks[1, 0])
            turn_qk(0, 0, 1)
            norm.wait_half(pe, 1)
            project(1, 1, 1, (0, 1), first_banks[1, 1])
            pe.wait_ge(s["qkT_hi"], 2)
            pe.wait_ge(s["qkT_lo"], 2)
            turn_qk(0, 1, 3)
            project(1, 1, 1, (2, 3), first_banks[1, 1])
            pe.wait_ge(s["constants"], 6)
            pe.wait_ge(s["copied"], 3)
            scores(0, 0, 0)
            scores(0, 0, 1)

            def step(g, b, n, kv):
                before = kv if b else kv - 1
                ahead(scores, g, b, n + 2)
                if lies_behind(g) and n == 5:
                    next_norm.tensor(pe, 0)
                if n == 0:
                    if lies(g + 1):
                        turn_qk(g + 1, 0, g * 2 + 4)
                if n == 1 and lies(g - 2):
                    project_out(g - 2, None, 1, 1)
                if n in (1, 2, 3) and lies(g - 1):
                    values(g - 1, b - 1, 1, ((0, 1), (2,), (3,))[n - 1])
                if n == 2 and lies(g + 2):
                    if b == 2:
                        wait_weights(kv + 1)
                    project(g + 2, b + 2, 0, (0, 1))
                if n == 3 and lies(g - 1):
                    project_out(g - 1, before, 0, 0)
                if n == 4:
                    if lies(g + 1):
                        turn_qk(g + 1, 1, g * 2 + 5 if lies(g + 2) else g * 2 + 4)
                if n == 5 and lies(g - 1):
                    project_out(g - 1, before, 1, 0)
                if n in (5, 6, 7) and lies(g):
                    values(g, b, 0, ((0, 1), (2,), (3,))[n - 5])
                if n == 6 and lies(g + 2):
                    project(g + 2, b + 2, 1, (0, 1))
                if n == 7 and lies(g - 1):
                    project_out(g - 1, before, 0, 1)
                if lies(g):
                    turn_p(g, n)
                if lies(g + 2):
                    if n == 2:
                        project(g + 2, b + 2, 0, (2, 3))
                    if n == 6:
                        project(g + 2, b + 2, 1, (2, 3))
            heads(pe, step)

        @block.vector
        def _(v):
            def split_lo(kv, part):
                v.wait_ge(s["w_hi"], kv * 2 + part + 1)
                at_least(v, s["projected"], kv * (2 * B))
                at = slice(part * WQ, part * WQ + WQ)
                v.tensor_tensor(w[1][:, at], raw[:, at], f32(w[0][:, at]), ALU.subtract).then_inc(s["w_lo"], 1)

            def split_wo_lo(kv):
                v.wait_ge(s["wo_hi"], kv + 1)
                v.tensor_tensor(wo[1][:], raw_o[:], f32(wo[0][:]), ALU.subtract).then_inc(s["wo_lo"], 1)

            def v_lo(g, b, j):
                v.wait_ge(s["v_hi"], g * 2 + j + 1)
                vv = ks[:, j].rearrange("p (c n) -> p c n", c=2)[:, :, HD:2 * HD]
                v.tensor_tensor(V[1][:, b % 4, :, j, :], vv, f32(V[0][:, b % 4, :, j, :]),
                                ALU.subtract).then_inc(s["v_lo"], 1)

            def sum_squares(g, j):
                n = g * 2 + j
                v.wait_ge(s["squared"], n * 2 + 2)
                v.tensor_reduce(sums[:], sq[:].rearrange("p (h d) -> p h d", d=HD), AX_X,
                                ALU.add).then_inc(s["sums_done"], 1)
                v.wait_ge(s["sums_done"], n + 1)
                at_least(v, s["r_ready"], n)
                v.tensor_scalar(means[:], sums[:], 1.0 / HD, RMS_EPS, ALU.mult,
                                ALU.add).then_inc(s["means_done"], 1)

            def add_rope(g, b, j):
                n = g * 2 + j
                v.wait_ge(s["roped"], n * 6 + 6)
                v.wait_ge(s["r_ready"], n + 1)
                at_least(v, s["qk_turned"], n - 1)
                v.tensor_tensor(qk[:, j, 0:NQ + HD], t1[:], t2[:], ALU.add).then_inc(s["rope_added"], 1)
                own.tick(v.scalar_tensor_tensor(qk[:, j, NQ + HD:], ks[:, j, 0:HD], r[:, b % 4, j, 4:5],
                                                headnorm[:, 1, :], ALU.mult, ALU.mult))
                own.settle(v)
                v.wait_ge(s["rope_added"], n + 1)
                v.tensor_scalar(qk[:, j, NQ:NQ + HD], qk[:, j, NQ:NQ + HD], r[:, b % 4, j, 5:6], None,
                                ALU.mult).then_inc(s["qk_ready"], 1)

            def qkT_lo(g, b, j):
                v.wait_ge(s["qkT_hi"], g * 4 + 2 * j + 2)
                at = (ALL, b % 2, ALL, slice(j * P, j * P + P))
                v.tensor_tensor(qT[1][at], banks[4][:].rearrange("p (h n) -> p h n", h=REP), f32(qT[0][at]),
                                ALU.subtract).then_inc(s["qkT_lo"], 1)
                part = lambda t: t[:, b % 2, :].rearrange("p (c n) -> p c n", c=2)[:, :, j * P:j * P + P]
                v.tensor_tensor(part(kT[1]), banks[5][:, 0:2 * P].rearrange("p (c n) -> p c n", c=2),
                                f32(part(kT[0])), ALU.subtract).then_inc(s["qkT_lo"], 1)

            def oT_lo(g, half):
                v.wait_ge(s["oT_hi"], g * 2 + half + 1)
                v.tensor_tensor(OT[1][:, 2 * half:2 * half + 2, :], banks[6][:].rearrange("p (h n) -> p h n", h=2),
                                f32(OT[0][:, 2 * half:2 * half + 2, :]), ALU.subtract).then_inc(s["oT_lo"], 1)

            def row_max(g, b, n):
                u, slot, keys = g * UNITS + n, n % 2, keys_of(n % 2)
                if n == 0:
                    v.wait_ge(s["r_ready"], g * 2 + 2)
                v.wait_ge(s["scores_ready"], u + 1)
                at_least(v, s["bias_ready"], u - 1)
                v.tensor_reduce(negmax[:, slot:slot + 1], banks[slot][:, 0:keys], AX_X, ALU.max,
                                negate=True).then_inc(s["negmax_done"], 1)
                v.wait_ge(s["negmax_done"], u + 1)
                at_least(v, s["exp_done"], u - 1)
                v.tensor_tensor(bias[:, slot:slot + 1], negmax[:, slot:slot + 1],
                                r[:, b % 4, n % 2, n // 2:n // 2 + 1], ALU.mult).then_inc(s["bias_ready"], 1)

            def pT_lo(g, n):
                u, j, kt = g * UNITS + n, n % 2, keys_of(n % 2) // P
                v.wait_ge(s["pT_hi"], u + 1)
                at = (ALL, n // 4, slice(0, kt), n // 2 % 2, slice(j * P, j * P + P))
                v.tensor_tensor(PT[1][at], banks[2 + j][:, 0:kt * P].rearrange("p (k n) -> p k n", k=kt),
                                f32(PT[0][at]), ALU.subtract).then_inc(s["pT_lo"], 1)

            def row_sum(g, b, n):
                u, slot = g * UNITS + n, n % 2
                v.wait_ge(s["exp_done"], u + 1)
                at_least(v, s["probs_ready"], u - 1)
                v.reciprocal(rtotal[:, slot:slot + 1], total[:, slot:slot + 1]).then_inc(s["rtotal_done"], 1)

            def add_out(g, b):
                v.wait_ge(s["out_done"], g + 1)
                at_least(v, s["out_added"], g)
                at = slice(2 * (b % B), 2 * (b % B) + 2)
                v.tensor_tensor(x[:, at, :], banks[7][:].rearrange("p (j d) -> p j d", j=2), x[:, at, :],
                                ALU.add).then_inc(s["out_added"], 1)

            norm.vector_moments(v, 1)
            norm.vector_lo(v, 0)
            norm.vector_normalize(v, 1)
            norm.vector_lo(v, 1)
            v.wait_ge(weights.tables_loaded, 64)
            H2 = HD // 2
            for m, scale in ((0, SCALE), (1, 1.0)):
                wide = headnorm[:, m:m + 1, :].to_broadcast([P, 2, HD])
                own.tick(v.scalar_tensor_tensor(cosw[m][:], cos[:], scale, wide, ALU.mult, ALU.mult))
                own.tick(v.scalar_tensor_tensor(sinw[m][:, :, 0:H2], sin[:, :, 0:H2], scale, wide[:, :, H2:],
                                                ALU.mult, ALU.mult))
                own.settle(v)
                v.scalar_tensor_tensor(sinw[m][:, :, H2:], sin[:, :, H2:], scale, wide[:, :, 0:H2],
                                       ALU.mult, ALU.mult).then_inc(s["constants"], 2)
            v.wait_ge(s["constants"], 6)
            rope(v, 0, 0)
            sum_squares(0, 0)
            add_rope(0, 0, 0)
            rope(v, 0, 1)
            sum_squares(0, 1)
            v_lo(0, 0, 0)
            v_lo(0, 0, 1)
            add_rope(0, 0, 1)
            qkT_lo(0, 0, 0)
            rope(v, 1, 0)
            sum_squares(1, 0)
            qkT_lo(0, 0, 1)
            add_rope(1, 1, 0)
            row_max(0, 0, 0)
            row_max(0, 0, 1)
            row_sum(0, 0, 0)

            def step(g, b, n, kv):
                if n and lies(g):
                    pT_lo(g, n - 1)
                if n == 0 and lies(g - 1):
                    pT_lo(g - 1, UNITS - 1)
                ahead(row_max, g, b, n + 2)
                ahead(row_sum, g, b, n + 1)
                if lies_behind(g):
                    if n == 3:
                        v.wait_ge(s["out_added"], GROUPS - 2)
                        next_norm.vector_moments(v, 0)
                    if n == 5:
                        next_norm.vector_normalize(v, 0)
                    if n == 7:
                        next_norm.vector_lo(v, 0)
                if n == 0:
                    if lies(g - 1):
                        oT_lo(g - 1, 0)
                    if b == 2 and lies(g + 2):
                        split_lo(kv + 1, 1)
                if n == 1:
                    if lies(g + 1):
                        qkT_lo(g + 1, b + 1, 0)
                        sum_squares(g + 1, 1)
                    if b == 1 and lies(g):
                        split_wo_lo(kv)
                if n == 2:
                    if lies(g - 2):
                        add_out(g - 2, b - 2)
                    if lies(g + 1):
                        v_lo(g + 1, b + 1, 0)
                        v_lo(g + 1, b + 1, 1)
                if n == 6 and lies(g + 2):
                    add_rope(g + 2, b + 2, 0)
                if n == 3 and lies(g + 1):
                    add_rope(g + 1, b + 1, 1)
                if n == 4 and lies(g - 1):
                    oT_lo(g - 1, 1)
                if n == 5:
                    if lies(g + 1):
                        qkT_lo(g + 1, b + 1, 1)
                    if lies(g + 2):
                        sum_squares(g + 2, 0)
                if n == 7 and b == 1 and lies(g + 3):
                    split_lo(kv + 1, 0)
            heads(v, step, own, 2 * B)


class Top2Start:

    def __init__(self, sb, sem, dram):
        self.raw1 = sb("w1_raw", [P, 2, KD * P], F32)
        self.raw2 = sb("w2_raw", [P, 2, D], F32)
        self.b1 = sb("b1", [P, ED * CHUNKS], F32)
        self.b2raw = sb("b2_raw", [ED, D], F32)
        self.gate = sb("gate_w", [P, KD * ED + ED], F32)
        self.w1_loaded = [sem(f"d_w1_loaded{slot}") for slot in range(2)]
        self.w2_loaded = [sem(f"d_w2_loaded{slot}") for slot in range(2)]
        self.small_loaded = sem("d_small_loaded")
        self.loads = [(into[:], dram[name], self.small_loaded)
                      for into, name in ((self.gate, "gate"), (self.b1, "b1"), (self.b2raw, "b2"))]
        for q in range(2):
            self.loads += [(self.raw1[:, q], dram["wd"][q][:, 0:KD * P], self.w1_loaded[q]),
                           (self.raw2[:, q], dram["wd"][q][:, KD * P:], self.w2_loaded[q])]


def top2_ffn(nc, banks, x, hT, ident, iota, dram, out, start, norm):
    CH = ED * CHUNKS
    LAST = CH - 1
    with ExitStack() as ctx:
        sb = lambda n, s, d: ctx.enter_context(nc.sbuf_tensor(n, s, d))
        sem = lambda n: ctx.enter_context(nc.semaphore(n))
        pair = lambda n, s: (sb(n + "_hi", s, F32R), sb(n + "_lo", s, F32R))
        ALL = slice(None)
        raw1, raw2, b1, b2raw, gate = start.raw1, start.raw2, start.b1, start.b2raw, start.gate
        w1 = pair("w1", [P, 2, KD * P])
        w2 = pair("w2", [P, 2, D])
        b1e = sb("b1_of_expert", [P, CHUNKS], F32)
        b2 = pair("b2", [ED, D])
        gw = pair("gate_split", [P, KD * ED])
        logitsT = sb("gate_logitsT", [ED, 2, HALF], F32)
        logits = sb("logits", [P, TILES, ED], F32)
        top = sb("logits_max", [P, TILES], F32)
        exps = sb("gate_exps", [P, TILES, ED], F32)
        gsum = sb("gate_sum", [P, TILES], F32)
        gprobs = sb("gate_probs", [P, TILES, ED], F32)
        comb = sb("d_comb", [P, TILES, ED], F32)
        mine = sb("d_comb_of_expert", [P, TILES], F32)
        combT = pair("combT", [ED, 2, HALF])
        g = sb("d_gelu", [P, 2, HALF], F32)
        aT = pair("d_aT", [P, 2, B * S])

        names = """w1_hi w1_lo w2_hi w2_lo small_hi small_lo logitsT_done logitsT_copied logits_done
            logits_shifted exps_ready comb_ready combT_done combT_hi combT_lo bias_done bias_added
            b1_ready up_done gelu_ready aT_hi aT_lo down_done last_down added stored"""
        s = {n: sem("d_" + n) for n in names.split()}
        own = Count(sem("d_vector_own"))
        block = ctx.enter_context(nc.Block())

        def lies(q):
            return not isinstance(q, int) or q < CH

        def first(e):
            return isinstance(e, int) and e == 0

        @block.sync
        def _(sp):
            def load(q, slot):
                one = dram["wd"][bass.ds(q, 1)].rearrange("a p n -> (a p) n")
                sp.wait_ge(s["w1_lo"], q - 1)
                sp.dma_start(raw1[:, slot], one[:, 0:KD * P]).then_inc(start.w1_loaded[slot], 16)
                sp.wait_ge(s["w2_lo"], q - 1)
                sp.dma_start(raw2[:, slot], one[:, KD * P:]).then_inc(start.w2_loaded[slot], 16)
            with sp.Fori(1, CH // 2) as i:
                load(i * 2, 0)
                load(i * 2 + 1, 1)
            for t in range(0, TILES, 2):
                sp.wait_ge(s["added"], (ED - 1) * TILES + t + 2)
                sp.dma_start(out[:, t:t + 2, :], x[:, t:t + 2, :]).then_inc(s["stored"], 16)
            sp.wait_ge(s["stored"], 16 * (TILES // 2))

        @block.gpsimd
        def _(p):
            def lo1(q, slot):
                p.wait_ge(s["w1_hi"], q + 1)
                p.tensor_tensor(w1[1][:, slot], raw1[:, slot], f32(w1[0][:, slot]),
                                ALU.subtract).then_inc(s["w1_lo"], 1)

            def lo2(q, slot):
                p.wait_ge(s["w2_hi"], q + 1)
                p.tensor_tensor(w2[1][:, slot], raw2[:, slot], f32(w2[0][:, slot]),
                                ALU.subtract).then_inc(s["w2_lo"], 1)

            lo1(0, 0)
            norm.gpsimd(p, 1)
            lo1(1, 1)
            lo2(0, 0)

            def expert(e):
                for c in range(CHUNKS):
                    q = e * CHUNKS + c
                    if lies(q + 1):
                        lo2(q + 1, (c + 1) % 2)
                    if lies(q + 2):
                        lo1(q + 2, c % 2)
            turns(p, ED, expert)

        @block.scalar
        def _(act):
            norm.scalar_hi(act, 1)
            act.wait_ge(start.small_loaded, 48)

            def unit(q, c, half):
                act.wait_ge(s["up_done"], q * 2 + half + 1)
                at_least(act, s["aT_hi"], q * 2 + half - 1)
                at_least(act, s["aT_lo"], q * 2 + half - 1)
                act.activation(g[:, half], banks[2 * (c % 2) + half][:], ACT.Gelu_apprx_tanh,
                               bias=b1e[:, c:c + 1]).then_inc(s["gelu_ready"], 1)
                act.wait_ge(s["gelu_ready"], q * 2 + half + 1)
                at_least(act, s["down_done"], q - 1)
                act.activation(aT[0][:, c % 2, half * HALF:(half + 1) * HALF], g[:, half],
                               ACT.Copy).then_inc(s["aT_hi"], 1)

            def expert(e):
                at = slice(e * CHUNKS, e * CHUNKS + CHUNKS) if isinstance(e, int) else bass.ds(e * CHUNKS, CHUNKS)
                act.activation(b1e[:], b1[:, at], ACT.Copy).then_inc(s["b1_ready"], 1)
                act.wait_ge(s["b1_ready"], e + 1)
                for c in range(CHUNKS):
                    for half in range(2):
                        unit(e * CHUNKS + c, c, half)
                        if first(e) and c == 0 and half == 0:
                            for part in range(2):
                                act.wait_ge(s["logitsT_done"], part + 1)
                                act.activation(logitsT[:, part], banks[4 + part][0:ED, :],
                                               ACT.Copy).then_inc(s["logitsT_copied"], 1)
                    if first(e) and c == 0:
                        act.wait_ge(s["logits_shifted"], 1)
                        act.activation(exps[:], logits[:], ACT.Exp).then_inc(s["exps_ready"], 1)
                    if first(e) and c == 2:
                        act.wait_ge(s["combT_done"], 2)
                        for half in range(2):
                            act.activation(combT[0][:, half], banks[half][0:ED, :],
                                           ACT.Copy).then_inc(s["combT_hi"], 1)
            turns(act, ED, expert)

        @block.tensor
        def _(pe):
            def up(q, c, halves=range(2)):
                if 0 in halves:
                    pe.wait_ge(s["w1_lo"], q + 1)
                for half in halves:
                    at_least(pe, s["gelu_ready"], (q - 2) * 2 + half + 1)
                    for k in range(KD):
                        ins = product(pe, banks[2 * (c % 2) + half][:],
                                      both(w1, ALL, c % 2, slice(k * P, k * P + P)),
                                      both(hT, ALL, k, slice(half * HALF, half * HALF + HALF)), k == 0, k == KD - 1)
                    ins.then_inc(s["up_done"], 1)

            def down(e, q, c):
                pe.wait_ge(s["w2_lo"], q + 1)
                for t in range(TILES):
                    if t % HT == 0:
                        pe.wait_ge(s["aT_lo"], q * 2 + t // HT + 1)
                    if c == 0 and t % 2 == 0 and not first(e):
                        pe.wait_ge(s["added"], (e - 1) * TILES + t + 2)
                    ins = product(pe, banks[4 + t // 2][:, (t % 2) * D:(t % 2) * D + D],
                                  both(aT, ALL, c % 2, slice(t * P, t * P + P)), both(w2, ALL, c % 2),
                                  c == 0 and t % 2 == 0, c == CHUNKS - 1, shared=True)
                    if isinstance(q, int) and q == LAST and t % 2 == 1 and t < TILES - 1:
                        ins.then_inc(s["last_down"], 1)
                ins.then_inc(s["down_done"], 1)

            def combine_biases(pair, half):
                for i in range(HT):
                    ins = product(pe, banks[2 * pair + i // 2][:, (i % 2) * D:(i % 2) * D + D],
                                  both(combT, ALL, half, slice(i * P, i * P + P)), both(b2, ALL, ALL))
                ins.then_inc(s["bias_done"], 1)

            up(0, 0, (0,))
            norm.tensor(pe, 1)
            pe.wait_ge(s["small_lo"], 2)
            logits_transposed(pe, banks[4][0:ED, :], hT, gw, ED, 0).then_inc(s["logitsT_done"], 1)
            norm.wait_half(pe, 1)
            logits_transposed(pe, banks[5][0:ED, :], hT, gw, ED, 1).then_inc(s["logitsT_done"], 1)
            up(0, 0, (1,))
            for t in range(TILES):
                pe.wait_ge(s["logitsT_copied"], t // HT + 1)
                ins = pe.transpose(banks[6][:, t * ED:t * ED + ED],
                                   logitsT[:, t // HT, t % HT * P:t % HT * P + P], ident[0:ED, 0:ED])
            ins.then_inc(s["logits_done"], 1)

            def expert(e):
                for c in range(CHUNKS):
                    q = e * CHUNKS + c
                    if first(e) and c in (4, 5):
                        pe.wait_ge(s["bias_added"], 2 * c - 6)
                    if lies(q + 1):
                        up(q + 1, c + 1)
                    if first(e) and c == 0:
                        pe.wait_ge(s["logits_shifted"], 1)
                    if first(e) and c == 2:
                        pe.wait_ge(s["gelu_ready"], 6)
                        pe.wait_ge(s["comb_ready"], 1)
                        for half in range(2):
                            for i in range(HT):
                                ins = pe.transpose(banks[half][0:ED, i * P:i * P + P],
                                                   comb[:, HT * half + i, :], ident[:])
                            ins.then_inc(s["combT_done"], 1)
                    if first(e) and c == 3:
                        pe.wait_ge(s["gelu_ready"], 8)
                        combine_biases(1, 0)
                    if first(e) and c == 4:
                        pe.wait_ge(s["gelu_ready"], 10)
                        combine_biases(0, 1)
                    down(e, q, c)
                    if first(e) and c == 2:
                        pe.wait_ge(s["combT_hi"], 2)
                        pe.wait_ge(s["combT_lo"], 2)
            turns(pe, ED, expert)

        @block.vector
        def _(v):
            def hi1(q, slot):
                at_least(v, s["up_done"], q * 2 - 2)
                at_least(v, s["w1_lo"], q - 1)
                v.wait_ge(start.w1_loaded[slot], (q - slot) * 8 + 16)
                v.tensor_copy(w1[0][:, slot], raw1[:, slot]).then_inc(s["w1_hi"], 1)

            def hi2(q, slot):
                at_least(v, s["down_done"], q - 1)
                at_least(v, s["w2_lo"], q - 1)
                v.wait_ge(start.w2_loaded[slot], (q - slot) * 8 + 16)
                v.tensor_copy(w2[0][:, slot], raw2[:, slot]).then_inc(s["w2_hi"], 1)

            def lo(q, c, half):
                v.wait_ge(s["aT_hi"], q * 2 + half + 1)
                v.tensor_tensor(aT[1][:, c % 2, half * HALF:(half + 1) * HALF], g[:, half],
                                f32(aT[0][:, c % 2, half * HALF:(half + 1) * HALF]),
                                ALU.subtract).then_inc(s["aT_lo"], 1)

            def add(e):
                last = isinstance(e, int) and e == ED - 1
                if not last:
                    v.wait_ge(s["down_done"], (e + 1) * CHUNKS)
                if first(e):
                    v.wait_ge(s["bias_added"], 4)
                else:
                    v.wait_ge(s["added"], e * TILES)
                column = comb[:, :, e:e + 1] if isinstance(e, int) else comb[:, :, bass.ds(e, 1)]
                own.tick(v.tensor_copy(mine[:], column.rearrange("p t a -> p (t a)")))
                own.settle(v)
                for t in range(TILES):
                    if last and t % 2 == 0:
                        if t < TILES - 2:
                            v.wait_ge(s["last_down"], t // 2 + 1)
                        else:
                            v.wait_ge(s["down_done"], CH)
                    v.scalar_tensor_tensor(x[:, t, :], banks[4 + t // 2][:, (t % 2) * D:(t % 2) * D + D],
                                           mine[:, t:t + 1], x[:, t, :], ALU.mult, ALU.add).then_inc(s["added"], 1)

            def shift_logits():
                shape = [P, TILES, ED]
                v.wait_ge(s["logits_done"], 1)
                own.tick(v.tensor_tensor(logits[:], banks[6][:, 0:TILES * ED].rearrange("p (t e) -> p t e", e=ED),
                                         gate[:, None, KD * ED:].to_broadcast(shape), ALU.add))
                own.settle(v)
                own.tick(v.tensor_reduce(top[:], logits[:], AX_X, ALU.max))
                own.settle(v)
                v.tensor_tensor(logits[:], logits[:], top[:, :, None].to_broadcast(shape),
                                ALU.subtract).then_inc(s["logits_shifted"], 1)

            def choose_experts():
                v.wait_ge(s["exps_ready"], 1)
                own.tick(v.tensor_reduce(gsum[:], exps[:], AX_X, ALU.add))
                own.settle(v)
                own.tick(v.reciprocal(gsum[:], gsum[:]))
                own.settle(v)
                own.tick(v.tensor_tensor(gprobs[:], exps[:], gsum[:, :, None].to_broadcast([P, TILES, ED]),
                                         ALU.mult))
                own.settle(v)
                choose(v, own, sb, "d", gprobs, gprobs, iota, KDTOP, ED, 0.0, comb).then_inc(s["comb_ready"], 1)
                v.wait_ge(s["comb_ready"], 1)

            hi1(0, 0)
            norm.vector_moments(v, 1)
            v.wait_ge(start.small_loaded, 48)
            v.tensor_copy(gw[0][:], gate[:, 0:KD * ED]).then_inc(s["small_hi"], 1)
            v.tensor_copy(b2[0][:], b2raw[:]).then_inc(s["small_hi"], 1)
            hi1(1, 1)
            hi2(0, 0)
            v.wait_ge(s["small_hi"], 2)
            v.tensor_tensor(gw[1][:], gate[:, 0:KD * ED], f32(gw[0][:]), ALU.subtract).then_inc(s["small_lo"], 1)
            v.tensor_tensor(b2[1][:], b2raw[:], f32(b2[0][:]), ALU.subtract).then_inc(s["small_lo"], 1)
            norm.vector_normalize(v, 1)
            norm.vector_lo(v, 1)

            def expert(e):
                for c in range(CHUNKS):
                    q = e * CHUNKS + c
                    lo(q, c, 0)
                    if first(e) and c == 0:
                        shift_logits()
                    lo(q, c, 1)
                    if c == 0 and not first(e):
                        add(e - 1)
                    if first(e) and c == 2:
                        for half in range(2):
                            v.wait_ge(s["combT_hi"], half + 1)
                            v.tensor_tensor(combT[1][:, half], banks[half][0:ED, :],
                                            f32(combT[0][:, half]), ALU.subtract).then_inc(s["combT_lo"], 1)
                    if first(e) and c in (3, 4):
                        v.wait_ge(s["bias_done"], c - 2)
                        for i in range(2):
                            t = HT * (c - 3) + 2 * i
                            v.tensor_tensor(x[:, t:t + 2, :],
                                            banks[2 * (4 - c) + i][:].rearrange("p (t d) -> p t d", t=2),
                                            x[:, t:t + 2, :], ALU.add).then_inc(s["bias_added"], 1)
                    if lies(q + 1):
                        hi2(q + 1, (c + 1) % 2)
                    if lies(q + 2):
                        hi1(q + 2, c % 2)
                    if first(e) and c == 0:
                        choose_experts()
            turns(v, ED, expert, own, 1)
            add(ED - 1)


def program(nc, dram, out):
    with ExitStack() as ctx:
        sb = lambda n, s, d: ctx.enter_context(nc.sbuf_tensor(n, s, d))
        sem = lambda n: ctx.enter_context(nc.semaphore(n))
        banks = [ctx.enter_context(nc.psum_tensor(f"bank{i}", [P, HALF], F32)) for i in range(8)]
        x = sb("x", [P, TILES, D], F32)
        h = sb("h", [P, TILES, D], F32)
        hT = (sb("hT_hi", [P, KD, B * S], F32R), sb("hT_lo", [P, KD, B * S], F32R))
        ident = sb("ident", [P, P], F32)
        iota = sb("iota", [P, EB], F32)
        norms = [Norm(sb, sem, f"ln{i}", x, h, hT, banks[4:8], ident) for i in range(1, 5)]
        start = Top2Start(sb, sem, dram)
        with ExitStack() as early:
            sb = lambda n, s, d: early.enter_context(nc.sbuf_tensor(n, s, d))
            ctxT = (sb("ctxT_hi", [P, KD, B, S], F32R), sb("ctxT_lo", [P, KD, B, S], F32R))
            weights = AttentionWeights(sb, sem, dram)
            with ExitStack() as part:
                sb = lambda n, s, d: part.enter_context(nc.sbuf_tensor(n, s, d))
                router = sb("router", [P, KD * EB + EB], F32)
                router_loaded = sem("router_loaded")
                raw_b = sb("b_w_raw", [P, 2, WB], F32)
                raw_b_loaded = [sem("b_w_loaded0"), sem("b_w_loaded1")]
                loads = [(iota[:], dram["iota"], router_loaded), (router[:], dram["router"], router_loaded),
                         (raw_b[:, 0, :], dram["wb"][0], raw_b_loaded[0]),
                         (raw_b[:, 1, :], dram["wb"][1], raw_b_loaded[1]), *weights.loads]
                token_expert_ffn(nc, banks, x, hT, ctxT, ident, dram, loads, norms[0], norms[1])
                routed_ffn(nc, banks, x, hT, ident, iota, dram, raw_b, raw_b_loaded, router, router_loaded,
                           norms[1], norms[2], weights)
            attention(nc, banks, x, hT, ctxT, ident, dram, weights, norms[2], norms[3], start.loads)
        top2_ffn(nc, banks, x, hT, ident, iota, dram, out, start, norms[3])


def kernel(**inputs):
    import numpy as np
    import concourse.bacc as bacc
    from concourse import mybir as mb
    from concourse.bass_utils import run_bass_kernel_spmd

    a = {n: np.asarray(v) for n, v in inputs.items()}

    def rows(w):
        return w.reshape(-1, P, w.shape[-1]).transpose(1, 0, 2)

    def flat(w):
        return rows(w).reshape(P, -1)

    lay = {}
    lay["x"] = rows(a["x"].reshape(B * S, D))
    lay["token"] = a["itok_BxS_13_99985"].reshape(TILES, P).T
    lay["ctxT"] = rows(a["ctx_2048"].transpose(2, 0, 1).reshape(D, B * S)).reshape(P, KD, B, S)
    lay["ident"] = np.eye(P, dtype=np.float32)
    lay["iota"] = np.broadcast_to(np.arange(EB, dtype=np.float32), (P, EB))
    lay["router"] = np.concatenate([flat(a["L0_ffn_router_w"].T),
                                    np.broadcast_to(a["L0_ffn_router_bias"], (P, EB))], 1)
    gate = [a["L0_ffn_shared_gate_w"], *a["L0_ffn_expert_gate_w"]]
    up = [a["L0_ffn_shared_up_w"], *a["L0_ffn_expert_up_w"]]
    down = [a["L0_ffn_shared_down_w"], *a["L0_ffn_expert_down_w"]]
    lay["wb"] = np.stack([np.concatenate([flat(g.T), flat(u.T), flat(d.T)], 1)
                          for g, u, d in zip(gate, up, down)])
    wk = [a["L1_xattn_wk_ctx"], a["L1_xattn_wv_ctx"], a["L1_xattn_wk"], a["L1_xattn_wv"]]
    head = lambda w, g: w[:, g * HD:(g + 1) * HD]
    lay["wqkv"] = np.stack([np.concatenate([
        flat(a["L1_xattn_wq"][:, g * REP * HD:(g + 1) * REP * HD]),
        flat(np.concatenate([head(w, g) for w in wk[:2]], 1)),
        flat(np.concatenate([head(w, g) for w in wk[2:]], 1))], 1) for g in range(KV)])
    lay["wo"] = np.stack([flat(a["L1_xattn_wo"][g * REP * HD:(g + 1) * REP * HD]) for g in range(KV)])
    inv = (np.float32(1) / np.float32(10000) ** (np.arange(0, HD, 2, dtype=np.float32) / np.float32(HD)))
    angle = np.outer(np.arange(S, dtype=np.float32), inv.astype(np.float32))
    cos, sin = np.cos(angle), np.sin(angle)
    lay["cos"] = rows(np.concatenate([cos, cos], 1).astype(np.float32))
    lay["sin"] = rows(np.concatenate([-sin, sin], 1).astype(np.float32))
    lay["headnorm"] = np.stack([np.broadcast_to(a[f"L1_xattn_{n}_norm_w"], (P, HD)) for n in "qk"], 1)
    lay["above"] = np.triu(np.full((P, P), MASKED, np.float32), 1)
    lay["wd"] = np.stack([np.concatenate([flat(a["L1_ffn_w1"][e][:, c * P:(c + 1) * P]),
                                          a["L1_ffn_w2"][e][c * P:(c + 1) * P]], 1)
                          for e in range(ED) for c in range(CHUNKS)])
    lay["b1"] = a["L1_ffn_b1"].reshape(ED * CHUNKS, P).T
    lay["b2"] = a["L1_ffn_b2"]
    lay["gate"] = np.concatenate([flat(a["L1_ffn_gate_w"]), np.broadcast_to(a["L1_ffn_gate_b"], (P, ED))], 1)

    nc = bacc.Bacc("TRN2", target_bir_lowering=False, num_devices=1)
    arrays, dram = {}, {}
    for name, v in lay.items():
        arrays[f"in_{name}"] = v = np.ascontiguousarray(v)
        dram[name] = nc.dram_tensor(f"in_{name}", v.shape, mb.dt.from_np(v.dtype), kind="ExternalInput").ap()
    out = nc.dram_tensor("out_x", (P, TILES, D), mb.dt.float32, kind="ExternalOutput").ap()
    program(nc, dram, out)
    got = run_bass_kernel_spmd(nc, [arrays], core_ids=[0]).results[0]["out_x"]
    return np.ascontiguousarray(got.transpose(1, 0, 2)).reshape(B, S, D)
```

```python
from contextlib import ExitStack

import concourse.bass as bass
from concourse import mybir

F32 = mybir.dt.float32
F32R = mybir.dt.float32r
BF16 = mybir.dt.bfloat16
I32 = mybir.dt.int32
U32 = mybir.dt.uint32
ALU = mybir.AluOpType
ACT = mybir.ActivationFunctionType
AX_X = mybir.AxisListType.X

P = 128
B, S, D = 4, 256, 256
TILES = B * S // P
KD = D // P
HALF = 512
HT = HALF // P
EA = 4
VOCAB = 12500
PER_EXPERT = VOCAB // EA
EB, KB, FB = 16, 4, 128
WG = 2 * KD * FB
WB = WG + D
HEADS, KV, HD = 16, 4, 128
REP = HEADS // KV
KEYS = 2 * S
SCALE = HD ** -0.5
RMS_EPS = 1e-6
WQ = KD * REP * HD
WK = KD * 2 * HD
WO = REP * D
ED, KDTOP, FD = 8, 2, 1024
CHUNKS = FD // P
WD = KD * P + D
LN_EPS = 1e-5
MASKED = -float(2 ** 100)


class Count:

    def __init__(self, sem):
        self.sem, self.n, self.base = sem, 0, 0

    def tick(self, ins):
        ins.then_inc(self.sem, 1)
        self.n += 1

    def settle(self, eng):
        eng.wait_ge(self.sem, self.base + self.n)

    def turn(self, i, per):
        self.base, self.start, self.per = i * per, self.n, per

    def turned(self, turns):
        assert self.n - self.start == self.per, (self.n - self.start, self.per)
        self.n, self.base = self.start + turns * self.per, 0


def f32(ap):
    return ap.bitcast(F32)


def product(pe, out, left, right, first=True, last=True, shared=False):
    (lh, ll), (rh, rl) = left, right
    pe.matmul(out, ll, rh, start=first, stop=False, skip_group_check=shared)
    pe.matmul(out, lh, rl, start=False, stop=False, skip_group_check=shared)
    return pe.matmul(out, lh, rh, start=False, stop=last, skip_group_check=shared)


def both(pair, *index):
    return tuple(t[index] for t in pair)


class Norm:

    def __init__(self, sb, sem, tag, x, h, hT, banks, ident):
        self.x, self.h, self.hT, self.banks, self.ident = x, h, hT, banks, ident
        self.stats = sb(f"{tag}_stats", [P, TILES, 6], F32)
        self.moments = sb(f"{tag}_moments", [P, TILES, 2], F32)
        self.shifted = sb(f"{tag}_var_eps", [P, TILES], F32)
        self.power = sb(f"{tag}_minus_half", [P, TILES], F32)
        self.rstd = sb(f"{tag}_rstd", [P, TILES], F32)
        self.stats_done = sem(f"{tag}_stats_done")
        self.moments_done = sem(f"{tag}_moments_done")
        self.power_set = sem(f"{tag}_power_set")
        self.eps_added = sem(f"{tag}_eps_added")
        self.rstd_ready = sem(f"{tag}_rstd_ready")
        self.normed = sem(f"{tag}_normed")
        self.turned = sem(f"{tag}_h_transposed")
        self.hi_ready = sem(f"{tag}_hT_hi_ready")
        self.lo_ready = sem(f"{tag}_hT_lo_ready")

    def vector_moments(self, v, half):
        tiles = range(HT * half, HT * half + HT)
        for t in tiles:
            v.bn_stats(self.stats[:, t, :], self.x[:, t, :]).then_inc(self.stats_done, 1)
        for t in tiles:
            v.wait_ge(self.stats_done, t + 1)
            v.bn_aggr(self.moments[:, t, :], self.stats[:, t, :]).then_inc(self.moments_done, 1)

    def gpsimd(self, p, half):
        if half == 0:
            p.memset(self.power[:], -0.5).then_inc(self.power_set, 1)
            p.wait_ge(self.power_set, 1)
        a, b = HT * half, HT * half + HT
        p.wait_ge(self.moments_done, b)
        p.tensor_scalar(self.shifted[:, a:b], self.moments[:, a:b, 1], LN_EPS, None,
                        ALU.add).then_inc(self.eps_added, 1)
        p.wait_ge(self.eps_added, half + 1)
        p.tensor_tensor(self.rstd[:, a:b], self.shifted[:, a:b], self.power[:, a:b],
                        ALU.pow).then_inc(self.rstd_ready, 1)

    def vector_normalize(self, v, half):
        v.wait_ge(self.moments_done, HT * half + HT)
        v.wait_ge(self.rstd_ready, half + 1)
        if half:
            v.wait_ge(self.turned, KD)
        for t in range(HT * half, HT * half + HT):
            v.tensor_scalar(self.h[:, t % HT, :], self.x[:, t, :], self.moments[:, t, 0:1],
                            self.rstd[:, t:t + 1], ALU.subtract, ALU.mult).then_inc(self.normed, 1)

    def tensor(self, pe, half):
        for k in range(KD):
            for r in range(HT):
                t = HT * half + r
                pe.wait_ge(self.normed, t + 1)
                ins = pe.transpose(self.banks[KD * half + k][:, r * P:(r + 1) * P],
                                   self.h[:, r, k * P:(k + 1) * P], self.ident[:])
            ins.then_inc(self.turned, 1)

    def scalar_hi(self, act, half):
        for k in range(KD):
            u = KD * half + k
            act.wait_ge(self.turned, u + 1)
            act.activation(self.hT[0][:, k, half * HALF:(half + 1) * HALF], self.banks[u][:],
                           ACT.Copy).then_inc(self.hi_ready, 1)

    def vector_lo(self, v, half):
        for k in range(KD):
            u = KD * half + k
            v.wait_ge(self.hi_ready, u + 1)
            v.tensor_tensor(self.hT[1][:, k, half * HALF:(half + 1) * HALF], self.banks[u][:],
                            f32(self.hT[0][:, k, half * HALF:(half + 1) * HALF]),
                            ALU.subtract).then_inc(self.lo_ready, 1)

    def wait_half(self, eng, half):
        eng.wait_ge(self.hi_ready, KD * (half + 1))
        eng.wait_ge(self.lo_ready, KD * (half + 1))


def logits_transposed(pe, rows, hT, w, width, half):
    for k in range(KD):
        ins = product(pe, rows, both(w, slice(None), slice(k * width, k * width + width)),
                      both(hT, slice(None), k, slice(half * HALF, half * HALF + HALF)), k == 0, k == KD - 1)
    return ins


def split(eng, hi, lo, raw, hi_ready, lo_ready, before=0):
    eng.tensor_copy(hi, raw).then_inc(hi_ready, 1)
    eng.wait_ge(hi_ready, before + 1)
    eng.tensor_tensor(lo, raw, f32(hi), ALU.subtract).then_inc(lo_ready, 1)


class Choice:

    def __init__(self, sb, own, tag, k, experts, eps, iota, comb):
        self.own, self.k, self.experts, self.eps, self.iota, self.comb = own, k, experts, eps, iota, comb
        self.best_of = sb(f"{tag}_best", [P, TILES, 8], F32)
        self.index = sb(f"{tag}_index", [P, TILES, 8], U32)
        self.indexf = sb(f"{tag}_indexf", [P, TILES, 8], F32)
        self.hit = sb(f"{tag}_hit", [P, TILES, k, experts], F32)
        self.picked = sb(f"{tag}_picked", [P, TILES, experts], F32)
        self.total = sb(f"{tag}_total", [P, TILES], F32)

    def indices(self, v, choice):
        own = self.own
        for t in range(TILES):
            own.tick(v.max(self.best_of[:, t, :], choice[:, t, :]))
        own.settle(v)
        for t in range(TILES):
            own.tick(v.max_index(self.index[:, t, :], self.best_of[:, t, :], choice[:, t, :]))
        own.settle(v)
        own.tick(v.tensor_copy(self.indexf[:], self.index[:]))
        own.settle(v)

    def combine(self, v, weights):
        own, hit, picked, total = self.own, self.hit, self.picked, self.total
        shape = [P, TILES, self.experts]
        each = [P, TILES, self.k, self.experts]
        own.tick(v.tensor_tensor(hit[:], self.iota[:, None, None, 0:self.experts].to_broadcast(each),
                                 self.indexf[:, :, 0:self.k, None].to_broadcast(each), ALU.is_equal))
        own.settle(v)
        own.tick(v.tensor_reduce(picked[:], hit[:].rearrange("p t k e -> p t e k"), AX_X, ALU.add))
        own.settle(v)
        own.tick(v.tensor_tensor(picked[:], picked[:], weights[:], ALU.mult))
        own.settle(v)
        own.tick(v.tensor_reduce(total[:], picked[:], AX_X, ALU.add))
        own.settle(v)
        if self.eps:
            own.tick(v.tensor_scalar(total[:], total[:], self.eps, None, ALU.add))
            own.settle(v)
        own.tick(v.reciprocal(total[:], total[:]))
        own.settle(v)
        return v.tensor_tensor(self.comb[:], picked[:], total[:, :, None].to_broadcast(shape), ALU.mult)


def token_expert_ffn(nc, banks, x, hT, ctxT, ident, dram, loads, norm, next_norm,
                     routed_start):
    with ExitStack() as ctx:
        sb = lambda n, s, d: ctx.enter_context(nc.sbuf_tensor(n, s, d))
        sem = lambda n: ctx.enter_context(nc.semaphore(n))
        raw = sb("ctxT_raw", [P, KD, EA, D], F32)
        token = sb("token", [P, TILES], I32)
        tokenf = sb("tokenf", [P, TILES], F32)
        atleast = sb("atleast", [P, EA, TILES], F32)
        mask = sb("mask", [P, EA, TILES], F32)
        z = sb("z", [P, 2, D], F32)
        silu = sb("silu", [P, 2, D], F32)
        gu = sb("gu", [P, 2, D], F32)
        guT = (sb("guT_hi", [P, 2, KD, P], F32R), sb("guT_lo", [P, 2, KD, P], F32R))

        x_loaded = [sem("x_loaded0"), sem("x_loaded1")]
        ctx_loaded = [sem(f"ctx_loaded{k}") for k in range(KD)]
        token_loaded = sem("token_loaded")
        ident_loaded = sem("ident_loaded")
        ctx_hi = sem("ctx_hi_ready")
        ctx_lo = sem("ctx_lo_ready")
        own = Count(sem("a_vector_own"))
        z_done = sem("z_done")
        z_chosen = sem("z_chosen")
        silu_ready = sem("silu_ready")
        gu_ready = sem("gu_ready")
        gu_turned = sem("gu_transposed")
        guT_hi = sem("guT_hi_ready")
        guT_lo = sem("guT_lo_ready")
        y_done = sem("y_done")
        y_added = sem("y_added")
        block = ctx.enter_context(nc.Block())
        LAST = TILES - 1

        def y_banks(i):
            return banks[2:4] if i == LAST else banks[4:6]

        @block.sync
        def _(sp):
            def load_x(half):
                sp.dma_start(x[:, HT * half:HT * half + HT, :],
                             dram["x"][:, HT * half:HT * half + HT, :]).then_inc(x_loaded[half], 16)
            load_x(0)
            sp.dma_start(ident[:], dram["ident"]).then_inc(ident_loaded, 16)
            sp.dma_start(token[:], dram["token"]).then_inc(token_loaded, 16)
            load_x(1)
            for into, source, landed in loads:
                sp.dma_start(into, source).then_inc(landed, 16)

        @block.gpsimd
        def _(p):
            norm.gpsimd(p, 0)
            norm.gpsimd(p, 1)
            routed_start.split(p)
            next_norm.gpsimd(p, 0)

        @block.scalar
        def _(act):
            def split_ctx(k):
                act.wait_ge(ctx_loaded[k], 16)
                for n in range(2):
                    act.activation(ctxT[0][:, k, 2 * n:2 * n + 2, :], raw[:, k, 2 * n:2 * n + 2, :],
                                   ACT.Copy).then_inc(ctx_hi, 1)

            def silu_of(i):
                act.wait_ge(z_chosen, i + 1)
                if i >= 2:
                    act.wait_ge(gu_ready, i - 1)
                act.activation(silu[:, i % 2], z[:, i % 2], ACT.Silu).then_inc(silu_ready, 1)

            for k in range(KD):
                act.dma_start(raw[:, k], dram["ctxT"][:, k]).then_inc(ctx_loaded[k], 16)
            split_ctx(0)
            norm.scalar_hi(act, 0)
            split_ctx(1)
            silu_of(0)
            for i in range(TILES):
                act.wait_ge(gu_turned, i + 1)
                if i >= 2:
                    act.wait_ge(y_done, i - 1)
                act.activation(guT[0][:, i % 2], banks[6 + i % 2][:, 0:D],
                               ACT.Copy).then_inc(guT_hi, 1)
                if i == 0:
                    norm.scalar_hi(act, 1)
                    silu_of(1)
                if i + 2 < TILES:
                    silu_of(i + 2)
            next_norm.scalar_hi(act, 0)

        @block.tensor
        def _(pe):
            def z_of(i):
                norm.wait_half(pe, i // HT)
                if i >= 2:
                    pe.wait_ge(z_chosen, i - 1)
                for n in range(2):
                    for k in range(KD):
                        if i == 0:
                            pe.wait_ge(ctx_hi, 2 * k + n + 1)
                            pe.wait_ge(ctx_lo, 2 * k + n + 1)
                        ins = product(pe, banks[2 * (i % 2) + n][:],
                                      both(hT, slice(None), k, slice(i * P, i * P + P)),
                                      both(ctxT, slice(None), k, slice(2 * n, 2 * n + 2)),
                                      k == 0, k == KD - 1)
                ins.then_inc(z_done, 1)

            pe.wait_ge(ident_loaded, 16)
            norm.tensor(pe, 0)
            def turn_gu(i):
                pe.wait_ge(gu_ready, i + 1)
                if i >= 2:
                    pe.wait_ge(guT_lo, i - 1)
                for k in range(KD):
                    ins = pe.transpose(banks[6 + i % 2][:, k * P:(k + 1) * P],
                                       gu[:, i % 2, k * P:(k + 1) * P], ident[:])
                ins.then_inc(gu_turned, 1)

            z_of(0)
            z_of(1)
            for i in range(TILES):
                if i < LAST:
                    turn_gu(i)
                if i == LAST - 1:
                    turn_gu(LAST)
                if i == 0:
                    norm.tensor(pe, 1)
                if i + 2 < TILES:
                    z_of(i + 2)
                pe.wait_ge(guT_hi, i + 1)
                pe.wait_ge(guT_lo, i + 1)
                if 1 <= i < LAST:
                    pe.wait_ge(y_added, EA * i)
                if i == 0:
                    norm.wait_half(pe, 1)
                for n in range(2):
                    for k in range(KD):
                        ins = product(pe, y_banks(i)[n][:], both(guT, slice(None), i % 2, k),
                                      both(ctxT, slice(None), k, slice(2 * n, 2 * n + 2)),
                                      k == 0, k == KD - 1)
                ins.then_inc(y_done, 1)
            next_norm.tensor(pe, 0)

        @block.vector
        def _(v):
            def choose_z(i):
                v.wait_ge(z_done, i + 1)
                if i >= 2:
                    v.wait_ge(gu_ready, i - 1)
                for e in range(EA):
                    ze = banks[2 * (i % 2) + e // 2][:, (e % 2) * D:(e % 2) * D + D]
                    m = mask[:, e, i:i + 1]
                    if e == 0:
                        ins = v.tensor_scalar(z[:, i % 2], ze, m, None, ALU.mult)
                    else:
                        own.settle(v)
                        ins = v.scalar_tensor_tensor(z[:, i % 2], ze, m, z[:, i % 2], ALU.mult, ALU.add)
                    if e < EA - 1:
                        own.tick(ins)
                ins.then_inc(z_chosen, 1)

            def gate_z(i):
                v.wait_ge(silu_ready, i + 1)
                v.wait_ge(z_chosen, i + 1)
                if i >= 2:
                    v.wait_ge(gu_turned, i - 1)
                v.tensor_tensor(gu[:, i % 2], silu[:, i % 2], z[:, i % 2], ALU.mult).then_inc(gu_ready, 1)

            def add_y(i, experts):
                v.wait_ge(y_done, i + 1)
                for e in experts:
                    if e:
                        v.wait_ge(y_added, EA * i + e)
                    ye = y_banks(i)[e // 2][:, (e % 2) * D:(e % 2) * D + D]
                    v.scalar_tensor_tensor(x[:, i, :], ye, mask[:, e, i:i + 1], x[:, i, :],
                                           ALU.mult, ALU.add).then_inc(y_added, 1)

            def token_masks():
                v.wait_ge(token_loaded, 16)
                own.tick(v.tensor_copy(tokenf[:], token[:]))
                own.settle(v)
                for e in range(1, EA):
                    own.tick(v.tensor_scalar(atleast[:, e, :], tokenf[:], float(e * PER_EXPERT), None, ALU.is_ge))
                own.settle(v)
                own.tick(v.tensor_scalar(mask[:, 0, :], atleast[:, 1, :], -1.0, 1.0, ALU.mult, ALU.add))
                for e in range(1, EA - 1):
                    own.tick(v.tensor_tensor(mask[:, e, :], atleast[:, e, :], atleast[:, e + 1, :], ALU.subtract))
                own.tick(v.tensor_copy(mask[:, EA - 1, :], atleast[:, EA - 1, :]))

            v.wait_ge(x_loaded[0], 16)
            norm.vector_moments(v, 0)
            norm.vector_normalize(v, 0)
            for k in range(KD):
                for n in range(2):
                    v.wait_ge(ctx_hi, 2 * k + n + 1)
                    v.tensor_tensor(ctxT[1][:, k, 2 * n:2 * n + 2, :], raw[:, k, 2 * n:2 * n + 2, :],
                                    f32(ctxT[0][:, k, 2 * n:2 * n + 2, :]), ALU.subtract).then_inc(ctx_lo, 1)
                if k == 0:
                    norm.vector_lo(v, 0)
                    token_masks()
            v.wait_ge(x_loaded[1], 16)
            norm.vector_moments(v, 1)
            norm.vector_normalize(v, 1)
            own.settle(v)
            choose_z(0)
            gate_z(0)
            choose_z(1)
            for i in range(TILES):
                if 1 <= i < LAST:
                    add_y(i - 1, (0, 1))
                v.wait_ge(guT_hi, i + 1)
                if i >= 2:
                    v.wait_ge(y_done, i - 1)
                v.tensor_tensor(guT[1][:, i % 2], banks[6 + i % 2][:, 0:D].rearrange("p (k n) -> p k n", k=KD),
                                f32(guT[0][:, i % 2]), ALU.subtract).then_inc(guT_lo, 1)
                if 1 <= i < LAST:
                    add_y(i - 1, (2, 3))
                if i == 0:
                    norm.vector_lo(v, 1)
                if i + 1 < LAST:
                    gate_z(i + 1)
                if i + 2 < TILES:
                    choose_z(i + 2)
                if i + 2 == LAST:
                    gate_z(LAST)
            next_norm.vector_moments(v, 0)
            add_y(LAST - 1, range(EA))
            next_norm.vector_normalize(v, 0)
            add_y(LAST, range(EA))
            next_norm.vector_lo(v, 0)


class RoutedStart:

    def __init__(self, sb, sem, dram, iota):
        self.raw = sb("b_w_raw", [P, 2, WB], F32)
        self.w = (sb("b_w_hi", [P, 2, WB], F32R), sb("b_w_lo", [P, 2, WB], F32R))
        self.router = sb("router", [P, KD * EB + EB], F32)
        self.rw = (sb("router_hi", [P, KD * EB], F32R), sb("router_lo", [P, KD * EB], F32R))
        self.loaded = [sem("b_w_loaded0"), sem("b_w_loaded1")]
        self.router_loaded = sem("router_loaded")
        self.router_hi, self.router_lo = sem("router_hi_ready"), sem("router_lo_ready")
        self.wg_hi, self.wg_lo = sem("b_wg_hi_ready"), sem("b_wg_lo_ready")
        self.wd_hi, self.wd_lo = sem("b_wd_hi_ready"), sem("b_wd_lo_ready")
        self.loads = [(iota[:], dram["iota"], self.router_loaded),
                      (self.router[:], dram["router"], self.router_loaded),
                      (self.raw[:, 0, :], dram["wb"][0], self.loaded[0]),
                      (self.raw[:, 1, :], dram["wb"][1], self.loaded[1])]

    def split(self, p):
        for e in range(2):
            p.wait_ge(self.loaded[e], 16)
            split(p, self.w[0][:, e, 0:WG], self.w[1][:, e, 0:WG], self.raw[:, e, 0:WG],
                  self.wg_hi, self.wg_lo, e)
            split(p, self.w[0][:, e, WG:], self.w[1][:, e, WG:], self.raw[:, e, WG:],
                  self.wd_hi, self.wd_lo, e)
        p.wait_ge(self.router_loaded, 32)
        split(p, self.rw[0][:], self.rw[1][:], self.router[:, 0:KD * EB], self.router_hi, self.router_lo)


def routed_ffn(nc, banks, x, hT, ident, iota, dram, start, norm, next_norm, attention_weights):
    with ExitStack() as ctx:
        sb = lambda n, s, d: ctx.enter_context(nc.sbuf_tensor(n, s, d))
        sem = lambda n: ctx.enter_context(nc.semaphore(n))
        raw, w, router, rw = start.raw, start.w, start.router, start.rw
        raw_loaded = start.loaded
        wg_hi, wg_lo, wd_hi, wd_lo = start.wg_hi, start.wg_lo, start.wd_hi, start.wd_lo
        logitsT = sb("router_logitsT", [EB, 2, HALF], F32)
        scores = sb("scores", [P, TILES, EB], F32)
        choice = sb("choice", [P, TILES, EB], F32)
        comb = sb("b_comb", [P, TILES, EB], F32)
        mine = sb("b_comb_of_expert", [P, 2, TILES], F32)
        gate = sb("b_gate", [P, 2, HALF], F32)
        a = sb("b_a", [P, 2, HALF], F32)
        aT = (sb("b_aT_hi", [P, 2, HALF], F32R), sb("b_aT_lo", [P, 2, HALF], F32R))

        own = Count(sem("b_vector_own"))
        picks = Choice(sb, own, "b", KB, EB, 1e-20, iota, comb)
        logitsT_done = sem("router_logitsT_done")
        logitsT_copied = sem("router_logitsT_copied")
        logits_done = sem("logits_done")
        scores_ready = sem("scores_ready")
        gu_done = sem("b_gate_up_done")
        gate_ready = sem("b_silu_ready")
        a_ready = sem("b_a_ready")
        a_hi = sem("b_aT_hi_ready")
        a_lo = sem("b_aT_lo_ready")
        down_done = sem("b_down_done")
        mine_ready = sem("b_mine_ready")
        added = sem("b_added")
        block = ctx.enter_context(nc.Block())
        PAIRS = EB // 2
        LAST = 2 * (EB + 1) - 1

        @block.sync
        def _(sp):
            def load(e, slot):
                sp.wait_ge(wg_lo, e - 1)
                sp.wait_ge(wd_lo, e - 1)
                sp.dma_start(raw[:, slot, :], dram["wb"][bass.ds(e, 1)].rearrange("a p n -> (a p) n"))\
                    .then_inc(raw_loaded[slot], 16)
            with sp.Fori(0, PAIRS - 1) as i:
                load(i * 2 + 2, 0)
                load(i * 2 + 3, 1)
            load(EB, 0)

        @block.gpsimd
        def _(p):
            def split_lo(e, slot):
                p.wait_ge(wg_hi, e + 1)
                p.tensor_tensor(w[1][:, slot, 0:WG], raw[:, slot, 0:WG], f32(w[0][:, slot, 0:WG]),
                                ALU.subtract).then_inc(wg_lo, 1)
                p.wait_ge(wd_hi, e + 1)
                p.tensor_tensor(w[1][:, slot, WG:], raw[:, slot, WG:], f32(w[0][:, slot, WG:]),
                                ALU.subtract).then_inc(wd_lo, 1)
            norm.gpsimd(p, 1)
            split_lo(2, 0)
            with p.Fori(1, PAIRS) as i:
                split_lo(i * 2 + 1, 1)
                split_lo(i * 2 + 2, 0)
            attention_weights.split_lo(p)
            next_norm.gpsimd(p, 0)

        @block.scalar
        def _(act):
            def unit(u, slot, first=False):
                act.wait_ge(gu_done, u + 1)
                if not first:
                    act.wait_ge(a_ready, u - 1)
                act.activation(gate[:, slot], banks[2 * slot][:], ACT.Silu).then_inc(gate_ready, 1)
                act.wait_ge(a_ready, u + 1)
                if not first:
                    act.wait_ge(down_done, u - 1)
                act.activation(aT[0][:, slot], a[:, slot], ACT.Copy).then_inc(a_hi, 1)

            norm.scalar_hi(act, 1)
            unit(0, 0, True)
            for half in range(2):
                act.wait_ge(logitsT_done, half + 1)
                act.activation(logitsT[:, half], banks[4 + half][0:EB, :], ACT.Copy).then_inc(logitsT_copied, 1)
            act.wait_ge(logits_done, 1)
            act.activation(scores[:], banks[6][:, 0:TILES * EB].rearrange("p (t e) -> p t e", e=EB),
                           ACT.Sigmoid).then_inc(scores_ready, 1)
            unit(1, 1, True)
            attention_weights.split_hi(act, ident)
            with act.Fori(0, PAIRS) as i:
                for c in range(4):
                    unit(i * 4 + 2 + c, c % 2)
            next_norm.scalar_hi(act, 0)

        @block.tensor
        def _(pe):
            def gate_up(u, e, half, slot, first=False):
                if half == 0:
                    pe.wait_ge(wg_lo, e + 1)
                if first:
                    norm.wait_half(pe, half)
                else:
                    pe.wait_ge(a_ready, u - 1)
                for m in range(2):
                    for k in range(KD):
                        c = (m * KD + k) * FB
                        ins = product(pe, banks[2 * half + m][:], both(w, slice(None), slot, slice(c, c + FB)),
                                      both(hT, slice(None), k, slice(half * HALF, half * HALF + HALF)),
                                      k == 0, k == KD - 1)
                ins.then_inc(gu_done, 1)

            def down(u, e, half, slot, first=False):
                if half == 0:
                    pe.wait_ge(wd_lo, e + 1)
                pe.wait_ge(a_hi, u + 1)
                pe.wait_ge(a_lo, u + 1)
                if not first:
                    pe.wait_ge(added, u * HT - HT + 1)
                for r in range(HT):
                    ins = product(pe, banks[4 + 2 * half + r // 2][:, (r % 2) * D:(r % 2) * D + D],
                                  both(aT, slice(None), half, slice(r * P, r * P + P)),
                                  both(w, slice(None), slot, slice(WB - D, WB)))
                ins.then_inc(down_done, 1)

            gate_up(0, 0, 0, 0, True)
            norm.tensor(pe, 1)
            pe.wait_ge(start.router_lo, 1)
            for half in range(2):
                norm.wait_half(pe, half)
                logits_transposed(pe, banks[4 + half][0:EB, :], hT, rw, EB, half).then_inc(logitsT_done, 1)
            gate_up(1, 0, 1, 0, True)
            for t in range(TILES):
                pe.wait_ge(logitsT_copied, t // HT + 1)
                ins = pe.transpose(banks[6][:, t * EB:t * EB + EB],
                                   logitsT[:, t // HT, t % HT * P:t % HT * P + P], ident[0:EB, 0:EB])
            ins.then_inc(logits_done, 1)
            gate_up(2, 1, 0, 1)
            down(0, 0, 0, 0, True)
            pe.wait_ge(scores_ready, 1)

            def pair(i, last=False):
                for c in range(4):
                    if not (last and c == 3):
                        gate_up(i * 4 + (3 + c), i * 2 + (3 + c) // 2, (3 + c) % 2, (3 + c) // 2 % 2)
                    down(i * 4 + (1 + c), i * 2 + (1 + c) // 2, (1 + c) % 2, (1 + c) // 2 % 2)
            with pe.Fori(0, PAIRS - 1) as i:
                pair(i)
            pair(PAIRS - 1, last=True)
            down(LAST, EB, 1, 0)
            next_norm.tensor(pe, 0)

        @block.vector
        def _(v):
            def split_gate_up(e, slot, landed):
                v.wait_ge(raw_loaded[slot], landed)
                v.wait_ge(gu_done, e * 2 - 2)
                v.wait_ge(wg_lo, e - 1)
                v.tensor_copy(w[0][:, slot, 0:WG], raw[:, slot, 0:WG]).then_inc(wg_hi, 1)

            def split_down(e, slot):
                v.wait_ge(down_done, e * 2 - 2)
                v.wait_ge(wd_lo, e - 1)
                v.tensor_copy(w[0][:, slot, WG:], raw[:, slot, WG:]).then_inc(wd_hi, 1)

            def gated(u, slot, first=False):
                v.wait_ge(gate_ready, u + 1)
                if not first:
                    v.wait_ge(a_hi, u - 1)
                    v.wait_ge(a_lo, u - 1)
                v.tensor_tensor(a[:, slot], gate[:, slot], banks[2 * slot + 1][:], ALU.mult).then_inc(a_ready, 1)

            def lo(u, slot, first=False):
                v.wait_ge(a_hi, u + 1)
                if not first:
                    v.wait_ge(down_done, u - 1)
                v.tensor_tensor(aT[1][:, slot], a[:, slot], f32(aT[0][:, slot]), ALU.subtract).then_inc(a_lo, 1)

            def add(u, half, slot):
                v.wait_ge(down_done, u + 1)
                v.wait_ge(added, u * HT + 1)
                for r in range(HT):
                    t = HT * half + r
                    y = banks[4 + 2 * half + r // 2][:, (r % 2) * D:(r % 2) * D + D]
                    v.scalar_tensor_tensor(x[:, t, :], y, mine[:, slot, t:t + 1], x[:, t, :],
                                           ALU.mult, ALU.add).then_inc(added, 1)

            def pair(i, last=False):
                for c in range(4):
                    e = i * 2 + (1 + c // 2)
                    slot = (1 + c // 2) % 2
                    if not (last and c == 3):
                        gated(i * 4 + (3 + c), (3 + c) % 2)
                    if c == 1 and isinstance(i, int) and i == 0:
                        own.tick(picks.combine(v, scores))
                        own.settle(v)
                    if c % 2 == 1:
                        own.tick(v.tensor_copy(mine[:, slot, :], comb[:, :, bass.ds(e - 1, 1)]
                                               .rearrange("p t a -> p (t a)")))
                        own.settle(v)
                    add(i * 4 + (1 + c), (1 + c) % 2, (1 + c) // 2 % 2)
                    if not (last and c == 3):
                        lo(i * 4 + (3 + c), (3 + c) % 2)
                    if c % 2 == 0:
                        if not (last and c == 2):
                            split_down(e + 1, 1 - slot)
                        if not last:
                            split_gate_up(e + 2, slot, i * 16 + (48 if c == 2 else 32))

            v.memset(mine[:, 0, :], 1.0).then_inc(added, 1)
            norm.vector_moments(v, 1)
            norm.vector_normalize(v, 1)
            norm.vector_lo(v, 1)
            gated(0, 0, True)
            lo(0, 0, True)
            v.wait_ge(scores_ready, 1)
            own.tick(v.tensor_tensor(choice[:], scores[:],
                                     router[:, None, KD * EB:KD * EB + EB].to_broadcast([P, TILES, EB]), ALU.add))
            own.settle(v)
            gated(1, 1, True)
            lo(1, 1, True)
            split_gate_up(2, 0, 32)
            gated(2, 0)
            lo(2, 0)
            add(0, 0, 0)
            picks.indices(v, choice)
            pair(0)
            with v.Fori(1, PAIRS - 1) as i:
                own.turn(i - 1, 2)
                pair(i)
            own.turned(PAIRS - 2)
            pair(PAIRS - 1, last=True)
            v.wait_ge(added, LAST * HT + 1)
            next_norm.vector_moments(v, 0)
            add(LAST, 1, 0)
            next_norm.vector_normalize(v, 0)
            next_norm.vector_lo(v, 0)


def at_least(eng, sem, value):
    if not isinstance(value, int) or value > 0:
        eng.wait_ge(sem, value)


def turns(eng, n, body, own=None, per=0):
    body(0)
    with eng.Fori(1, n - 1) as i:
        if own:
            own.turn(i - 1, per)
        body(i)
    if own:
        own.turned(n - 2)
    body(n - 1)


class AttentionWeights:

    def __init__(self, sb, sb_till_split, sem, dram):
        self.raw = sb("c_w_raw", [P, WQ + 2 * WK], F32)
        self.raw_o = sb("c_wo_raw", [P, WO], F32)
        self.w = (sb("c_w_hi", [P, WQ + 2 * WK], F32R), sb("c_w_lo", [P, WQ + 2 * WK], F32R))
        self.cos, self.sin = sb("cos", [P, 2, HD], F32), sb("sin", [P, 2, HD], F32)
        self.headnorm = sb("headnorm", [P, 2, HD], F32)
        self.above16 = sb("above_bf16", [P, P], BF16)
        self.ident16 = sb("ident_bf16", [P, P], BF16)
        self.above = sb_till_split("above", [P, P], F32)
        self.w_loaded, self.wo_loaded = sem("c_w_loaded"), sem("c_wo_loaded")
        self.tables_loaded = sem("c_tables_loaded")
        self.w_hi, self.w_lo = sem("c_w_hi"), sem("c_w_lo")
        self.constants_ready = sem("c_constants_ready")
        self.parts = [slice(part * WQ, part * WQ + WQ) for part in range(2)]
        self.loads = [(self.raw[:], dram["wqkv"][0], self.w_loaded),
                      (self.raw_o[:], dram["wo"][0], self.wo_loaded),
                      (self.cos[:], dram["cos"], self.tables_loaded),
                      (self.sin[:], dram["sin"], self.tables_loaded),
                      (self.headnorm[:], dram["headnorm"], self.tables_loaded),
                      (self.above[:], dram["above"], self.tables_loaded)]

    def split_hi(self, act, ident):
        act.wait_ge(self.tables_loaded, 64)
        act.activation(self.above16[:], self.above[:], ACT.Copy).then_inc(self.constants_ready, 1)
        act.activation(self.ident16[:], ident[:], ACT.Copy).then_inc(self.constants_ready, 1)
        act.wait_ge(self.w_loaded, 16)
        for at in self.parts:
            act.activation(self.w[0][:, at], self.raw[:, at], ACT.Copy).then_inc(self.w_hi, 1)

    def split_lo(self, p):
        for part, at in enumerate(self.parts):
            p.wait_ge(self.w_hi, part + 1)
            p.tensor_tensor(self.w[1][:, at], self.raw[:, at], f32(self.w[0][:, at]),
                            ALU.subtract).then_inc(self.w_lo, 1)


def attention(nc, banks, x, hT, ctxT, ident, dram, weights, norm, next_norm, next_start):
    GROUPS = KV * B
    UNITS = 2 * REP

    def lies(g):
        return not isinstance(g, int) or 0 <= g < GROUPS

    def is_step(g, n, at):
        return isinstance(g, int) and (g - GROUPS + 1) * UNITS + n == at

    def ahead(work, g, b, n):
        g, b, n = (g + 1, b + 1, n - UNITS) if n >= UNITS else (g, b, n)
        if lies(g):
            work(g, b, n)

    with ExitStack() as ctx:
        sb = lambda n, s, d: ctx.enter_context(nc.sbuf_tensor(n, s, d))
        sem = lambda n: ctx.enter_context(nc.semaphore(n))
        pair = lambda n, s: (sb(n + "_hi", s, F32R), sb(n + "_lo", s, F32R))
        ALL = slice(None)
        raw, raw_o, w = weights.raw, weights.raw_o, weights.w
        wo = pair("c_wo", [P, WO])
        cos, sin, headnorm = weights.cos, weights.sin, weights.headnorm
        above16, ident16 = weights.above16, weights.ident16
        cosw = [sb(f"cosw_{n}", [P, 2, HD], F32) for n in "qk"]
        sinw = [sb(f"sinw_{n}", [P, 2, HD], F32) for n in "qk"]
        power = sb("c_minus_half", [P, 6], F32)
        NQ = REP * HD
        qs = sb("q_rows", [P, 2, NQ], F32)
        ks = sb("kv_rows", [P, 2, 4 * HD], F32)
        sq = sb("squares", [P, NQ + 2 * HD], F32)
        sums = sb("sums", [P, 6], F32)
        means = sb("means", [P, 6], F32)
        r = sb("r", [P, 4, 2, 6], F32)
        t1 = sb("rope_cos", [P, NQ + HD], F32)
        t2 = sb("rope_sin", [P, NQ + HD], F32)
        qk = sb("qk", [P, 2, NQ + 2 * HD], F32)
        qT = pair("qT", [P, 2, REP, S])
        kT = pair("kT", [P, 2, KEYS])
        V = pair("V", [P, 4, 2, 2, HD])
        negmax = sb("negmax", [P, 2], F32)
        bias = sb("exp_bias", [P, 2], F32)
        total = sb("exp_total", [P, 2], F32)
        rtotal = sb("exp_rtotal", [P, 2], F32)
        probs = sb("probs", [P, 2, KEYS], F32)
        PT = pair("PT", [P, 2, 4, 2, S])
        OT = pair("OT", [P, REP, S])

        def heads(eng, step, own=None, per=0):
            def head(kv):
                for b in range(B):
                    for n in range(UNITS):
                        step(kv * B + b, b, n, kv)
            turns(eng, KV, head, own, per)
            for n in range(UNITS + 3):
                step(GROUPS + n // UNITS, n // UNITS, n % UNITS, KV)

        names = """wo_hi wo_lo constants power_set projected q_copied copied squared sums_done
            means_done r_ready roped rope_added qk_ready
            qk_turned qkT_hi qkT_lo v_hi v_lo scores_ready negmax_done bias_ready exp_done rtotal_done
            probs_ready p_turned pT_hi pT_lo pv_done oT_hi oT_lo out_half_done out_done out_added"""
        s = {n: sem("c_" + n) for n in names.split()}
        s.update(w_loaded=weights.w_loaded, wo_loaded=weights.wo_loaded, w_hi=weights.w_hi, w_lo=weights.w_lo)
        own = Count(sem("c_vector_own"))
        block = ctx.enter_context(nc.Block())

        first_banks = {(0, 1): banks[2:4], (1, 0): banks[0:2], (1, 1): banks[6:8]}

        def keys_of(j):
            return S + (j + 1) * P

        def rope(eng, g, j):
            n = g * 2 + j
            eng.wait_ge(s["copied"], n + 1)
            at_least(eng, s["rope_added"], n)
            H2 = HD // 2
            heads = lambda ap: ap.rearrange("p (h d) -> p h d", d=HD)
            for src, at, table, m in ((qs[:, j], slice(0, NQ), 0, REP),
                                      (ks[:, j, 2 * HD:3 * HD], slice(NQ, NQ + HD), 1, 1)):
                a, o1, o2 = heads(src), heads(t1[:, at]), heads(t2[:, at])
                wide = lambda t: t[:, None, :].to_broadcast([P, m, t.shape[-1]])
                eng.tensor_tensor(o1, a, wide(cosw[table][:, j]), ALU.mult).then_inc(s["roped"], 1)
                eng.tensor_tensor(o2[:, :, 0:H2], a[:, :, H2:], wide(sinw[table][:, j, 0:H2]),
                                  ALU.mult).then_inc(s["roped"], 1)
                eng.tensor_tensor(o2[:, :, H2:], a[:, :, 0:H2], wide(sinw[table][:, j, H2:]),
                                  ALU.mult).then_inc(s["roped"], 1)

        @block.sync
        def _(sp):
            with sp.Fori(1, KV) as kv:
                one = lambda t: t[bass.ds(kv, 1)].rearrange("a p n -> (a p) n")
                sp.wait_ge(s["w_lo"], kv * 2)
                sp.dma_start(raw[:], one(dram["wqkv"])).then_inc(s["w_loaded"], 16)
                sp.wait_ge(s["wo_lo"], kv)
                sp.dma_start(raw_o[:], one(dram["wo"])).then_inc(s["wo_loaded"], 16)
            for into, source, landed in next_start.loads:
                sp.dma_start(into, source).then_inc(landed, 16)

        @block.gpsimd
        def _(p):
            norm.gpsimd(p, 1)
            p.memset(power[:], -0.5).then_inc(s["power_set"], 1)
            p.wait_ge(s["power_set"], 1)

            def squares(g, j):
                n = g * 2 + j
                p.wait_ge(s["copied"], n + 1)
                at_least(p, s["sums_done"], n)
                p.tensor_tensor(sq[:, 0:NQ], qs[:, j], qs[:, j], ALU.mult).then_inc(s["squared"], 1)
                kk = ks[:, j].rearrange("p (c n) -> p c n", c=2)[:, :, 0:HD]
                p.tensor_tensor(sq[:, NQ:].rearrange("p (c n) -> p c n", c=2), kk, kk,
                                ALU.mult).then_inc(s["squared"], 1)

            def inverse_root(g, b, j):
                p.wait_ge(s["means_done"], g * 2 + j + 1)
                at_least(p, s["exp_done"], (g - 3) * UNITS)
                p.tensor_tensor(r[:, b % 4, j, :], means[:], power[:], ALU.pow).then_inc(s["r_ready"], 1)

            for g, j in ((0, 0), (0, 1), (1, 0)):
                squares(g, j)
                inverse_root(g, g, j)
            p.wait_ge(s["constants"], 4)
            squares(1, 1)
            rope(p, 1, 1)
            inverse_root(1, 1, 1)

            def step(g, b, n, kv):
                if n in (3, 7) and lies(g + 2):
                    squares(g + 2, n // 4)
                    rope(p, g + 2, n // 4)
                    inverse_root(g + 2, b + 2, n // 4)
            heads(p, step)
            next_norm.gpsimd(p, 0)
            next_start.split(p)

        @block.scalar
        def _(act):
            def split_hi(kv, part):
                act.wait_ge(s["w_loaded"], kv * 16 + 16)
                at_least(act, s["projected"], kv * (2 * B))
                at = slice(part * WQ, part * WQ + WQ)
                act.activation(w[0][:, at], raw[:, at], ACT.Copy).then_inc(s["w_hi"], 1)

            def split_wo_hi(kv):
                act.wait_ge(s["wo_loaded"], kv * 16 + 16)
                at_least(act, s["out_done"], kv * B)
                act.activation(wo[0][:], raw_o[:], ACT.Copy).then_inc(s["wo_hi"], 1)

            def copy(g, j, two=banks[4:6]):
                n = g * 2 + j
                act.wait_ge(s["projected"], n + 1)
                at_least(act, s["roped"], (n - 1) * 6)
                at_least(act, s["qk_ready"], n - 1)
                at_least(act, s["v_lo"], n - 1)
                act.activation(qs[:, j], two[0][:], ACT.Copy).then_inc(s["q_copied"], 1)
                act.activation(ks[:, j], two[1][:], ACT.Copy).then_inc(s["copied"], 1)

            def v_hi(g, b, j):
                at_least(act, s["pv_done"], (g - 3) * 2)
                act.wait_ge(s["copied"], g * 2 + j + 1)
                vv = ks[:, j].rearrange("p (c n) -> p c n", c=2)[:, :, HD:2 * HD]
                act.activation(V[0][:, b % 4, :, j, :], vv, ACT.Copy).then_inc(s["v_hi"], 1)

            def qkT_hi(g, b, j):
                act.wait_ge(s["qk_turned"], g * 2 + j + 1)
                at_least(act, s["scores_ready"], (g - 1) * UNITS)
                act.activation(qT[0][:, b % 2, :, j * P:j * P + P],
                               banks[4][:].rearrange("p (h n) -> p h n", h=REP), ACT.Copy).then_inc(s["qkT_hi"], 1)
                act.activation(kT[0][:, b % 2, :].rearrange("p (c n) -> p c n", c=2)[:, :, j * P:j * P + P],
                               banks[5][:, 0:2 * P].rearrange("p (c n) -> p c n", c=2),
                               ACT.Copy).then_inc(s["qkT_hi"], 1)

            def oT_hi(g, half):
                act.wait_ge(s["pv_done"], g * 2 + half + 1)
                at_least(act, s["out_done"] if half else s["out_half_done"], g)
                act.activation(OT[0][:, 2 * half:2 * half + 2, :], banks[6][:].rearrange("p (h n) -> p h n", h=2),
                               ACT.Copy).then_inc(s["oT_hi"], 1)

            def exp(g, b, n):
                u, slot, keys = g * UNITS + n, n % 2, keys_of(n % 2)
                act.wait_ge(s["bias_ready"], u + 1)
                at_least(act, s["p_turned"], u - 1)
                at_least(act, s["probs_ready"], u - 1)
                act.activation(probs[:, slot, 0:keys], banks[slot][:, 0:keys], ACT.Exp,
                               bias=bias[:, slot:slot + 1], scale=r[:, b % 4, n % 2, n // 2:n // 2 + 1],
                               accum_out=total[:, slot:slot + 1]).then_inc(s["exp_done"], 1)

            def divide(g, b, n):
                u, slot, keys = g * UNITS + n, n % 2, keys_of(n % 2)
                act.wait_ge(s["rtotal_done"], u + 1)
                act.activation(probs[:, slot, 0:keys], probs[:, slot, 0:keys], ACT.Copy,
                               scale=rtotal[:, slot:slot + 1]).then_inc(s["probs_ready"], 1)

            def pT_hi(g, n):
                u, j, kt = g * UNITS + n, n % 2, keys_of(n % 2) // P
                act.wait_ge(s["p_turned"], u + 1)
                at_least(act, s["pv_done"], g * 2 + n // 4 - 1)
                act.activation(PT[0][:, n // 4, 0:kt, n // 2 % 2, j * P:j * P + P],
                               banks[2 + j][:, 0:kt * P].rearrange("p (k n) -> p k n", k=kt),
                               ACT.Copy).then_inc(s["pT_hi"], 1)

            copy(0, 0)
            norm.scalar_hi(act, 1)
            copy(0, 1, first_banks[0, 1])
            v_hi(0, 0, 0)
            v_hi(0, 0, 1)
            copy(1, 0, first_banks[1, 0])
            qkT_hi(0, 0, 0)
            qkT_hi(0, 0, 1)
            copy(1, 1, first_banks[1, 1])
            exp(0, 0, 0)
            divide(0, 0, 0)

            def step(g, b, n, kv):
                ahead(exp, g, b, n + 1)
                if is_step(g, n, 9):
                    next_norm.scalar_hi(act, 0)
                if n == 0:
                    if lies(g - 1):
                        oT_hi(g - 1, 0)
                    if b == 2 and lies(g + 2):
                        split_hi(kv + 1, 1)
                if n == 1:
                    if lies(g + 1):
                        qkT_hi(g + 1, b + 1, 0)
                        v_hi(g + 1, b + 1, 0)
                        v_hi(g + 1, b + 1, 1)
                    if b == 1 and lies(g):
                        split_wo_hi(kv)
                if n == 3 and lies(g + 2):
                    copy(g + 2, 0)
                if n == 4 and lies(g - 1):
                    oT_hi(g - 1, 1)
                if n == 5 and lies(g + 1):
                    qkT_hi(g + 1, b + 1, 1)
                if n == 7 and lies(g + 2):
                    copy(g + 2, 1)
                    if b == 1 and lies(g + 3):
                        split_hi(kv + 1, 0)
                if lies(g):
                    pT_hi(g, n)
                ahead(divide, g, b, n + 1)
            heads(act, step)

        @block.tensor
        def _(pe):
            def project(g, b, j, pieces=range(4), two=banks[4:6]):
                n, b = g * 2 + j, b % B
                own_rows = both(hT, ALL, slice(0, KD), slice((2 * b + j) * P, (2 * b + j) * P + P))
                ctx_rows = both(ctxT, ALL, slice(0, KD), b, slice(j * P, j * P + P))
                if 0 in pieces:
                    if not isinstance(n, int) or n >= 4:
                        pe.wait_ge(s["qkT_hi"], n * 2 - 2)
                        pe.wait_ge(s["qkT_lo"], n * 2 - 2)
                for piece in pieces:
                    if piece < KD:
                        c = piece * NQ
                        product(pe, two[0][:], both(own_rows, ALL, piece), both(w, ALL, slice(c, c + NQ)),
                                piece == 0, piece == KD - 1)
                        continue
                    rows, at, out = ((ctx_rows, WQ, two[1][:, 0:2 * HD]) if piece == 2 else
                                     (own_rows, WQ + WK, two[1][:, 2 * HD:]))
                    for k in range(KD):
                        c = at + k * 2 * HD
                        ins = product(pe, out, both(rows, ALL, k), both(w, ALL, slice(c, c + 2 * HD)),
                                      k == 0, k == KD - 1)
                if 3 in pieces:
                    ins.then_inc(s["projected"], 1)

            def wait_weights(kv):
                pe.wait_ge(s["w_hi"], kv * 2 + 2)
                pe.wait_ge(s["w_lo"], kv * 2 + 2)

            def turn_qk(g, j, copied):
                n = g * 2 + j
                pe.wait_ge(s["qk_ready"], n + 1)
                pe.wait_ge(s["copied"], copied)
                for h in range(REP):
                    pe.transpose(banks[4][:, h * P:h * P + P], qk[:, j, h * HD:h * HD + HD], ident[:])
                pe.transpose(banks[5][:, 0:P], qk[:, j, NQ + HD:], ident[:])
                pe.transpose(banks[5][:, P:2 * P], qk[:, j, NQ:NQ + HD], ident[:]).then_inc(s["qk_turned"], 1)

            def scores(g, b, n):
                u, j, h, keys = g * UNITS + n, n % 2, n // 2, keys_of(n % 2)
                if n == 0:
                    pe.wait_ge(s["qkT_hi"], g * 4 + 4)
                    pe.wait_ge(s["qkT_lo"], g * 4 + 4)
                at_least(pe, s["exp_done"], u - 1)
                out = banks[j]
                product(pe, out[:, 0:keys], both(qT, ALL, b % 2, h, slice(j * P, j * P + P)),
                        both(kT, ALL, b % 2, slice(0, keys)), True, False, shared=True)
                pe.matmul(out[:, keys - P:keys], ident16[:], above16[:], start=False, stop=True,
                          skip_group_check=True).then_inc(s["scores_ready"], 1)

            def turn_p(g, n):
                u, j, kt = g * UNITS + n, n % 2, keys_of(n % 2) // P
                pe.wait_ge(s["probs_ready"], u + 1)
                at_least(pe, s["pT_hi"], u - 1)
                at_least(pe, s["pT_lo"], u - 1)
                for k in range(kt):
                    ins = pe.transpose(banks[2 + j][:, k * P:k * P + P], probs[:, j, k * P:k * P + P], ident[:])
                ins.then_inc(s["p_turned"], 1)

            def values(g, b, half, key_tiles):
                if 0 in key_tiles:
                    pe.wait_ge(s["pT_hi"], g * UNITS + 4 * half + 4)
                    pe.wait_ge(s["pT_lo"], g * UNITS + 4 * half + 4)
                    pe.wait_ge(s["v_lo"], g * 2 + 2)
                    at_least(pe, s["oT_hi"], g * 2 + half)
                    at_least(pe, s["oT_lo"], g * 2 + half)
                out = banks[6][:].rearrange("p (h n) -> p h n", h=2)
                for kt in key_tiles:
                    at = slice(P if kt == 3 else 0, S)
                    ins = product(pe, out[:, :, at], both(V, ALL, b % 4, kt // 2, kt % 2),
                                  both(PT, ALL, half, kt, ALL, at), kt == 0, kt == 3, shared=True)
                if 3 in key_tiles:
                    ins.then_inc(s["pv_done"], 1)

            def project_out(g, kv, j, half):
                if half == 0 and j == 0:
                    pe.wait_ge(s["oT_hi"], g * 2 + 1)
                    pe.wait_ge(s["oT_lo"], g * 2 + 1)
                    pe.wait_ge(s["wo_lo"], kv + 1)
                    at_least(pe, s["out_added"], g)
                if half == 1 and j == 0:
                    pe.wait_ge(s["oT_hi"], g * 2 + 2)
                    pe.wait_ge(s["oT_lo"], g * 2 + 2)
                for h in range(2 * half, 2 * half + 2):
                    ins = product(pe, banks[7][:, j * D:j * D + D], both(OT, ALL, h, slice(j * P, j * P + P)),
                                  both(wo, ALL, slice(h * D, h * D + D)), j == 0 and h == 0, h == REP - 1,
                                  shared=True)
                if j == 1:
                    ins.then_inc(s["out_done"] if half else s["out_half_done"], 1)

            wait_weights(0)
            project(0, 0, 0)
            norm.tensor(pe, 1)
            project(0, 0, 1, two=first_banks[0, 1])
            project(1, 1, 0, two=first_banks[1, 0])
            turn_qk(0, 0, 1)
            norm.wait_half(pe, 1)
            project(1, 1, 1, (0, 1), first_banks[1, 1])
            pe.wait_ge(s["qkT_hi"], 2)
            pe.wait_ge(s["qkT_lo"], 2)
            turn_qk(0, 1, 3)
            project(1, 1, 1, (2, 3), first_banks[1, 1])
            pe.wait_ge(weights.constants_ready, 2)
            pe.wait_ge(s["copied"], 3)
            scores(0, 0, 0)
            scores(0, 0, 1)

            def step(g, b, n, kv):
                before = kv if b else kv - 1
                if n != 6:
                    ahead(scores, g, b, n + 2)
                if is_step(g, n, 9):
                    next_norm.tensor(pe, 0)
                if n == 0:
                    if lies(g + 1):
                        turn_qk(g + 1, 0, g * 2 + 4)
                if n == 1 and lies(g - 2):
                    project_out(g - 2, None, 1, 1)
                if n in (1, 2, 3) and lies(g - 1):
                    values(g - 1, b - 1, 1, ((0, 1), (2,), (3,))[n - 1])
                if n == 2 and lies(g + 2):
                    if b == 2:
                        wait_weights(kv + 1)
                    project(g + 2, b + 2, 0, (0, 1))
                if n == 3 and lies(g - 1):
                    project_out(g - 1, before, 0, 0)
                if n == 5 and lies(g - 1):
                    project_out(g - 1, before, 1, 0)
                if n in (5, 6, 7) and lies(g):
                    values(g, b, 0, ((0, 1), (2,), (3,))[n - 5])
                if n == 6 and lies(g + 2):
                    project(g + 2, b + 2, 1, (0, 1))
                if n == 6:
                    ahead(scores, g, b, n + 2)
                if n == 7 and lies(g - 1):
                    project_out(g - 1, before, 0, 1)
                if lies(g):
                    turn_p(g, n)
                if n == 4 and lies(g + 1):
                    turn_qk(g + 1, 1, g * 2 + 5 if lies(g + 2) else g * 2 + 4)
                if lies(g + 2):
                    if n == 2:
                        project(g + 2, b + 2, 0, (2, 3))
                    if n == 6:
                        project(g + 2, b + 2, 1, (2, 3))
            heads(pe, step)

        @block.vector
        def _(v):
            def split_lo(kv, part):
                v.wait_ge(s["w_hi"], kv * 2 + part + 1)
                at_least(v, s["projected"], kv * (2 * B))
                at = slice(part * WQ, part * WQ + WQ)
                v.tensor_tensor(w[1][:, at], raw[:, at], f32(w[0][:, at]), ALU.subtract).then_inc(s["w_lo"], 1)

            def split_wo_lo(kv):
                v.wait_ge(s["wo_hi"], kv + 1)
                v.tensor_tensor(wo[1][:], raw_o[:], f32(wo[0][:]), ALU.subtract).then_inc(s["wo_lo"], 1)

            def v_lo(g, b, j):
                v.wait_ge(s["v_hi"], g * 2 + j + 1)
                vv = ks[:, j].rearrange("p (c n) -> p c n", c=2)[:, :, HD:2 * HD]
                v.tensor_tensor(V[1][:, b % 4, :, j, :], vv, f32(V[0][:, b % 4, :, j, :]),
                                ALU.subtract).then_inc(s["v_lo"], 1)

            def sum_squares(g, j):
                n = g * 2 + j
                v.wait_ge(s["squared"], n * 2 + 2)
                v.tensor_reduce(sums[:], sq[:].rearrange("p (h d) -> p h d", d=HD), AX_X,
                                ALU.add).then_inc(s["sums_done"], 1)
                v.wait_ge(s["sums_done"], n + 1)
                at_least(v, s["r_ready"], n)
                v.tensor_scalar(means[:], sums[:], 1.0 / HD, RMS_EPS, ALU.mult,
                                ALU.add).then_inc(s["means_done"], 1)

            def add_rope(g, b, j):
                n = g * 2 + j
                v.wait_ge(s["roped"], n * 6 + 6)
                v.wait_ge(s["r_ready"], n + 1)
                at_least(v, s["qk_turned"], n - 1)
                v.tensor_tensor(qk[:, j, 0:NQ + HD], t1[:], t2[:], ALU.add).then_inc(s["rope_added"], 1)
                own.tick(v.scalar_tensor_tensor(qk[:, j, NQ + HD:], ks[:, j, 0:HD], r[:, b % 4, j, 4:5],
                                                headnorm[:, 1, :], ALU.mult, ALU.mult))
                own.settle(v)
                v.wait_ge(s["rope_added"], n + 1)
                v.tensor_scalar(qk[:, j, NQ:NQ + HD], qk[:, j, NQ:NQ + HD], r[:, b % 4, j, 5:6], None,
                                ALU.mult).then_inc(s["qk_ready"], 1)

            def qkT_lo(g, b, j):
                v.wait_ge(s["qkT_hi"], g * 4 + 2 * j + 2)
                at = (ALL, b % 2, ALL, slice(j * P, j * P + P))
                v.tensor_tensor(qT[1][at], banks[4][:].rearrange("p (h n) -> p h n", h=REP), f32(qT[0][at]),
                                ALU.subtract).then_inc(s["qkT_lo"], 1)
                part = lambda t: t[:, b % 2, :].rearrange("p (c n) -> p c n", c=2)[:, :, j * P:j * P + P]
                v.tensor_tensor(part(kT[1]), banks[5][:, 0:2 * P].rearrange("p (c n) -> p c n", c=2),
                                f32(part(kT[0])), ALU.subtract).then_inc(s["qkT_lo"], 1)

            def oT_lo(g, half):
                v.wait_ge(s["oT_hi"], g * 2 + half + 1)
                v.tensor_tensor(OT[1][:, 2 * half:2 * half + 2, :], banks[6][:].rearrange("p (h n) -> p h n", h=2),
                                f32(OT[0][:, 2 * half:2 * half + 2, :]), ALU.subtract).then_inc(s["oT_lo"], 1)

            def row_max(g, b, n):
                u, slot, keys = g * UNITS + n, n % 2, keys_of(n % 2)
                if n == 0:
                    v.wait_ge(s["r_ready"], g * 2 + 2)
                v.wait_ge(s["scores_ready"], u + 1)
                at_least(v, s["bias_ready"], u - 1)
                v.tensor_reduce(negmax[:, slot:slot + 1], banks[slot][:, 0:keys], AX_X, ALU.max,
                                negate=True).then_inc(s["negmax_done"], 1)
                v.wait_ge(s["negmax_done"], u + 1)
                at_least(v, s["exp_done"], u - 1)
                v.tensor_tensor(bias[:, slot:slot + 1], negmax[:, slot:slot + 1],
                                r[:, b % 4, n % 2, n // 2:n // 2 + 1], ALU.mult).then_inc(s["bias_ready"], 1)

            def pT_lo(g, n):
                u, j, kt = g * UNITS + n, n % 2, keys_of(n % 2) // P
                v.wait_ge(s["pT_hi"], u + 1)
                at = (ALL, n // 4, slice(0, kt), n // 2 % 2, slice(j * P, j * P + P))
                v.tensor_tensor(PT[1][at], banks[2 + j][:, 0:kt * P].rearrange("p (k n) -> p k n", k=kt),
                                f32(PT[0][at]), ALU.subtract).then_inc(s["pT_lo"], 1)

            def row_sum(g, b, n):
                u, slot = g * UNITS + n, n % 2
                v.wait_ge(s["exp_done"], u + 1)
                at_least(v, s["probs_ready"], u - 1)
                v.reciprocal(rtotal[:, slot:slot + 1], total[:, slot:slot + 1]).then_inc(s["rtotal_done"], 1)

            def add_out(g, b):
                v.wait_ge(s["out_done"], g + 1)
                at_least(v, s["out_added"], g)
                at = slice(2 * (b % B), 2 * (b % B) + 2)
                v.tensor_tensor(x[:, at, :], banks[7][:].rearrange("p (j d) -> p j d", j=2), x[:, at, :],
                                ALU.add).then_inc(s["out_added"], 1)

            norm.vector_moments(v, 1)
            norm.vector_normalize(v, 1)
            v.wait_ge(weights.tables_loaded, 64)
            H2 = HD // 2
            for m, scale in ((0, SCALE), (1, 1.0)):
                wide = headnorm[:, m:m + 1, :].to_broadcast([P, 2, HD])
                own.tick(v.scalar_tensor_tensor(cosw[m][:], cos[:], scale, wide, ALU.mult, ALU.mult))
                own.tick(v.scalar_tensor_tensor(sinw[m][:, :, 0:H2], sin[:, :, 0:H2], scale, wide[:, :, H2:],
                                                ALU.mult, ALU.mult))
                own.settle(v)
                v.scalar_tensor_tensor(sinw[m][:, :, H2:], sin[:, :, H2:], scale, wide[:, :, 0:H2],
                                       ALU.mult, ALU.mult).then_inc(s["constants"], 2)
            v.wait_ge(s["constants"], 4)
            rope(v, 0, 0)
            sum_squares(0, 0)
            norm.vector_lo(v, 1)
            v_lo(0, 0, 0)
            v_lo(0, 0, 1)
            add_rope(0, 0, 0)
            rope(v, 0, 1)
            sum_squares(0, 1)
            qkT_lo(0, 0, 0)
            add_rope(0, 0, 1)
            rope(v, 1, 0)
            sum_squares(1, 0)
            qkT_lo(0, 0, 1)
            add_rope(1, 1, 0)
            row_max(0, 0, 0)
            row_max(0, 0, 1)
            row_sum(0, 0, 0)

            def step(g, b, n, kv):
                if n and lies(g):
                    pT_lo(g, n - 1)
                if n == 0 and lies(g - 1):
                    pT_lo(g - 1, UNITS - 1)
                ahead(row_max, g, b, n + 2)
                ahead(row_sum, g, b, n + 1)
                if is_step(g, n, 5):
                    v.wait_ge(s["out_added"], GROUPS - 2)
                    next_norm.vector_moments(v, 0)
                if is_step(g, n, 7):
                    next_norm.vector_normalize(v, 0)
                if is_step(g, n, 10):
                    next_norm.vector_lo(v, 0)
                if n == 0:
                    if lies(g - 1):
                        oT_lo(g - 1, 0)
                    if b == 2 and lies(g + 2):
                        split_lo(kv + 1, 1)
                if n == 1:
                    if lies(g + 1):
                        qkT_lo(g + 1, b + 1, 0)
                        sum_squares(g + 1, 1)
                    if b == 1 and lies(g):
                        split_wo_lo(kv)
                if n == 2:
                    if lies(g - 2):
                        add_out(g - 2, b - 2)
                    if lies(g + 1):
                        v_lo(g + 1, b + 1, 0)
                        v_lo(g + 1, b + 1, 1)
                if n == 6 and lies(g + 2):
                    add_rope(g + 2, b + 2, 0)
                if n == 3 and lies(g + 1):
                    add_rope(g + 1, b + 1, 1)
                if n == 4 and lies(g - 1):
                    oT_lo(g - 1, 1)
                if n == 5:
                    if lies(g + 1):
                        qkT_lo(g + 1, b + 1, 1)
                    if lies(g + 2):
                        sum_squares(g + 2, 0)
                if n == 7 and b == 1 and lies(g + 3):
                    split_lo(kv + 1, 0)
            heads(v, step, own, 2 * B)


class Top2Start:

    def __init__(self, sb, sem, dram):
        self.raw1 = sb("w1_raw", [P, 2, KD * P], F32)
        self.raw2 = sb("w2_raw", [P, 2, D], F32)
        self.b1 = sb("b1", [P, ED * CHUNKS], F32)
        self.b2raw = sb("b2_raw", [ED, D], F32)
        self.gate = sb("gate_w", [P, KD * ED + ED], F32)
        self.w1_loaded = [sem(f"d_w1_loaded{slot}") for slot in range(2)]
        self.w2_loaded = [sem(f"d_w2_loaded{slot}") for slot in range(2)]
        self.small_loaded = sem("d_small_loaded")
        pair = lambda n, s: (sb(n + "_hi", s, F32R), sb(n + "_lo", s, F32R))
        self.w1, self.gw = pair("w1", [P, 2, KD * P]), pair("gate_split", [P, KD * ED])
        names = "w1_hi w1_lo gw_hi gw_lo"
        self.ready = {n: sem("d_" + n) for n in names.split()}
        self.loads = [(into[:], dram[name], self.small_loaded)
                      for into, name in ((self.gate, "gate"), (self.b1, "b1"), (self.b2raw, "b2"))]
        for q in range(2):
            self.loads += [(self.raw1[:, q], dram["wd"][q][:, 0:KD * P], self.w1_loaded[q]),
                           (self.raw2[:, q], dram["wd"][q][:, KD * P:], self.w2_loaded[q])]

    def split(self, p):
        s, w1 = self.ready, self.w1
        for q in range(2):
            p.wait_ge(self.w1_loaded[q], 16)
            split(p, w1[0][:, q], w1[1][:, q], self.raw1[:, q], s["w1_hi"], s["w1_lo"], q)
        p.wait_ge(self.small_loaded, 48)
        split(p, self.gw[0][:], self.gw[1][:], self.gate[:, 0:KD * ED], s["gw_hi"], s["gw_lo"])


def top2_ffn(nc, banks, x, hT, ident, iota, dram, out, start, norm):
    CH = ED * CHUNKS
    LAST = CH - 1
    with ExitStack() as ctx:
        sb = lambda n, s, d: ctx.enter_context(nc.sbuf_tensor(n, s, d))
        sem = lambda n: ctx.enter_context(nc.semaphore(n))
        pair = lambda n, s: (sb(n + "_hi", s, F32R), sb(n + "_lo", s, F32R))
        ALL = slice(None)
        raw1, raw2, b1, gate = start.raw1, start.raw2, start.b1, start.gate
        w1, gw = start.w1, start.gw
        w2, b2 = pair("w2", [P, 2, D]), pair("b2", [ED, D])
        b1e = sb("b1_of_expert", [P, CHUNKS], F32)
        logitsT = sb("gate_logitsT", [ED, 2, HALF], F32)
        logits = sb("logits", [P, TILES, ED], F32)
        top = sb("logits_max", [P, TILES], F32)
        exps = sb("gate_exps", [P, TILES, ED], F32)
        gsum = sb("gate_sum", [P, TILES], F32)
        gprobs = sb("gate_probs", [P, TILES, ED], F32)
        comb = sb("d_comb", [P, TILES, ED], F32)
        mine = sb("d_comb_of_expert", [P, TILES], F32)
        combT = pair("combT", [ED, 2, HALF])
        g = sb("d_gelu", [P, 2, HALF], F32)
        aT = pair("d_aT", [P, 2, B * S])

        names = """w2_hi w2_lo b2_hi b2_lo logitsT_done logitsT_copied logits_done
            logits_shifted exps_ready comb_ready combT_done combT_hi combT_lo bias_done bias_added
            b1_ready up_done0 up_done1 gelu_ready aT_hi aT_lo down_done last_down added stored"""
        s = {n: sem("d_" + n) for n in names.split()}
        s.update(start.ready)
        own = Count(sem("d_vector_own"))
        picks = Choice(sb, own, "d", KDTOP, ED, 0.0, iota, comb)
        block = ctx.enter_context(nc.Block())

        def lies(q):
            return not isinstance(q, int) or q < CH

        def first(e):
            return isinstance(e, int) and e == 0

        @block.sync
        def _(sp):
            def load(q, slot):
                one = dram["wd"][bass.ds(q, 1)].rearrange("a p n -> (a p) n")
                sp.wait_ge(s["w1_lo"], q - 1)
                sp.dma_start(raw1[:, slot], one[:, 0:KD * P]).then_inc(start.w1_loaded[slot], 16)
                sp.wait_ge(s["w2_lo"], q - 1)
                sp.dma_start(raw2[:, slot], one[:, KD * P:]).then_inc(start.w2_loaded[slot], 16)
            with sp.Fori(1, CH // 2) as i:
                load(i * 2, 0)
                load(i * 2 + 1, 1)
            for t in range(0, TILES, 2):
                sp.wait_ge(s["added"], (ED - 1) * TILES + t + 2)
                sp.dma_start(out[:, t:t + 2, :], x[:, t:t + 2, :]).then_inc(s["stored"], 16)
            sp.wait_ge(s["stored"], 16 * (TILES // 2))

        @block.gpsimd
        def _(p):
            def lo1(q, slot):
                p.wait_ge(s["w1_hi"], q + 1)
                p.tensor_tensor(w1[1][:, slot], raw1[:, slot], f32(w1[0][:, slot]),
                                ALU.subtract).then_inc(s["w1_lo"], 1)

            def lo2(q, slot):
                p.wait_ge(s["w2_hi"], q + 1)
                p.tensor_tensor(w2[1][:, slot], raw2[:, slot], f32(w2[0][:, slot]),
                                ALU.subtract).then_inc(s["w2_lo"], 1)

            norm.gpsimd(p, 1)
            lo2(0, 0)
            split(p, b2[0][:], b2[1][:], start.b2raw[:], s["b2_hi"], s["b2_lo"])

            def expert(e):
                for c in range(CHUNKS):
                    q = e * CHUNKS + c
                    if lies(q + 1):
                        lo2(q + 1, (c + 1) % 2)
                    if lies(q + 2):
                        lo1(q + 2, c % 2)
            turns(p, ED, expert)

        @block.scalar
        def _(act):
            norm.scalar_hi(act, 1)
            act.wait_ge(start.small_loaded, 48)

            def unit(q, c, half):
                act.wait_ge(s[f"up_done{half}"], q + 1)
                at_least(act, s["aT_hi"], q * 2 + half - 1)
                at_least(act, s["aT_lo"], q * 2 + half - 1)
                act.activation(g[:, half], banks[2 * (c % 2) + half][:], ACT.Gelu_apprx_tanh,
                               bias=b1e[:, c:c + 1]).then_inc(s["gelu_ready"], 1)
                act.wait_ge(s["gelu_ready"], q * 2 + half + 1)
                at_least(act, s["down_done"], q - 1)
                act.activation(aT[0][:, c % 2, half * HALF:(half + 1) * HALF], g[:, half],
                               ACT.Copy).then_inc(s["aT_hi"], 1)

            def expert(e):
                at = slice(e * CHUNKS, e * CHUNKS + CHUNKS) if isinstance(e, int) else bass.ds(e * CHUNKS, CHUNKS)
                act.activation(b1e[:], b1[:, at], ACT.Copy).then_inc(s["b1_ready"], 1)
                act.wait_ge(s["b1_ready"], e + 1)
                for c in range(CHUNKS):
                    for half in range(2):
                        unit(e * CHUNKS + c, c, half)
                        if first(e) and c == 0 and half == 0:
                            for part in range(2):
                                act.wait_ge(s["logitsT_done"], part + 1)
                                act.activation(logitsT[:, part], banks[4 + part][0:ED, :],
                                               ACT.Copy).then_inc(s["logitsT_copied"], 1)
                    if first(e) and c == 0:
                        act.wait_ge(s["logits_shifted"], 1)
                        act.activation(exps[:], logits[:], ACT.Exp).then_inc(s["exps_ready"], 1)
                    if first(e) and c == 2:
                        act.wait_ge(s["combT_done"], 2)
                        for half in range(2):
                            act.activation(combT[0][:, half], banks[half][0:ED, :],
                                           ACT.Copy).then_inc(s["combT_hi"], 1)
            turns(act, ED, expert)

        @block.tensor
        def _(pe):
            def up(q, c, halves=range(2)):
                if 0 in halves:
                    pe.wait_ge(s["w1_lo"], q + 1)
                for half in halves:
                    at_least(pe, s["gelu_ready"], (q - 2) * 2 + half + 1)
                    for k in range(KD):
                        ins = product(pe, banks[2 * (c % 2) + half][:],
                                      both(w1, ALL, c % 2, slice(k * P, k * P + P)),
                                      both(hT, ALL, k, slice(half * HALF, half * HALF + HALF)), k == 0, k == KD - 1)
                    ins.then_inc(s[f"up_done{half}"], 1)

            def down(e, q, c):
                pe.wait_ge(s["w2_lo"], q + 1)
                for t in range(TILES):
                    if t % HT == 0:
                        pe.wait_ge(s["aT_lo"], q * 2 + t // HT + 1)
                    if c == 0 and t % 2 == 0 and not first(e):
                        pe.wait_ge(s["added"], (e - 1) * TILES + t + 2)
                    ins = product(pe, banks[4 + t // 2][:, (t % 2) * D:(t % 2) * D + D],
                                  both(aT, ALL, c % 2, slice(t * P, t * P + P)), both(w2, ALL, c % 2),
                                  c == 0 and t % 2 == 0, c == CHUNKS - 1, shared=True)
                    if isinstance(q, int) and q == LAST and t % 2 == 1 and t < TILES - 1:
                        ins.then_inc(s["last_down"], 1)
                ins.then_inc(s["down_done"], 1)

            def combine_biases(pair, half):
                pe.wait_ge(s["b2_lo"], 1)
                for i in range(HT):
                    ins = product(pe, banks[2 * pair + i // 2][:, (i % 2) * D:(i % 2) * D + D],
                                  both(combT, ALL, half, slice(i * P, i * P + P)), both(b2, ALL, ALL))
                ins.then_inc(s["bias_done"], 1)

            up(0, 0, (0,))
            up(1, 1, (0,))
            norm.tensor(pe, 1)
            pe.wait_ge(s["gw_lo"], 1)
            logits_transposed(pe, banks[4][0:ED, :], hT, gw, ED, 0).then_inc(s["logitsT_done"], 1)
            norm.wait_half(pe, 1)
            logits_transposed(pe, banks[5][0:ED, :], hT, gw, ED, 1).then_inc(s["logitsT_done"], 1)
            up(0, 0, (1,))
            for t in range(TILES):
                pe.wait_ge(s["logitsT_copied"], t // HT + 1)
                ins = pe.transpose(banks[6][:, t * ED:t * ED + ED],
                                   logitsT[:, t // HT, t % HT * P:t % HT * P + P], ident[0:ED, 0:ED])
            ins.then_inc(s["logits_done"], 1)

            def expert(e):
                for c in range(CHUNKS):
                    q = e * CHUNKS + c
                    if first(e) and c in (4, 5):
                        pe.wait_ge(s["bias_added"], 2 * c - 6)
                    if lies(q + 1):
                        up(q + 1, c + 1, (1,) if first(e) and c == 0 else (0, 1))
                    if first(e) and c == 0:
                        pe.wait_ge(s["logits_shifted"], 1)
                    if first(e) and c == 2:
                        pe.wait_ge(s["gelu_ready"], 6)
                        pe.wait_ge(s["comb_ready"], 1)
                        for half in range(2):
                            for i in range(HT):
                                ins = pe.transpose(banks[half][0:ED, i * P:i * P + P],
                                                   comb[:, HT * half + i, :], ident[:])
                            ins.then_inc(s["combT_done"], 1)
                    if first(e) and c == 3:
                        pe.wait_ge(s["gelu_ready"], 8)
                        combine_biases(1, 0)
                    if first(e) and c == 4:
                        pe.wait_ge(s["gelu_ready"], 10)
                        combine_biases(0, 1)
                    down(e, q, c)
                    if first(e) and c == 2:
                        pe.wait_ge(s["combT_hi"], 2)
                        pe.wait_ge(s["combT_lo"], 2)
            turns(pe, ED, expert)

        @block.vector
        def _(v):
            def hi1(q, slot):
                at_least(v, s["up_done1"], q - 1)
                at_least(v, s["w1_lo"], q - 1)
                v.wait_ge(start.w1_loaded[slot], (q - slot) * 8 + 16)
                v.tensor_copy(w1[0][:, slot], raw1[:, slot]).then_inc(s["w1_hi"], 1)

            def hi2(q, slot):
                at_least(v, s["down_done"], q - 1)
                at_least(v, s["w2_lo"], q - 1)
                v.wait_ge(start.w2_loaded[slot], (q - slot) * 8 + 16)
                v.tensor_copy(w2[0][:, slot], raw2[:, slot]).then_inc(s["w2_hi"], 1)

            def lo(q, c, half):
                v.wait_ge(s["aT_hi"], q * 2 + half + 1)
                v.tensor_tensor(aT[1][:, c % 2, half * HALF:(half + 1) * HALF], g[:, half],
                                f32(aT[0][:, c % 2, half * HALF:(half + 1) * HALF]),
                                ALU.subtract).then_inc(s["aT_lo"], 1)

            def add(e):
                last = isinstance(e, int) and e == ED - 1
                if not last:
                    v.wait_ge(s["down_done"], (e + 1) * CHUNKS)
                if first(e):
                    v.wait_ge(s["bias_added"], 4)
                else:
                    v.wait_ge(s["added"], e * TILES)
                column = comb[:, :, e:e + 1] if isinstance(e, int) else comb[:, :, bass.ds(e, 1)]
                own.tick(v.tensor_copy(mine[:], column.rearrange("p t a -> p (t a)")))
                own.settle(v)
                for t in range(TILES):
                    if last and t % 2 == 0:
                        if t < TILES - 2:
                            v.wait_ge(s["last_down"], t // 2 + 1)
                        else:
                            v.wait_ge(s["down_done"], CH)
                    v.scalar_tensor_tensor(x[:, t, :], banks[4 + t // 2][:, (t % 2) * D:(t % 2) * D + D],
                                           mine[:, t:t + 1], x[:, t, :], ALU.mult, ALU.add).then_inc(s["added"], 1)

            def shift_logits():
                shape = [P, TILES, ED]
                v.wait_ge(s["logits_done"], 1)
                own.tick(v.tensor_tensor(logits[:], banks[6][:, 0:TILES * ED].rearrange("p (t e) -> p t e", e=ED),
                                         gate[:, None, KD * ED:].to_broadcast(shape), ALU.add))
                own.settle(v)
                own.tick(v.tensor_reduce(top[:], logits[:], AX_X, ALU.max))
                own.settle(v)
                v.tensor_tensor(logits[:], logits[:], top[:, :, None].to_broadcast(shape),
                                ALU.subtract).then_inc(s["logits_shifted"], 1)

            def choose_experts():
                v.wait_ge(s["exps_ready"], 1)
                own.tick(v.tensor_reduce(gsum[:], exps[:], AX_X, ALU.add))
                own.settle(v)
                own.tick(v.reciprocal(gsum[:], gsum[:]))
                own.settle(v)
                own.tick(v.tensor_tensor(gprobs[:], exps[:], gsum[:, :, None].to_broadcast([P, TILES, ED]),
                                         ALU.mult))
                own.settle(v)
                picks.indices(v, gprobs)
                picks.combine(v, gprobs).then_inc(s["comb_ready"], 1)
                v.wait_ge(s["comb_ready"], 1)

            norm.vector_moments(v, 1)
            v.wait_ge(start.small_loaded, 48)
            hi2(0, 0)
            norm.vector_normalize(v, 1)
            norm.vector_lo(v, 1)

            def expert(e):
                for c in range(CHUNKS):
                    q = e * CHUNKS + c
                    lo(q, c, 0)
                    if first(e) and c == 0:
                        shift_logits()
                    lo(q, c, 1)
                    if first(e) and c == 2:
                        for half in range(2):
                            v.wait_ge(s["combT_hi"], half + 1)
                            v.tensor_tensor(combT[1][:, half], banks[half][0:ED, :],
                                            f32(combT[0][:, half]), ALU.subtract).then_inc(s["combT_lo"], 1)
                    if first(e) and c in (3, 4):
                        v.wait_ge(s["bias_done"], c - 2)
                        for i in range(2):
                            t = HT * (c - 3) + 2 * i
                            v.tensor_tensor(x[:, t:t + 2, :],
                                            banks[2 * (4 - c) + i][:].rearrange("p (t d) -> p t d", t=2),
                                            x[:, t:t + 2, :], ALU.add).then_inc(s["bias_added"], 1)
                    if lies(q + 1):
                        hi2(q + 1, (c + 1) % 2)
                    if lies(q + 2):
                        hi1(q + 2, c % 2)
                    if c == 0 and not first(e):
                        add(e - 1)
                    if first(e) and c == 0:
                        choose_experts()
            turns(v, ED, expert, own, 1)
            add(ED - 1)


def program(nc, dram, out):
    with ExitStack() as ctx:
        sb = lambda n, s, d: ctx.enter_context(nc.sbuf_tensor(n, s, d))
        sem = lambda n: ctx.enter_context(nc.semaphore(n))
        banks = [ctx.enter_context(nc.psum_tensor(f"bank{i}", [P, HALF], F32)) for i in range(8)]
        x = sb("x", [P, TILES, D], F32)
        h = sb("h", [P, HT, D], F32)
        hT = (sb("hT_hi", [P, KD, B * S], F32R), sb("hT_lo", [P, KD, B * S], F32R))
        ident = sb("ident", [P, P], F32)
        iota = sb("iota", [P, EB], F32)
        norms = [Norm(sb, sem, f"ln{i + 1}", x, h, hT, use, ident) for i, use in
                 enumerate((banks[6:8] + banks[4:6], banks[0:4], banks[0:2] + banks[6:8], banks[4:8]))]
        start = Top2Start(sb, sem, dram)
        with ExitStack() as early:
            sb = lambda n, s, d: early.enter_context(nc.sbuf_tensor(n, s, d))
            ctxT = (sb("ctxT_hi", [P, KD, B, S], F32R), sb("ctxT_lo", [P, KD, B, S], F32R))
            with ExitStack() as part:
                sb_part = lambda n, s, d: part.enter_context(nc.sbuf_tensor(n, s, d))
                weights = AttentionWeights(sb, sb_part, sem, dram)
                routed = RoutedStart(sb_part, sem, dram, iota)
                token_expert_ffn(nc, banks, x, hT, ctxT, ident, dram, routed.loads + weights.loads,
                                 norms[0], norms[1], routed)
                routed_ffn(nc, banks, x, hT, ident, iota, dram, routed, norms[1], norms[2], weights)
            attention(nc, banks, x, hT, ctxT, ident, dram, weights, norms[2], norms[3], start)
        top2_ffn(nc, banks, x, hT, ident, iota, dram, out, start, norms[3])


def kernel(**inputs):
    import numpy as np
    import concourse.bacc as bacc
    from concourse import mybir as mb
    from concourse.bass_utils import run_bass_kernel_spmd

    a = {n: np.asarray(v) for n, v in inputs.items()}

    def rows(w):
        return w.reshape(-1, P, w.shape[-1]).transpose(1, 0, 2)

    def flat(w):
        return rows(w).reshape(P, -1)

    lay = {}
    lay["x"] = rows(a["x"].reshape(B * S, D))
    lay["token"] = a["itok_BxS_13_99985"].reshape(TILES, P).T
    lay["ctxT"] = rows(a["ctx_2048"].transpose(2, 0, 1).reshape(D, B * S)).reshape(P, KD, B, S)
    lay["ident"] = np.eye(P, dtype=np.float32)
    lay["iota"] = np.broadcast_to(np.arange(EB, dtype=np.float32), (P, EB))
    lay["router"] = np.concatenate([flat(a["L0_ffn_router_w"].T),
                                    np.broadcast_to(a["L0_ffn_router_bias"], (P, EB))], 1)
    gate = [a["L0_ffn_shared_gate_w"], *a["L0_ffn_expert_gate_w"]]
    up = [a["L0_ffn_shared_up_w"], *a["L0_ffn_expert_up_w"]]
    down = [a["L0_ffn_shared_down_w"], *a["L0_ffn_expert_down_w"]]
    lay["wb"] = np.stack([np.concatenate([flat(g.T), flat(u.T), flat(d.T)], 1)
                          for g, u, d in zip(gate, up, down)])
    wk = [a["L1_xattn_wk_ctx"], a["L1_xattn_wv_ctx"], a["L1_xattn_wk"], a["L1_xattn_wv"]]
    head = lambda w, g: w[:, g * HD:(g + 1) * HD]
    lay["wqkv"] = np.stack([np.concatenate([
        flat(a["L1_xattn_wq"][:, g * REP * HD:(g + 1) * REP * HD]),
        flat(np.concatenate([head(w, g) for w in wk[:2]], 1)),
        flat(np.concatenate([head(w, g) for w in wk[2:]], 1))], 1) for g in range(KV)])
    lay["wo"] = np.stack([flat(a["L1_xattn_wo"][g * REP * HD:(g + 1) * REP * HD]) for g in range(KV)])
    inv = (np.float32(1) / np.float32(10000) ** (np.arange(0, HD, 2, dtype=np.float32) / np.float32(HD)))
    angle = np.outer(np.arange(S, dtype=np.float32), inv.astype(np.float32))
    cos, sin = np.cos(angle), np.sin(angle)
    lay["cos"] = rows(np.concatenate([cos, cos], 1).astype(np.float32))
    lay["sin"] = rows(np.concatenate([-sin, sin], 1).astype(np.float32))
    lay["headnorm"] = np.stack([np.broadcast_to(a[f"L1_xattn_{n}_norm_w"], (P, HD)) for n in "qk"], 1)
    lay["above"] = np.triu(np.full((P, P), MASKED, np.float32), 1)
    lay["wd"] = np.stack([np.concatenate([flat(a["L1_ffn_w1"][e][:, c * P:(c + 1) * P]),
                                          a["L1_ffn_w2"][e][c * P:(c + 1) * P]], 1)
                          for e in range(ED) for c in range(CHUNKS)])
    lay["b1"] = a["L1_ffn_b1"].reshape(ED * CHUNKS, P).T
    lay["b2"] = a["L1_ffn_b2"]
    lay["gate"] = np.concatenate([flat(a["L1_ffn_gate_w"]), np.broadcast_to(a["L1_ffn_gate_b"], (P, ED))], 1)

    nc = bacc.Bacc("TRN2", target_bir_lowering=False, num_devices=1)
    arrays, dram = {}, {}
    for name, v in lay.items():
        arrays[f"in_{name}"] = v = np.ascontiguousarray(v)
        dram[name] = nc.dram_tensor(f"in_{name}", v.shape, mb.dt.from_np(v.dtype), kind="ExternalInput").ap()
    out = nc.dram_tensor("out_x", (P, TILES, D), mb.dt.float32, kind="ExternalOutput").ap()
    program(nc, dram, out)
    got = run_bass_kernel_spmd(nc, [arrays], core_ids=[0]).results[0]["out_x"]
    return np.ascontiguousarray(got.transpose(1, 0, 2)).reshape(B, S, D)
```
